# Optimizing a Trainium2 kernel written in Bass

```python
import numpy as np
import jax
import jax.numpy as jnp

def _softmax(x, axis=-1):
    return jax.nn.softmax(x, axis=axis)

def _gelu(x):
    return jax.nn.gelu(x, approximate=True)

def _silu(x):
    return jax.nn.silu(x)

def _sigmoid(x):
    return jax.nn.sigmoid(x)

def _layernorm(x, axis=-1, eps=1e-05):
    m = jnp.mean(x, axis=axis, keepdims=True)
    v = jnp.var(x, axis=axis, keepdims=True)
    return (x - m) / jnp.sqrt(v + eps)

def _scatter_add(tgt, idx, src, axis=0):
    return tgt.at[idx].add(src)

def _segment_sum(src, seg, n):
    return jax.ops.segment_sum(src, seg, n)
kernel_name = 'mk_flamingo_gated_d1_seqx_r2_831869'

def setup_inputs(seed: int=0):
    np.random.seed(seed)
    _w = jnp.asarray

    def _rec_inputs():
        import jax
        import jax.numpy as jnp
        _rk = jax.random.key(seed)
        x = -0.000125 + 0.9999 * jax.random.normal(jax.random.fold_in(_rk, 1), (16, 512, 1024), jnp.float32)
        _lenS = 512 - jax.random.randint(jax.random.fold_in(_rk, 7), (16,), 0, max(1, 512 // 4) + 1, jnp.int32)
        _lenS2 = 512 - jax.random.randint(jax.random.fold_in(_rk, 8), (16,), 0, max(1, 512 // 4) + 1, jnp.int32)
        _ctx_2048P = jax.random.normal(jax.random.fold_in(_rk, 11), (16, 16, 1024), jnp.float32)
        _ctx_2048c = jax.random.dirichlet(jax.random.fold_in(_rk, 511), 0.3 * jnp.ones((16,), jnp.float32), (16, 512))
        _ctx_2048t = jnp.einsum('bsk,bkd->bsd', _ctx_2048c, _ctx_2048P)
        _ctx_2048t = _ctx_2048t * jax.lax.rsqrt(jnp.mean(jnp.square(_ctx_2048t)) + 1e-12) * 0.953939
        ctx_2048 = -0.000514642 + 1.00011 * (_ctx_2048t + 0.3 * jax.random.normal(jax.random.fold_in(_rk, 611), (16, 512, 1024), jnp.float32))
        _validS = jnp.arange(512)[None, :] < _lenS[:, None]
        _validS2 = jnp.arange(512)[None, :] < _lenS2[:, None]
        _causal = jnp.tril(jnp.ones((512, 512), dtype=bool))
        mask_BxS2_bk0 = jnp.logical_not(jnp.broadcast_to(_validS2[:, :], (16, 512)))
        _g = jax.random.normal(jax.random.fold_in(_rk, 9001), (2, 1), jnp.float32)
        _g = jnp.sign(_g) * jnp.maximum(jnp.abs(_g), 1.0) + (_g == 0) * 1.0
        g_xattn = _g[0]
        g_ffn = _g[1]
        return (x, ctx_2048, mask_BxS2_bk0, g_xattn, g_ffn)
    x, ctx_2048, mask_BxS2_bk0, g_xattn, g_ffn = _rec_inputs()

    def _L0_xattn_setup():
        import jax, jax.numpy as jnp
        import numpy as np
        key = jax.random.key(seed)
        k1, k2, k3 = jax.random.split(key, 3)
        B, S, D, M = (8, 1024, 1024, 128)
        hidden_states = jax.random.normal(k1, (B, S, D), dtype=jnp.float32)
        memory_tokens = jax.random.normal(k2, (B, M, D), dtype=jnp.float32)
        memory_mask = jax.random.randint(k3, (B, M), 0, 2).astype(jnp.bool_)
        return {'hidden_states': hidden_states, 'memory_tokens': memory_tokens, 'memory_mask': memory_mask}
    _L0_xattn_all = _L0_xattn_setup()
    _L0_xattn_in = {k: v for k, v in _L0_xattn_all.items() if k in ()}
    del _L0_xattn_all

    def _L0_ffn_setup():
        import jax, jax.numpy as jnp
        import numpy as np
        D_MODEL = 1024
        NUM_TILES = 64
        D_SLICE = D_MODEL // NUM_TILES
        TILES_PER_CLUSTER = 8
        NUM_CLUSTERS = NUM_TILES // TILES_PER_CLUSTER
        GRID = 16
        LN_EPS = 1e-05
        DIMS = (np.arange(NUM_TILES)[:, None] * D_SLICE + np.arange(D_SLICE)[None, :]) % D_MODEL
        DIMS = jnp.asarray(DIMS, dtype=jnp.int32)

        def _forward(x, ln_gamma, ln_beta, spline_bases, spline_slopes, output_scale):
            B, S, D = x.shape
            N = B * S
            mu = jnp.mean(x, axis=-1, keepdims=True)
            var = jnp.mean(jnp.square(x - mu), axis=-1, keepdims=True)
            xn = (x - mu) * jax.lax.rsqrt(var + LN_EPS) * ln_gamma + ln_beta
            xf = xn.reshape(N, D)
            slope_sign = jnp.sign(jnp.mean(spline_slopes, axis=-1))
            tile_sigs = jnp.zeros((NUM_TILES, D), dtype=x.dtype)
            tile_sigs = tile_sigs.at[jnp.arange(NUM_TILES)[:, None], DIMS].set(slope_sign)
            cluster_sigs = jnp.sign(tile_sigs.reshape(NUM_CLUSTERS, TILES_PER_CLUSTER, D).mean(axis=1))
            cluster_assign = jnp.arange(NUM_TILES, dtype=jnp.int32) // TILES_PER_CLUSTER
            input_sigs = jnp.sign(xf)
            cluster_scores = input_sigs @ cluster_sigs.T
            best_cluster = jnp.argmax(cluster_scores, axis=-1)
            tile_scores = input_sigs @ tile_sigs.T
            in_cluster = cluster_assign[None, :] == best_cluster[:, None]
            tile_idx = jnp.argmax(jnp.where(in_cluster, tile_scores, -jnp.inf), axis=-1)
            tok_dims = DIMS[tile_idx]
            x_slice = jnp.take_along_axis(xf, tok_dims, axis=1)
            tok_min = x_slice.min(axis=1)
            tok_max = x_slice.max(axis=1)
            onehot = tile_idx[None, :] == jnp.arange(NUM_TILES)[:, None]
            tile_min = jnp.where(onehot, tok_min[None, :], jnp.inf).min(axis=1)
            tile_max = jnp.where(onehot, tok_max[None, :], -jnp.inf).max(axis=1)
            mn = tile_min[tile_idx][:, None]
            mx = tile_max[tile_idx][:, None]
            u = jnp.clip((x_slice - mn) / (mx - mn + 1e-08), 0.0, 1.0 - 1e-06)
            gi = jnp.clip((u * GRID).astype(jnp.int32), 0, GRID - 1)
            j = jnp.arange(D_SLICE)[None, :]
            b = spline_bases[tile_idx[:, None], j, gi]
            s = spline_slopes[tile_idx[:, None], j, gi]
            x_local = (u - gi.astype(u.dtype) / GRID) * GRID
            delta = (b + s * x_local) * output_scale[tile_idx][:, None]
            out = jnp.zeros_like(xf).at[jnp.arange(N)[:, None], tok_dims].set(delta)
            return x + out.reshape(B, S, D)
        key = jax.random.key(seed)
        k1, k2, k3, k4, k5, k6 = jax.random.split(key, 6)
        x = jax.random.normal(k1, (4, 2048, D_MODEL), dtype=jnp.float32)
        ln_gamma = 1.0 + 0.1 * jax.random.normal(k2, (D_MODEL,), dtype=jnp.float32)
        ln_beta = 0.1 * jax.random.normal(k3, (D_MODEL,), dtype=jnp.float32)
        spline_bases = 0.1 * jax.random.normal(k4, (NUM_TILES, D_SLICE, GRID), dtype=jnp.float32)
        spline_slopes = 0.1 + 0.1 * jax.random.normal(k5, (NUM_TILES, D_SLICE, GRID), dtype=jnp.float32)
        output_scale = 1.0 + 0.1 * jax.random.normal(k6, (NUM_TILES,), dtype=jnp.float32)
        return {'x': x, 'ln_gamma': ln_gamma, 'ln_beta': ln_beta, 'spline_bases': spline_bases, 'spline_slopes': spline_slopes, 'output_scale': output_scale}
    _L0_ffn_all = _L0_ffn_setup()
    _L0_ffn_in = {k: v for k, v in _L0_ffn_all.items() if k in ('ln_gamma', 'ln_beta', 'spline_bases', 'spline_slopes', 'output_scale')}
    del _L0_ffn_all
    return {'x': x, 'ctx_2048': ctx_2048, 'mask_BxS2_bk0': mask_BxS2_bk0, 'g_xattn': g_xattn, 'g_ffn': g_ffn, 'L0_ffn_ln_gamma': _L0_ffn_in['ln_gamma'], 'L0_ffn_ln_beta': _L0_ffn_in['ln_beta'], 'L0_ffn_spline_bases': _L0_ffn_in['spline_bases'], 'L0_ffn_spline_slopes': _L0_ffn_in['spline_slopes'], 'L0_ffn_output_scale': _L0_ffn_in['output_scale']}

def reference(x, ctx_2048, mask_BxS2_bk0, g_xattn, g_ffn, L0_ffn_ln_gamma, L0_ffn_ln_beta, L0_ffn_spline_bases, L0_ffn_spline_slopes, L0_ffn_output_scale):
    import jax
    import jax.numpy as jnp

    def _L0_xattn_ref(hidden_states, memory_tokens, memory_mask):
        import jax, jax.numpy as jnp
        import numpy as np
        B, S, D = hidden_states.shape
        scale = 1.0 / jnp.sqrt(jnp.asarray(D, hidden_states.dtype))
        scores = jnp.einsum('bsd,bmd->bsm', hidden_states, memory_tokens) * scale
        neg_inf = jnp.asarray(-1e+30, scores.dtype)
        scores = jnp.where(memory_mask[:, None, :], scores, neg_inf)
        attn = jax.nn.softmax(scores, axis=-1)
        readout = jnp.einsum('bsm,bmd->bsd', attn, memory_tokens)
        valid_b = jnp.any(memory_mask, axis=-1)
        out = jnp.where(valid_b[:, None, None], readout, jnp.zeros_like(readout))
        return out

    def _L0_ffn_ref(x, ln_gamma, ln_beta, spline_bases, spline_slopes, output_scale):
        import jax, jax.numpy as jnp
        import numpy as np
        D_MODEL = 1024
        NUM_TILES = 64
        D_SLICE = D_MODEL // NUM_TILES
        TILES_PER_CLUSTER = 8
        NUM_CLUSTERS = NUM_TILES // TILES_PER_CLUSTER
        GRID = 16
        LN_EPS = 1e-05
        DIMS = (np.arange(NUM_TILES)[:, None] * D_SLICE + np.arange(D_SLICE)[None, :]) % D_MODEL
        DIMS = jnp.asarray(DIMS, dtype=jnp.int32)

        def _forward(x, ln_gamma, ln_beta, spline_bases, spline_slopes, output_scale):
            B, S, D = x.shape
            N = B * S
            mu = jnp.mean(x, axis=-1, keepdims=True)
            var = jnp.mean(jnp.square(x - mu), axis=-1, keepdims=True)
            xn = (x - mu) * jax.lax.rsqrt(var + LN_EPS) * ln_gamma + ln_beta
            xf = xn.reshape(N, D)
            slope_sign = jnp.sign(jnp.mean(spline_slopes, axis=-1))
            tile_sigs = jnp.zeros((NUM_TILES, D), dtype=x.dtype)
            tile_sigs = tile_sigs.at[jnp.arange(NUM_TILES)[:, None], DIMS].set(slope_sign)
            cluster_sigs = jnp.sign(tile_sigs.reshape(NUM_CLUSTERS, TILES_PER_CLUSTER, D).mean(axis=1))
            cluster_assign = jnp.arange(NUM_TILES, dtype=jnp.int32) // TILES_PER_CLUSTER
            input_sigs = jnp.sign(xf)
            cluster_scores = input_sigs @ cluster_sigs.T
            best_cluster = jnp.argmax(cluster_scores, axis=-1)
            tile_scores = input_sigs @ tile_sigs.T
            in_cluster = cluster_assign[None, :] == best_cluster[:, None]
            tile_idx = jnp.argmax(jnp.where(in_cluster, tile_scores, -jnp.inf), axis=-1)
            tok_dims = DIMS[tile_idx]
            x_slice = jnp.take_along_axis(xf, tok_dims, axis=1)
            tok_min = x_slice.min(axis=1)
            tok_max = x_slice.max(axis=1)
            onehot = tile_idx[None, :] == jnp.arange(NUM_TILES)[:, None]
            tile_min = jnp.where(onehot, tok_min[None, :], jnp.inf).min(axis=1)
            tile_max = jnp.where(onehot, tok_max[None, :], -jnp.inf).max(axis=1)
            mn = tile_min[tile_idx][:, None]
            mx = tile_max[tile_idx][:, None]
            u = jnp.clip((x_slice - mn) / (mx - mn + 1e-08), 0.0, 1.0 - 1e-06)
            gi = jnp.clip((u * GRID).astype(jnp.int32), 0, GRID - 1)
            j = jnp.arange(D_SLICE)[None, :]
            b = spline_bases[tile_idx[:, None], j, gi]
            s = spline_slopes[tile_idx[:, None], j, gi]
            x_local = (u - gi.astype(u.dtype) / GRID) * GRID
            delta = (b + s * x_local) * output_scale[tile_idx][:, None]
            out = jnp.zeros_like(xf).at[jnp.arange(N)[:, None], tok_dims].set(delta)
            return x + out.reshape(B, S, D)
        return _forward(x, ln_gamma, ln_beta, spline_bases, spline_slopes, output_scale)
    x = x + jnp.tanh(g_xattn[0]) * _L0_xattn_ref(_layernorm(x, axis=-1), ctx_2048, mask_BxS2_bk0)
    x = x + jnp.tanh(g_ffn[0]) * _L0_ffn_ref(_layernorm(x, axis=-1), L0_ffn_ln_gamma, L0_ffn_ln_beta, L0_ffn_spline_bases, L0_ffn_spline_slopes, L0_ffn_output_scale)
    return x

_drawn_inputs = setup_inputs


def setup_inputs(seed=0):
    import zlib

    import numpy as np

    out = dict(_drawn_inputs(seed))
    spreads = {}
    factors = {'L0_ffn_output_scale': 5.815}
    for name, (base, spread) in spreads.items():
        noise = np.random.default_rng([zlib.crc32(name.encode()), seed]).standard_normal(out[name].shape)
        drawn = base * np.exp(spread * noise) if base else spread * noise
        out[name] = jnp.asarray(drawn.astype(out[name].dtype))
    for name, factor in factors.items():
        out[name] = (out[name] * factor).astype(out[name].dtype)
    return out
```

```python
from contextlib import ExitStack

import concourse.bass as bass
from concourse import mybir

ALU = mybir.AluOpType
ACT = mybir.ActivationFunctionType
AX_X = mybir.AxisListType.X
F32 = mybir.dt.float32
F16 = mybir.dt.float16
BF16 = mybir.dt.bfloat16
U8 = mybir.dt.uint8
I32 = mybir.dt.int32

P = 128
BIG = 1e30
EPS = 1e-5
STAGES = 5


class Step:

    def __init__(self, q, u, batches):
        self.q, self.u, self.batches = q, u, batches
        self.static = isinstance(q, int)

    def number(self):
        return 3 * self.q + self.u

    def batch(self, lag):
        return 3 * self.q + (self.u - lag)

    def slot(self, lag):
        return (self.u - lag) % 3

    def round(self, lag):
        return self.q + (self.u - lag) // 3

    def on(self, lag):
        return not self.static or 0 <= self.batch(lag) < self.batches

    def after(self, lag, n):
        return not self.static or self.batch(lag) >= n


def wait_apart(engine, sem, value, apart):
    engine.wait_ge(sem, value).then_inc(apart, 1)


class Counts:

    def __init__(self, per_stage, batches):
        self.per_stage, self.batches = per_stage, batches

    def before(self, step):
        total = 0
        first = STAGES - 1
        upto = step.number() if step.static else first
        for s in range(min(upto, self.batches + first)):
            total += self.of(s)
        if not step.static:
            total = total + self.of(first) * (step.number() - first)
        return total

    def of(self, s):
        return sum(n for lag, n in self.per_stage.items() if 0 <= s - lag < self.batches)


class Chain:

    def __init__(self, engine, sem, per_stage, batches, start, apart=None):
        self.engine, self.sem, self.start, self.apart = engine, sem, start, apart
        self.counts = Counts(per_stage, batches)

    def begin(self, step):
        self.base = self.counts.before(step) + self.start
        self.local = 0

    def mark(self, instruction):
        instruction.then_inc(self.sem, 1)
        self.local += 1

    def wait(self):
        if self.apart is None:
            self.engine.wait_ge(self.sem, self.base + self.local)
        else:
            wait_apart(self.engine, self.sem, self.base + self.local, self.apart)

    def link(self, instruction):
        self.mark(instruction)
        self.wait()

    def end(self, step):
        if step.static:
            assert self.local == self.counts.of(step.number()), (self.local, step.number())
        else:
            assert self.local == self.counts.of(STAGES - 1), self.local


def build_kernel(nc, x, ctx, mask, g_xattn, g_ffn, gamma, beta, bases, slopes, out_scale, out):
    NB, S, D = x.shape
    NT, DS, GRID = bases.shape
    R = S // P
    NC = D // P
    TC = P // DS
    KEYS = ctx.shape[1]
    KB = KEYS // P
    TT = NB * R
    HALF = D // 2
    LW = 2 * DS + 1
    GROUPS = TT // 4
    assert NC * TC == NT and S == 512 and R == 4 and KB == 4 and NC == 8

    xv = x.rearrange("b (p i) d -> b p (i d)", i=R)
    outv = out.rearrange("b (p i) d -> b p i d", i=R)
    out_rows = out.rearrange("b s (t j) -> (b s t) j", j=DS)

    es = ExitStack()
    with es:
        def sb(name, shape, dt):
            return es.enter_context(nc.sbuf_tensor(name, shape, dt))

        def sem(name):
            return es.enter_context(nc.semaphore(name))

        X = sb("X", [P, 3, R, D], F32)
        X1 = sb("X1", [P, 3, R, D], F32)
        XH = sb("XH", [P, R, D], F32)
        CTX = sb("CTX", [P, 3, D], F32)
        CC = sb("CC", [P, D], F32)
        CT = sb("CT", [P, NC, P], F32)
        XT = sb("XT", [P, 4, S], F32)
        ST = sb("ST", [P, S], F32)
        PR = sb("PR", [P, R, P], F32)
        PT = sb("PT", [P, S], F32)
        SG = sb("SG", [P, NC, S], F16)
        PROD = sb("PROD", [P, 2, D], F32)
        JUNK = sb("JUNK", [P, D], BF16)
        OH = sb("OH", [P, 3, R, 2, NT], BF16)
        OHT = sb("OHT", [P, TT * P], BF16)
        XN = sb("XN", [P, TT, DS], F32)
        Y0S = sb("Y0S", [P, TT, DS], F32)
        TK = sb("TK", [P, TT], F32)
        CAND = sb("CAND", [P, 2, R, NT], F32)
        RUN = sb("RUN", [P, 2, R, NT], F32)
        PEN = sb("PEN", [P, R, NT], F32)

        ST1 = sb("ST1", [P, R, 2, 6], F32)
        MV1 = sb("MV1", [P, R, 2], F32)
        RX = sb("RX", [P, 3, R], F32)
        STC = sb("STC", [P, 2, 6], F32)
        MVC = sb("MVC", [P, 2], F32)
        NMC = sb("NMC", [P, 1], F32)
        MX = sb("MX", [P, R], F32)
        NBIAS = sb("NBIAS", [P, R], F32)
        SUMS = sb("SUMS", [P, R], F32)
        REC = sb("REC", [P, R], F32)
        COEF = sb("COEF", [P, R], F32)
        OSUM = sb("OSUM", [P, R, 2], F32)
        SQ = sb("SQ", [P, R], F32)
        SM = sb("SM", [P, R], F32)
        MSQ = sb("MSQ", [P, R], F32)
        MEAN = sb("MEAN", [P, 3, R], F32)
        VAR = sb("VAR", [P, R], F32)
        W1 = sb("W1", [P, R], F32)
        W2 = sb("W2", [P, R], F32)
        W3 = sb("W3", [P, R], F32)
        R1 = sb("R1", [P, R], F32)
        RR = sb("RR", [P, 3, R], F32)
        YA = sb("YA", [P, 3, R], F32)
        YC = sb("YC", [P, 3, R], F32)
        WL = sb("WL", [P, R], F32)
        KEY = sb("KEY", [P, R, NT], F32)
        KMAX = sb("KMAX", [P, R], F32)
        LOOK = sb("LOOK", [P, R, LW], F32)
        XS = sb("XS", [P, R, DS], F32)
        E1 = sb("E1", [P, R, DS], F32)
        E2 = sb("E2", [P, R, DS], F32)
        E3 = sb("E3", [P, R, DS], F32)
        Y1 = sb("Y1", [P, R, DS], F32)
        V = sb("V", [P, 2, R], F32)

        IDENT = sb("IDENT", [P, P], F32)
        IDENTB = sb("IDENTB", [P, P], BF16)
        ONES = sb("ONES", [P, P], F32)
        HALFNEG = sb("HALFNEG", [P, R], F32)
        MASKW = SG[0:NB, NC - 1, :].bitcast(I32)[:, 0:KEYS // 4]
        MASKU = MASKW.bitcast(U8)
        SLOPE = sb("SLOPE", [P, NC, GRID], F32)
        SSUM = sb("SSUM", [P, NC], F32)
        SIGN = sb("SIGN", [P, NC], F32)
        GB = sb("GB", [P, 2 * NC], F32)
        KW = sb("KW", [P, TC], F32)
        KWS = sb("KWS", [P, NC, TC], F16)
        KCI = JUNK[:, 0:2 * NT].bitcast(I32)
        KC = sb("KC", [P, NT], F32)
        IDX = sb("IDX", [P, TT], I32)
        TOKI = IDX
        TOK = sb("TOK", [P, TT], F32)
        MT = sb("MT", [P, KB, NB], F32)
        MBIAS = sb("MBIAS", [P, NB], F32)
        CNT = sb("CNT", [P, NB], F32)
        HASBIG = sb("HASBIG", [P, NB], F32)
        HASLAST = sb("HASLAST", [P, NB], F32)
        OTHER = sb("OTHER", [P, 1], F32)
        FLAG = sb("FLAG", [P, 1], I32)
        G1 = sb("G1", [P, 1], F32)
        G2 = sb("G2", [P, 1], F32)
        TG1 = sb("TG1", [P, 1], F32)
        TG2 = sb("TG2", [P, 1], F32)
        NTG2 = sb("NTG2", [P, 1], F32)
        TGV = sb("TGV", [P, NB], F32)
        LT = sb("LT", [NT, LW], F32)
        LTR = sb("LTR", [NT, LW], F32)
        LTI = sb("LTI", [NT, 1], I32)
        LTP = sb("LTP", [NT, 3, LW], BF16)
        OSC = sb("OSC", [NT, 1], F32)
        SPA = sb("SPA", [P, NT // 4 * GRID * 2], BF16)
        SPB = sb("SPB", [NT, DS * GRID * 2], BF16)
        MM = sb("MM", [NT, 2], F32)
        M2 = sb("M2", [NT, 2], F32)
        M2R = sb("M2R", [NT, 2], F32)
        M2P = sb("M2P", [NT, 3, 2], BF16)
        RUN2 = sb("RUN2", [P, 2, NT], F32)

        GX = X1[:, 0]
        GCTX = X1[:, 1]
        GC = X1[:, 2]
        GXT = XH[:, :, :].rearrange("p i d -> p (i d)").rearrange("p (c n) -> p c n", n=S)
        GCT = OHT[:, :].bitcast(F32).rearrange("p (c k) -> p c k", k=KEYS)
        GMASKW = SG[:, 0, :].bitcast(I32)[:, 0:KEYS // 4]
        GMASKU = GMASKW.bitcast(U8)
        GMB = SG[:, 2:4, :].rearrange("p a b -> p (a b)").bitcast(F32)
        GS = XT[:, 0, :]
        GE = XT[:, 1, :]
        GPT = XT[:, 2, :]
        GVX = ST[:, 0:2 * R].rearrange("p (i w) -> p i w", w=2)
        GVC = ST[:, 16:16 + 2 * KB].rearrange("p (i w) -> p i w", w=2)
        GVE = ST[:, 24:24 + R]
        GSTATS = ST[:, 32:32 + 48].rearrange("p (i h w) -> p i h w", h=2, w=6)
        x1_dram = nc.dram_tensor("x1_scratch", [NB, P, R * D], F32).ap()

        MASKF = XH[:, 0, 0:KEYS]
        GBPAD = XH[:, 1, 0:P]
        GBROW = GBPAD
        SPRAW = [PROD[0:NT, 0, 0:DS * GRID], PROD[0:NT, 0, 512:512 + DS * GRID]]
        SPS = PROD[0:NT, 1, 0:512]
        SPR = PROD[0:NT, 1, 512:1024]
        U = X[:, 0, 0, :].rearrange("p (t j) -> p t j", j=DS)
        U2 = X[:, 0, 1, :].rearrange("p (t j) -> p t j", j=DS)
        VFRAC = X[:, 0, 2, :]
        FIN = X[:, 0, 3, :].rearrange("p (t j) -> p t j", j=DS)
        BIT = [X[:, 1, 0, 256 * n:256 * (n + 1)].bitcast(U8) for n in range(4)]
        SEL = [X[:, 1, 1 + n, :].rearrange("p (a c) -> p a c", c=DS) for n in range(2)]
        FT = [X[:, 2, n, 0:64] for n in range(2)]
        FT2 = [X[:, 2, n, 64:128] for n in range(2)]

        PS = es.enter_context(nc.psum_tensor("PS", [P, 8, 512], F32))
        TB = [PS[:, n, :] for n in range(3)]
        SC = PS[:, 3, :]
        SN = PS[:, 4, :].rearrange("p (i k) -> p i k", i=R)
        OB = [PS[:, 5 + n, :] for n in range(2)]
        KEYP = PS[:, 7, 0:R * NT].rearrange("p (i t) -> p i t", i=R)
        CNTP = PS[:, 7, 0:KB * NB]

        x_in = [sem(f"x_in{n}") for n in range(3)]
        ctx_in = [sem(f"ctx_in{n}") for n in range(3)]
        y_out = [sem(f"y_out{n}") for n in range(3)]
        params_in = sem("params_in")
        mask_in = sem("mask_in")
        gb_in = sem("gb_in")
        padded = sem("padded")
        consts = sem("consts")
        mask_f32 = sem("mask_f32")
        setup_t = sem("setup_t")
        mask_t = sem("mask_t")
        tanh_done = sem("tanh_done")
        setup_done = sem("setup_done")
        identb = sem("identb")
        bank_full = sem("bank_full")
        bank_free = sem("bank_free")
        centred = sem("centred")
        scores_full = sem("scores_full")
        scores_sb = sem("scores_sb")
        turned = sem("turned")
        bias_ready = sem("bias_ready")
        exps = sem("exps")
        o_full = sem("o_full")
        x1_half = sem("x1_half")
        squares = sem("squares")
        var_x = sem("var_x")
        rstd_x = sem("rstd_x")
        var_x1 = sem("var_x1")
        norm_ready = sem("norm_ready")
        normed = sem("normed")
        keys_full = sem("keys_full")
        onehot = sem("onehot")
        product = sem("product")
        picked = sem("picked")
        y0_ready = sem("y0_ready")
        ctx_mean = sem("ctx_mean")
        slice_done = sem("slice_done")
        cand_ready = sem("cand_ready")
        ran = sem("ran")
        v_chain = sem("v_chain")
        p_chain = sem("p_chain")
        v_apart = sem("v_apart")
        p_apart = sem("p_apart")
        flag_ready = sem("flag_ready")
        g_in = sem("g_in")
        g_var = sem("g_var")
        g_rstd = sem("g_rstd")
        g_centred = sem("g_centred")
        g_full = sem("g_full")
        g_free = sem("g_free")
        g_scores = sem("g_scores")
        g_bias = sem("g_bias")
        g_exp = sem("g_exp")
        g_o = sem("g_o")
        g_x1 = sem("g_x1")
        g_out = sem("g_out")
        g_again = sem("g_again")
        g_chain = sem("g_chain")
        no_readout = sem("no_readout")
        g_apart = sem("g_apart")
        run_t = sem("run_t")
        run_sb = sem("run_sb")
        table_ready = sem("table_ready")
        range_full = sem("range_full")
        bits_ready = sem("bits_ready")
        idx_ready = sem("idx_ready")
        group_full = sem("group_full")
        lows_sb = sem("lows_sb")
        group_taken = sem("group_taken")
        fin_ready = sem("fin_ready")
        scattered = sem("scattered")

        ORDER = [(0, "ctx0"), (0, "ctx1"), (0, "x0"), (0, "x1"), (2, "h0"), (0, "x2"), (1, "pt"),
                 (2, "h1"), (0, "x3"), (2, "h2"), (3, "oht"), (0, "x4"), (2, "h3"), (0, "x5"),
                 (2, "h4"), (3, "look"), (0, "x6"), (2, "h5"), (0, "x7"), (2, "h6"), (2, "h7")]
        bank_uses = Counts({n: sum(lag == n for lag, _ in ORDER) for n in range(STAGES)}, NB)

        def bank(step, what):
            names = [name for lag, name in ORDER if step.on(lag)]
            at = names.index(what)
            if step.static:
                n = bank_uses.before(step) + at
                return n % 3, n + 1
            fixed = bank_uses.before(Step(1, 1, NB))
            u = step.u - (STAGES - 1)
            return (fixed + u * len(names) + at) % 3, bank_uses.before(step) + at + 1

        def steps(engine, step):
            first = STAGES - 1
            turns = (NB - first) // 3
            for s in range(first):
                step(Step(s // 3, s % 3, NB))
            with engine.Fori(0, turns - 1) as i:
                for u in range(first, first + 3):
                    step(Step(i, u, NB))
            for s in range(first + 3 * (turns - 1), NB + first):
                step(Step(s // 3, s % 3, NB))

        block = es.enter_context(nc.Block())

        def general_flag(engine):
            engine.wait_ge(flag_ready, 1)
            return engine.value_load(FLAG[0:1, 0:1], min_val=0, max_val=1)

        @block.sync
        def _(sp):
            def load(source, slot, batch):
                sp.dma_start(X[:, slot].rearrange("p i d -> p (i d)"), source[batch]).then_inc(x_in[slot], 16)
                sp.dma_start(CTX[:, slot, :], ctx[batch, KEYS - P:KEYS, :]).then_inc(ctx_in[slot], 16)

            sp.dma_start(MASKW, mask).then_inc(mask_in, 16)
            sp.dma_start(CTX[:, 0, :], ctx[0, KEYS - P:KEYS, :]).then_inc(ctx_in[0], 16)
            sp.dma_start(X[:, 0].rearrange("p i d -> p (i d)"), xv[0]).then_inc(x_in[0], 16)
            load(xv, 1, 1)
            load(xv, 2, 2)

            def step(st, source):
                if st.on(3):
                    slot = st.slot(3)
                    for i in range(R):
                        sp.wait_ge(y0_ready, R * st.batch(3) + i + 1)
                        sp.dma_start(outv[st.batch(3), :, i, :], X1[:, slot, i, :]).then_inc(y_out[slot], 16)
                if st.on(1) and st.on(-2):
                    sp.wait_ge(x1_half, 2 * R * (st.batch(1) + 1))
                    load(source, st.slot(1), st.batch(-2))

            def general():
                sp.wait_ge(flag_ready, 1).then_inc(g_out, 16)
                with sp.Fori(0, NB) as b:
                    sp.wait_ge(g_out, 16 * b + 16)
                    sp.dma_start(GX.rearrange("p i d -> p (i d)"), xv[b]).then_inc(g_in, 16)
                    sp.dma_start(GCTX, ctx[b].rearrange("(k p) d -> p k d", p=P)).then_inc(g_in, 16)
                    sp.dma_start(GMASKW, mask[bass.ds(b, 1), :].to_broadcast([P, KEYS // 4])).then_inc(g_in, 16)
                    sp.wait_ge(g_x1, 2 * R * b + 2 * R + 1)
                    sp.dma_start(x1_dram[b], GX.rearrange("p i d -> p (i d)")).then_inc(g_out, 16)
                sp.wait_ge(g_out, 16 * NB + 16)
                for n in range(3):
                    sp.wait_ge(x_in[n], 16)
                    sp.dma_start(X[:, n].rearrange("p i d -> p (i d)"), x1_dram[n]).then_inc(g_again, 16)

            with sp.If(general_flag(sp)):
                general()
                steps(sp, lambda st: step(st, x1_dram))
            with sp.Else():
                steps(sp, lambda st: step(st, xv))
            for n in range(3):
                sp.wait_ge(y_out[n], 16 * R * len(range(n, NB, 3)))

        @block.gpsimd
        def _(pool):
            nc.gpsimd.memset(IDENT[:, :], 0.0).then_inc(consts, 1)
            nc.gpsimd.memset(ONES[:, :], 1.0).then_inc(consts, 1)
            nc.gpsimd.memset(HALFNEG[:, :], -0.5).then_inc(consts, 1)
            nc.gpsimd.memset(KW[:, :], 4104.0).then_inc(consts, 1)
            pool.wait_ge(consts, 4)
            nc.gpsimd.affine_select(out=IDENT[:, :], in_=IDENT[:, :], compare_op=ALU.not_equal, fill=1.0,
                                    base=0, pattern=[[-1, P]], channel_multiplier=1).then_inc(consts, 1)
            nc.gpsimd.affine_select(out=KW[:, :], in_=KW[:, :], compare_op=ALU.is_ge, fill=4096.0,
                                    base=0, pattern=[[-DS, TC]], channel_multiplier=1).then_inc(consts, 1)
            pool.wait_ge(consts, 6)
            nc.gpsimd.affine_select(out=KW[:, :], in_=KW[:, :], compare_op=ALU.is_ge, fill=4096.0,
                                    base=DS - 1, pattern=[[DS, TC]], channel_multiplier=-1).then_inc(consts, 1)
            nc.gpsimd.iota(KCI, pattern=[[-512, NC], [-1, TC]], base=512 * (NC - 1) + TC - 1,
                           channel_multiplier=0).then_inc(consts, 1)
            nc.gpsimd.iota(TOKI[:, :], pattern=[[S, NB], [1, R]], base=0,
                           channel_multiplier=R).then_inc(consts, 1)
            nc.gpsimd.iota(LTI[:, :], pattern=[[0, 1]], base=0, channel_multiplier=1).then_inc(consts, 1)
            chain = Chain(pool, p_chain, {0: 1, 2: 9, 4: 3}, NB, 0, p_apart)

            def centre(batch, slot, n):
                wait_apart(pool, ctx_mean, n + 1, p_apart)
                nc.gpsimd.tensor_scalar(CC[:, :], CTX[:, slot, :], NMC[:, 0:1], None,
                                        ALU.add).then_inc(centred, 1)

            centre(0, 0, 0)
            with pool.If(general_flag(pool)):
                with pool.Fori(0, NB) as b:
                    wait_apart(pool, g_var, b + 1, g_apart)
                    nc.gpsimd.tensor_tensor(R1[:, :], GVE, HALFNEG[:, :], ALU.pow).then_inc(g_rstd, 1)
                pool.wait_ge(g_again, 48)
            with pool.Else():
                pool.wait_ge(flag_ready, 1)

            def step(st):
                chain.begin(st)
                if st.static and st.number() == 2:
                    pool.wait_ge(setup_done, 1)
                if st.on(2):
                    k = st.slot(2)
                    wait_apart(pool, var_x1, st.batch(2) + 1, p_apart)
                    chain.link(nc.gpsimd.tensor_scalar(W1[:, :], VAR[:, :], EPS, None, ALU.add))
                    chain.link(nc.gpsimd.tensor_tensor(R1[:, :], W1[:, :], HALFNEG[:, :], ALU.pow))
                    chain.link(nc.gpsimd.tensor_tensor(W2[:, :], R1[:, :], R1[:, :], ALU.mult))
                    chain.link(nc.gpsimd.tensor_tensor(W3[:, :], W2[:, :], VAR[:, :], ALU.mult))
                    chain.link(nc.gpsimd.tensor_scalar(W1[:, :], W3[:, :], EPS, None, ALU.add))
                    chain.link(nc.gpsimd.tensor_tensor(W2[:, :], W1[:, :], HALFNEG[:, :], ALU.pow))
                    chain.mark(nc.gpsimd.tensor_tensor(RR[:, k, :], R1[:, :], W2[:, :], ALU.mult))
                    chain.mark(nc.gpsimd.tensor_scalar(YA[:, k, :], R1[:, :], TG2[:, 0:1], 1.0,
                                                       ALU.mult, ALU.add))
                    chain.link(nc.gpsimd.tensor_tensor(W3[:, :], R1[:, :], MEAN[:, k, :], ALU.mult))
                    nc.gpsimd.tensor_scalar(YC[:, k, :], W3[:, :], NTG2[:, 0:1], None,
                                            ALU.mult).then_inc(norm_ready, 1)
                if st.on(3):
                    k = st.slot(3)
                    wait_apart(pool, onehot, st.batch(3) + 1, p_apart)
                    for i in range(R):
                        if i >= 2 or st.after(3, 1):
                            wait_apart(pool, picked, R * st.batch(3) + i - 1, p_apart)
                        nc.gpsimd.tensor_tensor(
                            PROD[:, i % 2, :].rearrange("p (t j) -> p t j", j=DS),
                            X1[:, k, i, :].rearrange("p (t j) -> p t j", j=DS),
                            OH[:, k, i, 0, :].unsqueeze(2).to_broadcast([P, NT, DS]),
                            ALU.mult).then_inc(product, 1)
                        wait_apart(pool, product, R * st.batch(3) + i + 1, p_apart)
                        nc.gpsimd.tensor_scalar(X1[:, k, i, :], X1[:, k, i, :], YA[:, k, i:i + 1],
                                                YC[:, k, i:i + 1], ALU.mult, ALU.add).then_inc(y0_ready, 1)
                if st.on(0):
                    wait_apart(pool, var_x, st.batch(0) + 1, p_apart)
                    chain.link(nc.gpsimd.tensor_scalar(WL[:, :], MV1[:, :, 1], EPS, None, ALU.add))
                    nc.gpsimd.tensor_tensor(RX[:, st.slot(0), :], WL[:, :], HALFNEG[:, :],
                                            ALU.pow).then_inc(rstd_x, 1)
                if st.on(4):
                    k = st.slot(4)
                    wait_apart(pool, slice_done, st.batch(4) + 1, p_apart)
                    chain.link(nc.gpsimd.tensor_scalar(PEN[:, :, :], OH[:, k, :, 0, :], -1.0, BIG,
                                                       ALU.add, ALU.mult))
                    wait_apart(pool, ran, st.batch(4) + 1, p_apart)
                    for w in range(2):
                        chain.mark(nc.gpsimd.tensor_tensor(
                            CAND[:, w, :, :], OH[:, k, :, 0, :],
                            V[:, w, :].unsqueeze(2).to_broadcast([P, R, NT]), ALU.mult))
                    chain.wait()
                    for w in range(2):
                        nc.gpsimd.tensor_tensor(CAND[:, w, :, :], CAND[:, w, :, :], PEN[:, :, :],
                                                ALU.add).then_inc(cand_ready, 1)
                if st.on(-1):
                    wait_apart(pool, bank_free, bank(st, "ctx1")[1], p_apart)
                    centre(None, st.slot(-1), st.number() + 1)
                chain.end(st)

            steps(pool, step)

            pool.wait_ge(idx_ready, 1)
            for n in range(3):
                pool.wait_ge(y_out[n], 16 * R * len(range(n, NB, 3)))
            for t in range(TT):
                pool.wait_ge(fin_ready, t // 4 + 1)
                nc.gpsimd.indirect_dma_start(
                    out_rows, bass.IndirectOffsetOnAxis(ap=IDX[:, t:t + 1], axis=0),
                    FIN[:, t, :], None).then_inc(scattered, 16)
            pool.wait_ge(scattered, 16 * TT)

        @block.scalar
        def _(act):
            act.wait_ge(padded, 2)
            act.dma_start(GBROW[NC:2 * NC, :], beta.rearrange("(c p) -> c p", p=P)).then_inc(gb_in, 16)
            act.dma_start(GBROW[0:NC, :], gamma.rearrange("(c p) -> c p", p=P)).then_inc(gb_in, 16)
            act.dma_start(G1[:, :], g_xattn.unsqueeze(0).to_broadcast([P, 1])).then_inc(params_in, 16)
            act.dma_start(G2[:, :], g_ffn.unsqueeze(0).to_broadcast([P, 1])).then_inc(params_in, 16)
            act.dma_start(SLOPE[:, :, :], slopes.rearrange("t j g -> (t j) g").rearrange(
                "(c p) g -> p c g", p=P)).then_inc(params_in, 16)
            act.dma_start(LT[:, 0:DS], gamma.rearrange("(t j) -> t j", j=DS)).then_inc(params_in, 16)
            act.dma_start(LT[:, DS:2 * DS], beta.rearrange("(t j) -> t j", j=DS)).then_inc(params_in, 16)
            act.dma_start(SPRAW[0], bases.rearrange("t j g -> t (j g)")).then_inc(params_in, 16)
            act.dma_start(SPRAW[1], slopes.rearrange("t j g -> t (j g)")).then_inc(params_in, 16)
            act.dma_start(OSC[:, :], out_scale.rearrange("(t a) -> t a", a=1)).then_inc(params_in, 16)
            act.wait_ge(params_in, 16 * 8)
            nc.scalar.activation(TG1[:, :], G1[:, :], ACT.Tanh).then_inc(tanh_done, 1)
            nc.scalar.activation(TG2[:, :], G2[:, :], ACT.Tanh).then_inc(tanh_done, 1)
            with act.If(general_flag(act)):
                act.wait_ge(flag_ready, 1).then_inc(g_free, 1)
                with act.Fori(0, NB) as b:
                    uses = 2 * NC + R
                    for n in range(2 * NC):
                        act.wait_ge(g_full, uses * b + n + 1)
                        dst = GXT[:, n, :] if n < NC else GCT[:, n - NC, :]
                        nc.scalar.activation(dst, OB[n % 2], ACT.Copy).then_inc(g_free, 1)
                    act.wait_ge(g_rstd, b + 1)
                    for i in range(R):
                        act.wait_ge(g_bias, R * b + i + 1)
                        nc.scalar.activation(GE, GS, ACT.Exp, bias=NBIAS[:, i:i + 1], scale=R1[:, i:i + 1],
                                             accum_out=SUMS[:, i:i + 1]).then_inc(g_exp, 1)
                        act.wait_ge(g_full, uses * b + 2 * NC + i + 1)
                        nc.scalar.activation(GPT, OB[0], ACT.Copy).then_inc(g_free, 1)
                act.wait_ge(g_again, 48)
            with act.Else():
                act.wait_ge(flag_ready, 1)

            def take(st, name, out, function=ACT.Copy, width=S, **more):
                n, count = bank(st, name)
                act.wait_ge(bank_full, count)
                source = TB[n][:, 0:width] if name != "oht" else TB[n].bitcast(BF16)[:, 0:S]
                nc.scalar.activation(out, source, function, **more).then_inc(bank_free, 1)

            def take_x(st, c):
                if st.on(0):
                    take(st, f"x{c}", XT[:, c % 4, :])

            def take_h(st, c):
                if st.on(2):
                    take(st, f"h{c}", SG[:, c, :], ACT.Sign, scale=GB[:, c:c + 1], bias=GB[:, NC + c:NC + c + 1])

            def square(st, i):
                if st.on(1):
                    b = st.batch(1)
                    act.wait_ge(x1_half, 2 * R * b + 2 * i + 2)
                    if i == 0 and st.after(1, 1):
                        act.wait_ge(var_x1, b)
                    if i > 0 or st.after(1, 1):
                        act.wait_ge(squares, R * b + i)
                    nc.scalar.activation(JUNK[:, :], X1[:, st.slot(1), i, :], ACT.Square,
                                         accum_out=SQ[:, i:i + 1]).then_inc(squares, 1)

            def step(st):
                if st.static and st.number() == 2:
                    act.wait_ge(setup_done, 1)
                if st.on(0):
                    for n in range(2):
                        take(st, f"ctx{n}", CT[:, 4 * n:4 * n + 4, :].rearrange("p c k -> p (c k)"))
                take_x(st, 0)
                if st.on(1):
                    act.wait_ge(bias_ready, st.batch(1) + 1)
                    for i in range(R):
                        nc.scalar.activation(PR[:, i, :], SN[:, i, :], ACT.Exp, bias=NBIAS[:, i:i + 1],
                                             scale=RX[:, st.slot(1), i:i + 1],
                                             accum_out=SUMS[:, i:i + 1]).then_inc(exps, 1)
                take_x(st, 1)
                take_h(st, 0)
                take_x(st, 2)
                if st.on(1):
                    take(st, "pt", PT[:, :])
                take_h(st, 1)
                take_x(st, 3)
                take_h(st, 2)
                if st.on(3):
                    take(st, "oht", OHT[:, bass.ds(S * st.batch(3), S)])
                take_x(st, 4)
                take_h(st, 3)
                take_x(st, 5)
                take_h(st, 4)
                if st.on(3):
                    if st.after(3, 1):
                        act.wait_ge(slice_done, st.batch(3))
                    take(st, "look", LOOK[:, :, :].rearrange("p i w -> p (i w)"), width=R * LW)
                take_x(st, 6)
                square(st, 0)
                take_h(st, 5)
                take_x(st, 7)
                square(st, 1)
                take_h(st, 6)
                take_h(st, 7)
                if st.on(0):
                    act.wait_ge(scores_full, st.batch(0) + 1)
                    nc.scalar.activation(ST[:, :], SC, ACT.Identity, scale=float(D) ** -0.5,
                                         bias=MBIAS[:, bass.ds(st.batch(0), 1)]).then_inc(scores_sb, 1)
                square(st, 2)
                square(st, 3)

            steps(act, step)

            with act.Fori(0, GROUPS // 2) as i:
                for n in range(2):
                    act.wait_ge(group_full, 2 * i + n + 1)
                    rows = PS[:, 4 * n:4 * n + 4, :].rearrange("p b (j c) -> p (b j) c", c=2 * GRID)
                    act.wait_ge(group_taken, 2 * i + n + 1)
                    nc.scalar.activation(SEL[n][:, :, 0:GRID], rows[:, :, 0:GRID], ACT.Copy).then_inc(lows_sb, 1)

        @block.tensor
        def _(pe):
            pe.wait_ge(consts, 10)
            pe.wait_ge(mask_f32, 1)
            for kb in range(KB):
                last = nc.tensor.transpose(OB[0][:, kb * P:(kb + 1) * P], MASKF[:, kb * P:(kb + 1) * P], IDENT[:, :])
            last.then_inc(setup_t, 1)
            pe.wait_ge(mask_t, 1)
            nc.tensor.matmul(CNTP, ONES[:, :], MT[:, :, :].rearrange("p k b -> p (k b)"), start=True,
                             stop=True).then_inc(setup_t, 1)
            pe.wait_ge(gb_in, 32)
            nc.tensor.transpose(OB[1][:, 0:P], GBROW, IDENT[:, :]).then_inc(setup_t, 1)
            with pe.If(general_flag(pe)):
                pe.wait_ge(setup_done, 1)
                with pe.Fori(0, NB) as b:
                    uses = 2 * NC + R
                    pe.wait_ge(g_in, 48 * b + 48)
                    pe.wait_ge(g_centred, b + 1)
                    for n in range(2 * NC):
                        pe.wait_ge(g_free, uses * b + max(n - 1, 0) + 1)
                        if n == 0:
                            pe.wait_ge(g_x1, 2 * R * b + 1)
                        source, c = (GX, n) if n < NC else (GC, n - NC)
                        for i in range(4):
                            last = nc.tensor.transpose(OB[n % 2][:, i * P:(i + 1) * P],
                                                       source[:, i, c * P:(c + 1) * P], IDENT[:, :])
                        last.then_inc(g_full, 1)
                    pe.wait_ge(g_free, uses * b + 2 * NC + 1)
                    for i in range(R):
                        for c in range(NC):
                            mm = nc.tensor.matmul(SC, GXT[:, c, i * P:(i + 1) * P], GCT[:, c, :], start=(c == 0),
                                                  stop=(c == NC - 1))
                        mm.then_inc(g_scores, 1)
                        pe.wait_ge(g_exp, R * b + i + 1)
                        pe.wait_ge(g_x1, 2 * R * b + 2 * i + 1)
                        for kb in range(KB):
                            last = nc.tensor.transpose(OB[0][:, kb * P:(kb + 1) * P], GE[:, kb * P:(kb + 1) * P],
                                                       IDENT[:, :])
                        last.then_inc(g_full, 1)
                        pe.wait_ge(g_free, uses * b + 2 * NC + i + 2)
                        for h in range(2):
                            for kb in range(KB):
                                mm = nc.tensor.matmul(OB[h], GPT[:, kb * P:(kb + 1) * P],
                                                      GCTX[:, kb, h * HALF:(h + 1) * HALF], start=(kb == 0),
                                                      stop=(kb == KB - 1))
                            mm.then_inc(g_o, 1)
                pe.wait_ge(g_again, 48)
            with pe.Else():
                pe.wait_ge(flag_ready, 1)

            def rotating(st, name):
                n, count = bank(st, name)
                if not st.static or count > 3:
                    pe.wait_ge(bank_free, count - 3)
                return TB[n]

            def turn_x(st, c):
                if st.on(0):
                    dst = rotating(st, f"x{c}")
                    if c == 0:
                        pe.wait_ge(x_in[st.slot(0)], 16 * st.round(0) + 16)
                    for i in range(R):
                        last = nc.tensor.transpose(dst[:, i * P:(i + 1) * P],
                                                   X[:, st.slot(0), i, c * P:(c + 1) * P], IDENT[:, :])
                    last.then_inc(bank_full, 1)

            def score(st, c):
                if st.on(0):
                    pe.wait_ge(bank_free, bank(st, f"x{c}")[1])
                    if c == 0 and st.after(0, 1):
                        pe.wait_ge(scores_sb, st.batch(0))
                    mm = nc.tensor.matmul(SC, CT[:, c, :], XT[:, c % 4, :], start=(c == 0), stop=(c == NC - 1))
                    if c == NC - 1:
                        mm.then_inc(scores_full, 1)

            def turn_h(st, c):
                if st.on(2):
                    dst = rotating(st, f"h{c}")
                    for i in range(R):
                        if c == 0:
                            pe.wait_ge(normed, R * st.batch(2) + i + 1)
                        last = nc.tensor.transpose(dst[:, i * P:(i + 1) * P], XH[:, i, c * P:(c + 1) * P],
                                                   IDENT[:, :])
                    last.then_inc(bank_full, 1)

            def key(st, c):
                if st.on(2):
                    pe.wait_ge(bank_free, bank(st, f"h{c}")[1])
                    if c == 0 and st.after(2, 1):
                        pe.wait_ge(onehot, st.batch(2))
                    for i in range(R):
                        mm = nc.tensor.matmul(KEYP[:, i, TC * c:TC * (c + 1)], SG[:, c, i * P:(i + 1) * P],
                                              KWS[:, c, :], start=True, stop=True)
                    if c == NC - 1:
                        mm.then_inc(keys_full, 1)

            def turn_scores(st):
                if st.on(1):
                    pe.wait_ge(scores_sb, st.batch(1) + 1)
                    if st.after(1, 1):
                        pe.wait_ge(exps, R * st.batch(1))
                    for i in range(R):
                        last = nc.tensor.transpose(SN[:, i, :], ST[:, i * P:(i + 1) * P], IDENT[:, :])
                    last.then_inc(turned, 1)

            def turn_probs(st):
                if st.on(1):
                    dst = rotating(st, "pt")
                    for i in range(R):
                        pe.wait_ge(exps, R * st.batch(1) + i + 1)
                        last = nc.tensor.transpose(dst[:, i * P:(i + 1) * P], PR[:, i, :], IDENT[:, :])
                    last.then_inc(bank_full, 1)

            def readout(st, n):
                if st.on(1):
                    i, h = n // 2, n % 2
                    if n == 0:
                        pe.wait_ge(bank_free, bank(st, "pt")[1])
                    if n >= 2 or st.after(1, 1):
                        pe.wait_ge(x1_half, 2 * R * st.batch(1) + n - 1)
                    nc.tensor.matmul(OB[n % 2], PT[:, i * P:(i + 1) * P],
                                     CTX[:, st.slot(1), h * HALF:(h + 1) * HALF], start=True,
                                     stop=True).then_inc(o_full, 1)

            def turn_onehot(st):
                if st.on(3):
                    dst = rotating(st, "oht").bitcast(BF16)
                    pe.wait_ge(onehot, st.batch(3) + 1)
                    for i in range(R):
                        twice = OH[:, st.slot(3), i, :, :].rearrange("p a t -> p (a t)")
                        last = nc.tensor.transpose(dst[:, i * P:(i + 1) * P], twice, IDENTB[:, :])
                    last.then_inc(bank_full, 1)

            def look_up(st):
                if st.on(3):
                    pe.wait_ge(bank_free, bank(st, "oht")[1])
                    dst = rotating(st, "look")
                    for i in range(R):
                        for part in range(3):
                            mm = nc.tensor.matmul(dst[:, i * LW:(i + 1) * LW],
                                                  OHT[0:NT, bass.ds(S * st.batch(3) + i * P, P)],
                                                  LTP[:, part, :], start=(part == 0), stop=(part == 2))
                    mm.then_inc(bank_full, 1)

            def step(st):
                if st.static and st.number() == 1:
                    pe.wait_ge(setup_done, 1)
                turn_scores(st)
                if st.on(0):
                    pe.wait_ge(centred, st.batch(0) + 1)
                    for n in range(2):
                        dst = rotating(st, f"ctx{n}")
                        for c in range(4):
                            last = nc.tensor.transpose(dst[:, c * P:(c + 1) * P],
                                                       CC[:, (4 * n + c) * P:(4 * n + c + 1) * P], IDENT[:, :])
                        last.then_inc(bank_full, 1)
                turn_x(st, 0)
                turn_x(st, 1)
                score(st, 0)
                turn_h(st, 0)
                turn_x(st, 2)
                score(st, 1)
                turn_probs(st)
                turn_h(st, 1)
                key(st, 0)
                turn_x(st, 3)
                score(st, 2)
                turn_h(st, 2)
                key(st, 1)
                turn_onehot(st)
                for c in range(4, 8):
                    turn_x(st, c)
                    score(st, c - 1)
                    readout(st, 2 * (c - 4))
                    turn_h(st, c - 1)
                    key(st, c - 2)
                    readout(st, 2 * (c - 4) + 1)
                    if c == 5:
                        look_up(st)
                score(st, 7)
                turn_h(st, 7)
                key(st, 6)
                key(st, 7)

            steps(pe, step)

            pe.wait_ge(run_sb, 1)
            for w in range(2):
                last = nc.tensor.transpose(PS[0:NT, 0, w * P:(w + 1) * P], RUN2[:, w, :], IDENT[:, :])
            last.then_inc(run_t, 1)
            pe.wait_ge(table_ready, 1)
            for t in range(TT):
                for part in range(3):
                    mm = nc.tensor.matmul(PS[:, 7, 2 * t:2 * t + 2], OHT[0:NT, t * P:(t + 1) * P], M2P[:, part, :],
                                          start=(part == 0), stop=(part == 2))
            mm.then_inc(range_full, 1)
            with pe.Fori(0, GROUPS // 2) as i:
                for n in range(2):
                    pe.wait_ge(group_taken, 2 * i + n + 1)
                    for r in range(4):
                        tile = bass.ds(P * 4 * (2 * i + n) + P * r, P)
                        nc.tensor.matmul(PS[:, 4 * n + r, :], OHT[:, tile], SPA[:, :], start=True, stop=False)
                        mm = nc.tensor.matmul(PS[:, 4 * n + r, :], OHT[0:NT, tile], SPB[:, :], start=False, stop=True)
                    mm.then_inc(group_full, 1)

        @block.vector
        def _(dve):
            made = [0]

            def link(instruction):
                made[0] += 1
                instruction.then_inc(v_chain, 1)
                dve.wait_ge(v_chain, made[0])

            def context_mean(slot, count, batch, after):
                dve.wait_ge(ctx_in[slot], count)
                if after is not None:
                    dve.wait_ge(centred, after)
                for h in range(2):
                    chain.mark(nc.vector.bn_stats(STC[:, h, :], CTX[:, slot, h * HALF:(h + 1) * HALF]))
                wait_apart(dve, v_chain, chain.base + chain.local, v_apart)
                chain.link(nc.vector.bn_aggr(MVC[:, :], STC[:, :, :]))
                nc.vector.tensor_scalar(NMC[:, :], MVC[:, 0:1], -1.0, None, ALU.mult).then_inc(ctx_mean, 1)

            nc.vector.memset(MASKF, 0.0).then_inc(padded, 1)
            nc.vector.memset(GBPAD, 0.0).then_inc(padded, 1)
            dve.wait_ge(mask_in, 16)
            dve.wait_ge(padded, 2)
            nc.vector.tensor_copy(MASKF[0:NB, :], MASKU).then_inc(mask_f32, 1)
            dve.wait_ge(ctx_in[0], 16)
            link(nc.vector.bn_stats(STC[:, 0, :], CTX[:, 0, 0:HALF]))
            link(nc.vector.bn_stats(STC[:, 1, :], CTX[:, 0, HALF:D]))
            link(nc.vector.bn_aggr(MVC[:, :], STC[:, :, :]))
            nc.vector.tensor_scalar(NMC[:, :], MVC[:, 0:1], -1.0, None, ALU.mult).then_inc(ctx_mean, 1)
            dve.wait_ge(setup_t, 1)
            nc.vector.tensor_copy(MT[:, :, :], OB[0].rearrange("p (k b) -> p k b", k=KB)[:, :, 0:NB]).then_inc(mask_t, 1)
            dve.wait_ge(mask_t, 1)
            dve.wait_ge(setup_t, 2)
            link(nc.vector.tensor_scalar(HASLAST[:, :], CNTP[:, (KB - 1) * NB:KB * NB], 0.0, BIG, ALU.is_gt,
                                         ALU.mult))
            link(nc.vector.tensor_reduce(CNT[:, :], CNTP.rearrange("p (k b) -> p b k", k=KB), AX_X, ALU.add))
            link(nc.vector.tensor_scalar(HASBIG[:, :], CNT[:, :], 0.0, BIG, ALU.is_gt, ALU.mult))
            link(nc.vector.scalar_tensor_tensor(MBIAS[:, :], MT[:, KB - 1, :], -1.0, HASLAST[:, :], ALU.add, ALU.mult))
            link(nc.vector.tensor_reduce(OTHER[:, :], CNTP[:, 0:(KB - 1) * NB], AX_X, ALU.add))
            nc.vector.tensor_scalar(FLAG[:, :], OTHER[:, :], 0.0, None, ALU.is_gt).then_inc(flag_ready, 1)
            dve.wait_ge(consts, 10)
            nc.vector.tensor_copy(KC[:, :], KCI)
            nc.vector.tensor_copy(TOK[:, :], TOKI[:, :])
            nc.vector.tensor_copy(IDENTB[:, :], IDENT[:, :])
            dve.wait_ge(setup_t, 3)
            nc.vector.tensor_copy(GB[:, :], OB[1][:, 0:2 * NC])
            dve.wait_ge(params_in, 16 * 8)
            link(nc.vector.tensor_reduce(SSUM[:, :], SLOPE[:, :, :], AX_X, ALU.add))
            link(nc.vector.tensor_scalar(SIGN[:, :], SSUM[:, :], 0.0, None, ALU.is_gt))
            link(nc.vector.tensor_scalar(SSUM[:, :], SSUM[:, :], 0.0, None, ALU.is_lt))
            link(nc.vector.tensor_tensor(SIGN[:, :], SIGN[:, :], SSUM[:, :], ALU.subtract))
            nc.vector.tensor_tensor(KWS[:, :, :], SIGN[:, :].unsqueeze(2).to_broadcast([P, NC, TC]),
                                    KW[:, :].unsqueeze(1).to_broadcast([P, NC, TC]), ALU.mult)
            link(nc.vector.tensor_copy(LT[:, 2 * DS:LW], LTI[:, :]))

            def split(source, rest, parts):
                link(nc.vector.tensor_copy(parts[0], source))
                link(nc.vector.tensor_tensor(rest, source, parts[0], ALU.subtract))
                link(nc.vector.tensor_copy(parts[1], rest))
                link(nc.vector.tensor_tensor(rest, rest, parts[1], ALU.subtract))
                link(nc.vector.tensor_copy(parts[2], rest))

            split(LT[:, :], LTR[:, :], [LTP[:, n, :] for n in range(3)])
            dve.wait_ge(tanh_done, 2)
            link(nc.vector.tensor_scalar(TGV[:, :], CNT[:, :], 0.0, TG1[:, 0:1], ALU.is_gt, ALU.mult))
            nc.vector.tensor_scalar(NTG2[:, :], TG2[:, :], -1.0, None, ALU.mult)
            table = SPS.rearrange("t (a w) -> t a w", w=2)
            for w in range(2):
                link(nc.vector.tensor_scalar(table[:, :, w], SPRAW[w], OSC[:, 0:1], TG2[0:NT, 0:1],
                                             ALU.mult, ALU.mult))
            link(nc.vector.tensor_copy(SPA[0:NT, :], SPS))
            link(nc.vector.tensor_tensor(SPR, SPS, SPA[0:NT, :], ALU.subtract))
            link(nc.vector.tensor_copy(SPB[:, :], SPR))
            link(nc.vector.tensor_tensor(SPR, SPR, SPB[:, :], ALU.subtract))
            link(nc.vector.tensor_copy(SPA[NT:2 * NT, :], SPB[:, :]))
            link(nc.vector.tensor_copy(SPB[:, :], SPR))
            nc.vector.memset(RUN[:, :, :, :], -BIG).then_inc(ran, 1)
            nc.vector.memset(SUMS[:, :], 0.0).then_inc(setup_done, 1)

            with dve.If(general_flag(dve)):
                dve.wait_ge(setup_done, 1).then_inc(g_x1, 1)
                with dve.Fori(0, NB) as b:
                    made_in_turn = 3 * R + 3 * KB + KB + 4 * R
                    done = [0]

                    def mark(instruction):
                        done[0] += 1
                        instruction.then_inc(g_chain, 1)

                    def wait():
                        wait_apart(dve, g_chain, made_in_turn * b + done[0], g_apart)

                    def g_link(instruction):
                        mark(instruction)
                        wait()

                    def statistics(source, mean_var, rows):
                        for i in range(rows):
                            for h in range(2):
                                mark(nc.vector.bn_stats(GSTATS[:, i, h, :], source[:, i, h * HALF:(h + 1) * HALF]))
                        wait()
                        for i in range(rows):
                            mark(nc.vector.bn_aggr(mean_var[:, i, :], GSTATS[:, i, :, :]))
                        wait()

                    dve.wait_ge(g_in, 48 * b + 48)
                    statistics(GX, GVX, R)
                    nc.vector.tensor_scalar(GVE, GVX[:, :, 1], EPS, None, ALU.add).then_inc(g_var, 1)
                    statistics(GCTX, GVC, KB)
                    for k in range(KB):
                        mark(nc.vector.tensor_scalar(GC[:, k, :], GCTX[:, k, :], GVC[:, k, 0:1], None, ALU.subtract))
                    wait()
                    nc.vector.tensor_scalar(GMB, GMASKU, -1.0, HASBIG[:, bass.ds(b, 1)], ALU.add,
                                            ALU.mult).then_inc(g_centred, 1)
                    dve.wait_ge(g_centred, b + 1)
                    dve.wait_ge(g_rstd, b + 1)
                    for i in range(R):
                        dve.wait_ge(g_scores, R * b + i + 1)
                        g_link(nc.vector.scalar_tensor_tensor(GS, SC, float(D) ** -0.5, GMB, ALU.mult, ALU.add))
                        g_link(nc.vector.tensor_reduce(MX[:, i:i + 1], GS, AX_X, ALU.max))
                        nc.vector.scalar_tensor_tensor(NBIAS[:, i:i + 1], MX[:, i:i + 1], -1.0, R1[:, i:i + 1],
                                                       ALU.mult, ALU.mult).then_inc(g_bias, 1)
                        dve.wait_ge(g_exp, R * b + i + 1)
                        g_link(nc.vector.reciprocal(REC[:, i:i + 1], SUMS[:, i:i + 1]))
                        g_link(nc.vector.tensor_scalar(COEF[:, i:i + 1], REC[:, i:i + 1], TGV[:, bass.ds(b, 1)],
                                                       None, ALU.mult))
                        for h in range(2):
                            dve.wait_ge(g_o, 2 * R * b + 2 * i + h + 1)
                            cols = slice(h * HALF, (h + 1) * HALF)
                            nc.vector.scalar_tensor_tensor(GX[:, i, cols], OB[h], COEF[:, i:i + 1], GX[:, i, cols],
                                                           ALU.mult, ALU.add).then_inc(g_x1, 1)
                    assert done[0] == made_in_turn
                nc.vector.memset(TGV[:, :], 0.0).then_inc(no_readout, 1)
                dve.wait_ge(no_readout, 1)
                dve.wait_ge(g_again, 48)
            with dve.Else():
                dve.wait_ge(flag_ready, 1)

            chain = Chain(dve, v_chain, {-1: 3, 0: 11, 1: 3, 2: 3, 3: 11}, NB, made[0])

            def softmax_bias(st):
                if st.on(1):
                    dve.wait_ge(turned, st.batch(1) + 1)
                    chain.link(nc.vector.tensor_reduce(MX[:, :], SN[:, :, :], AX_X, ALU.max))
                    dve.wait_ge(rstd_x, st.batch(1) + 1)
                    nc.vector.scalar_tensor_tensor(NBIAS[:, :], MX[:, :], -1.0, RX[:, st.slot(1), :],
                                                   ALU.mult, ALU.mult).then_inc(bias_ready, 1)

            def coefficient(st):
                if st.on(1):
                    dve.wait_ge(exps, R * (st.batch(1) + 1))
                    chain.link(nc.vector.reciprocal(REC[:, :], SUMS[:, :]))
                    chain.link(nc.vector.tensor_scalar(COEF[:, :], REC[:, :], TGV[:, bass.ds(st.batch(1), 1)],
                                                       None, ALU.mult))

            def add_readout(st, n):
                if st.on(1):
                    i, h, k = n // 2, n % 2, st.slot(1)
                    if n == 0 and st.after(1, 3):
                        dve.wait_ge(y_out[k], 16 * R * st.round(1))
                    dve.wait_ge(o_full, 2 * R * st.batch(1) + n + 1)
                    cols = slice(h * HALF, (h + 1) * HALF)
                    nc.vector.scalar_tensor_tensor(X1[:, k, i, cols], OB[n % 2], COEF[:, i:i + 1],
                                                   X[:, k, i, cols], ALU.mult, ALU.add,
                                                   accum_out=OSUM[:, i, h:h + 1]).then_inc(x1_half, 1)

            def x1_stats(st):
                if st.on(2):
                    k = st.slot(2)
                    dve.wait_ge(squares, R * (st.batch(2) + 1))
                    dve.wait_ge(x1_half, 2 * R * (st.batch(2) + 1))
                    chain.link(nc.vector.tensor_tensor(SM[:, :], OSUM[:, :, 0], OSUM[:, :, 1], ALU.add))
                    chain.link(nc.vector.tensor_scalar(MEAN[:, k, :], SM[:, :], 1.0 / D, None, ALU.mult))
                    chain.link(nc.vector.tensor_tensor(MSQ[:, :], MEAN[:, k, :], MEAN[:, k, :], ALU.mult))
                    nc.vector.scalar_tensor_tensor(VAR[:, :], SQ[:, :], 1.0 / D, MSQ[:, :], ALU.mult,
                                                   ALU.subtract).then_inc(var_x1, 1)

            def norm(st):
                if st.on(2):
                    k = st.slot(2)
                    dve.wait_ge(norm_ready, st.batch(2) + 1)
                    if st.after(2, 1):
                        dve.wait_ge(keys_full, st.batch(2))
                    for i in range(R):
                        nc.vector.tensor_scalar(XH[:, i, :], X1[:, k, i, :], MEAN[:, k, i:i + 1],
                                                RR[:, k, i:i + 1], ALU.subtract, ALU.mult).then_inc(normed, 1)

            def pick_tile(st):
                if st.on(3):
                    dve.wait_ge(keys_full, st.batch(3) + 1)
                    chain.link(nc.vector.tensor_tensor(KEY[:, :, :], KEYP,
                                                       KC[:, :].unsqueeze(1).to_broadcast([P, R, NT]), ALU.add))
                    chain.link(nc.vector.tensor_reduce(KMAX[:, :], KEY[:, :, :], AX_X, ALU.max))
                    nc.vector.tensor_tensor(OH[:, st.slot(3), :, :, :],
                                            KEY[:, :, :].unsqueeze(2).to_broadcast([P, R, 2, NT]),
                                            KMAX[:, :].unsqueeze(2).unsqueeze(3).to_broadcast([P, R, 2, NT]),
                                            ALU.is_equal).then_inc(onehot, 1)

            def x_stats(st, i):
                if st.on(0):
                    if i == 0:
                        dve.wait_ge(x_in[st.slot(0)], 16 * st.round(0) + 16)
                        if st.after(0, 1):
                            dve.wait_ge(rstd_x, st.batch(0))
                    for h in range(2):
                        chain.mark(nc.vector.bn_stats(ST1[:, i, h, :],
                                                      X[:, st.slot(0), i, h * HALF:(h + 1) * HALF]))
                    if i == R - 1:
                        wait_apart(dve, v_chain, chain.base + chain.local, v_apart)
                        for n in range(R):
                            ins = nc.vector.bn_aggr(MV1[:, n, :], ST1[:, n, :, :])
                            if n < R - 1:
                                chain.mark(ins)
                            else:
                                ins.then_inc(var_x, 1)

            def sum_slice(st, i):
                if st.on(3):
                    dve.wait_ge(product, R * st.batch(3) + i + 1)
                    nc.vector.tensor_reduce(XS[:, i, :], PROD[:, i % 2, :].rearrange("p (t j) -> p j t", j=DS),
                                            AX_X, ALU.add).then_inc(picked, 1)

            def slices(st):
                if st.on(3):
                    k, b = st.slot(3), st.batch(3)
                    rows = bass.ds(R * b, R)

                    def wide(values):
                        return values.unsqueeze(2).to_broadcast([P, R, DS])

                    dve.wait_ge(picked, R * (b + 1))
                    chain.mark(nc.vector.tensor_tensor(E1[:, :, :], XS[:, :, :], wide(MEAN[:, k, :]), ALU.subtract))
                    chain.link(nc.vector.tensor_tensor(Y1[:, :, :], XS[:, :, :], wide(YA[:, k, :]), ALU.mult))
                    chain.mark(nc.vector.tensor_tensor(E2[:, :, :], E1[:, :, :], wide(RR[:, k, :]), ALU.mult))
                    chain.link(nc.vector.tensor_tensor(Y0S[:, rows, :], Y1[:, :, :], wide(YC[:, k, :]), ALU.add))
                    dve.wait_ge(bank_free, bank(st, "look")[1])
                    chain.link(nc.vector.tensor_tensor(E3[:, :, :], E2[:, :, :], LOOK[:, :, 0:DS], ALU.mult))
                    chain.mark(nc.vector.tensor_copy(TK[:, rows], LOOK[:, :, 2 * DS]))
                    chain.link(nc.vector.tensor_tensor(E1[:, :, :], E3[:, :, :], LOOK[:, :, DS:2 * DS], ALU.add))
                    chain.mark(nc.vector.tensor_copy(XN[:, rows, :], E1[:, :, :]))
                    if st.after(3, 1):
                        dve.wait_ge(cand_ready, 2 * b)
                    chain.mark(nc.vector.tensor_reduce(V[:, 0, :], E1[:, :, :], AX_X, ALU.max))
                    nc.vector.tensor_reduce(V[:, 1, :], E1[:, :, :], AX_X, ALU.min,
                                            negate=True).then_inc(slice_done, 1)

            def take_candidates(st):
                if st.on(4):
                    dve.wait_ge(cand_ready, 2 * (st.batch(4) + 1))
                    dve.wait_ge(ran, st.batch(4) + 1)
                    nc.vector.tensor_tensor(RUN[:, :, :, :].rearrange("p w i t -> p (w i t)"),
                                            RUN[:, :, :, :].rearrange("p w i t -> p (w i t)"),
                                            CAND[:, :, :, :].rearrange("p w i t -> p (w i t)"),
                                            ALU.max).then_inc(ran, 1)

            def step(st):
                chain.begin(st)
                x1_stats(st)
                softmax_bias(st)
                pick_tile(st)
                x_stats(st, 0)
                norm(st)
                x_stats(st, 1)
                sum_slice(st, 0)
                coefficient(st)
                add_readout(st, 0)
                add_readout(st, 1)
                sum_slice(st, 1)
                add_readout(st, 2)
                add_readout(st, 3)
                x_stats(st, 2)
                add_readout(st, 4)
                add_readout(st, 5)
                sum_slice(st, 2)
                add_readout(st, 6)
                add_readout(st, 7)
                x_stats(st, 3)
                take_candidates(st)
                sum_slice(st, 3)
                slices(st)
                if st.on(-1):
                    context_mean(st.slot(-1), 16 * st.round(-1) + 16, None, st.batch(0) + 1)
                chain.end(st)

            steps(dve, step)

            made[0] += sum(chain.counts.of(s) for s in range(NB + STAGES - 1))
            dve.wait_ge(ran, NB + 1)
            nc.vector.tensor_reduce(RUN2[:, :, :], RUN[:, :, :, :].rearrange("p w i t -> p w t i"), AX_X,
                                    ALU.max).then_inc(run_sb, 1)
            nc.vector.scalar_tensor_tensor(IDX[:, :], TOK[:, :], float(NT), TK[:, :], ALU.mult,
                                           ALU.add).then_inc(idx_ready, 1)
            dve.wait_ge(run_t, 1)
            link(nc.vector.tensor_reduce(MM[:, :], PS[0:NT, 0, 0:2 * P].rearrange("p (w n) -> p w n", w=2), AX_X,
                                         ALU.max))
            link(nc.vector.tensor_copy(M2[:, 0:1], MM[:, 1:2]))
            link(nc.vector.tensor_tensor(MM[:, 0:1], MM[:, 0:1], MM[:, 1:2], ALU.add))
            link(nc.vector.tensor_scalar(MM[:, 0:1], MM[:, 0:1], 1e-8, None, ALU.add))
            link(nc.vector.reciprocal(MM[:, 1:2], MM[:, 0:1]))
            link(nc.vector.tensor_scalar(M2[:, 1:2], MM[:, 1:2], float(GRID), None, ALU.mult))
            split(M2[:, :], M2R[:, :], [M2P[:, n, :] for n in range(3)])
            nc.vector.memset(FT[0], 0.0).then_inc(table_ready, 1)
            dve.wait_ge(range_full, 1)
            ranges = PS[:, 7, 0:2 * TT].rearrange("p (t w) -> p t w", w=2)
            link(nc.vector.tensor_tensor(U, XN[:, :, :], ranges[:, :, 0:1].to_broadcast([P, TT, DS]), ALU.add))
            link(nc.vector.tensor_tensor(U2, U, ranges[:, :, 1:2].to_broadcast([P, TT, DS]), ALU.mult))
            top = 0.9999989867210388 * GRID
            vf = VFRAC
            link(nc.vector.tensor_scalar(vf, U2.rearrange("p t j -> p (t j)"), 0.0, top, ALU.max, ALU.min))
            nc.vector.memset(FT[1], 0.0).then_inc(group_taken, 1)
            nc.vector.memset(FT[0], 0.0).then_inc(group_taken, 1)
            for n in range(4):
                link(nc.vector.tensor_scalar(BIT[n], vf, float(8 >> n), None, ALU.is_ge))
                link(nc.vector.scalar_tensor_tensor(vf, BIT[n], -float(8 >> n), vf, ALU.mult, ALU.add))
            y0f = Y0S[:, :, :].rearrange("p t j -> p (t j)")
            finf = FIN.rearrange("p t j -> p (t j)")
            for g in range(GROUPS):
                n = g % 2
                at = slice(64 * g, 64 * (g + 1))
                dve.wait_ge(lows_sb, g + 1)
                rows = PS[:, 4 * n:4 * n + 4, :].rearrange("p b (j c) -> p (b j) c", c=2 * GRID)
                width = GRID
                for level in range(4):
                    bit = BIT[level][:, at].unsqueeze(2).to_broadcast([P, 64, width])
                    upper = rows[:, :, width:2 * width] if level == 0 else SEL[n][:, :, width:2 * width]
                    link(nc.vector.copy_predicated(SEL[n][:, :, 0:width], bit, upper))
                    width //= 2
                link(nc.vector.tensor_tensor(FT[n], SEL[n][:, :, 1], vf[:, at], ALU.mult))
                link(nc.vector.tensor_tensor(FT2[n], SEL[n][:, :, 0], y0f[:, at], ALU.add))
                link(nc.vector.tensor_tensor(finf[:, at], FT[n], FT2[n], ALU.add))
                nc.vector.tensor_copy(FT2[n][:, 0:1], FT[n][:, 0:1]).then_inc(fin_ready, 1)
                nc.vector.tensor_copy(FT2[n][:, 1:2], FT[n][:, 1:2]).then_inc(group_taken, 1)


_INS = ["x", "ctx_2048", "mask_BxS2_bk0", "g_xattn", "g_ffn", "L0_ffn_ln_gamma", "L0_ffn_ln_beta",
        "L0_ffn_spline_bases", "L0_ffn_spline_slopes", "L0_ffn_output_scale"]


def kernel(**inputs):
    import numpy as _np
    import concourse.bacc as _bacc
    from concourse import mybir as _mybir
    from concourse.bass_utils import run_bass_kernel_spmd as _run

    nc = _bacc.Bacc("TRN2", target_bir_lowering=False, num_devices=1)
    arrays, args = {}, []
    for name in _INS:
        a = _np.ascontiguousarray(inputs[name])
        if a.dtype.kind == "b":
            a = a.view(_np.int32)
        arrays[f"in_{name}_dram"] = a
        args.append(nc.dram_tensor(f"in_{name}_dram", a.shape, _mybir.dt.from_np(a.dtype), kind="ExternalInput").ap())
    args.append(nc.dram_tensor("out_0_dram", (16, 512, 1024), _mybir.dt.float32, kind="ExternalOutput").ap())
    build_kernel(nc, *args)
    r = _run(nc, [arrays], core_ids=[0])
    return r.results[0]["out_0_dram"]
```

```python
from contextlib import ExitStack

import concourse.bass as bass
from concourse import mybir

ALU = mybir.AluOpType
ACT = mybir.ActivationFunctionType
AX_X = mybir.AxisListType.X
F32 = mybir.dt.float32
F16 = mybir.dt.float16
BF16 = mybir.dt.bfloat16
U8 = mybir.dt.uint8
I32 = mybir.dt.int32

P = 128
BIG = 1e30
EPS = 1e-5
STAGES = 5


class Step:

    def __init__(self, q, u, batches):
        self.q, self.u, self.batches = q, u, batches
        self.static = isinstance(q, int)

    def number(self):
        return 3 * self.q + self.u

    def batch(self, lag):
        return 3 * self.q + (self.u - lag)

    def slot(self, lag):
        return (self.u - lag) % 3

    def round(self, lag):
        return self.q + (self.u - lag) // 3

    def on(self, lag):
        return not self.static or 0 <= self.batch(lag) < self.batches

    def after(self, lag, n):
        return not self.static or self.batch(lag) >= n


def wait_apart(engine, sem, value, apart):
    engine.wait_ge(sem, value).then_inc(apart, 1)


class Counts:

    def __init__(self, per_stage, batches):
        self.per_stage, self.batches = per_stage, batches

    def before(self, step):
        total = 0
        first = STAGES - 1
        upto = step.number() if step.static else first
        for s in range(min(upto, self.batches + first)):
            total += self.of(s)
        if not step.static:
            total = total + self.of(first) * (step.number() - first)
        return total

    def of(self, s):
        return sum(n for lag, n in self.per_stage.items() if 0 <= s - lag < self.batches)


class Chain:

    def __init__(self, engine, sem, per_stage, batches, start, apart, always_apart=False):
        self.engine, self.sem, self.start = engine, sem, start
        self.apart, self.always_apart = apart, always_apart
        self.counts = Counts(per_stage, batches)

    def begin(self, step):
        self.base = self.counts.before(step) + self.start
        self.local = 0

    def mark(self, instruction):
        instruction.then_inc(self.sem, 1)
        self.local += 1

    def wait(self, apart=False):
        if apart or self.always_apart:
            wait_apart(self.engine, self.sem, self.base + self.local, self.apart)
        else:
            self.engine.wait_ge(self.sem, self.base + self.local)

    def link(self, instruction, apart=False):
        self.mark(instruction)
        self.wait(apart)

    def end(self, step):
        if step.static:
            assert self.local == self.counts.of(step.number()), (self.local, step.number())
        else:
            assert self.local == self.counts.of(STAGES - 1), self.local


def build_kernel(nc, x, ctx, mask, g_xattn, g_ffn, gamma, beta, bases, slopes, out_scale, out):
    NB, S, D = x.shape
    NT, DS, GRID = bases.shape
    R = S // P
    NC = D // P
    TC = P // DS
    KEYS = ctx.shape[1]
    KB = KEYS // P
    TT = NB * R
    HALF = D // 2
    LW = 2 * DS + 1
    GROUPS = TT // 4
    assert NC * TC == NT and S == 512 and R == 4 and KB == 4 and NC == 8

    xv = x.rearrange("b (p i) d -> b p (i d)", i=R)
    outv = out.rearrange("b (p i) d -> b p i d", i=R)
    out_rows = out.rearrange("b s (t j) -> (b s t) j", j=DS)

    es = ExitStack()
    with es:
        def sb(name, shape, dt):
            return es.enter_context(nc.sbuf_tensor(name, shape, dt))

        def sem(name):
            return es.enter_context(nc.semaphore(name))

        X = sb("X", [P, 3, R, D], F32)
        X1 = sb("X1", [P, 3, R, D], F32)
        XH = sb("XH", [P, R, D], F32)
        CTX = sb("CTX", [P, 3, D], F32)
        CC = sb("CC", [P, D], F32)
        CT = sb("CT", [P, NC, P], F32)
        XT = sb("XT", [P, 4, S], F32)
        ST = sb("ST", [P, S], F32)
        PR = sb("PR", [P, R, P], F32)
        PT = sb("PT", [P, S], F32)
        SG = sb("SG", [P, NC, S], F16)
        JUNK = sb("JUNK", [P, D], BF16)
        OH = sb("OH", [P, 3, R, 2, NT], BF16)
        OHT = sb("OHT", [P, TT * P], BF16)
        XN = sb("XN", [P, TT, DS], F32)
        Y0S = sb("Y0S", [P, TT, DS], F32)
        TK = sb("TK", [P, TT], F32)
        CAND = sb("CAND", [P, 2, R, NT], F32)
        RUN = sb("RUN", [P, 2, R, NT], F32)
        PEN = sb("PEN", [P, R, NT], F32)

        ST1 = sb("ST1", [P, R, 2, 6], F32)
        MV1 = sb("MV1", [P, R, 2], F32)
        RX = sb("RX", [P, 3, R], F32)
        STC = sb("STC", [P, 2, 6], F32)
        MVC = sb("MVC", [P, 2], F32)
        NMC = sb("NMC", [P, 1], F32)
        MX = sb("MX", [P, R], F32)
        NBIAS = sb("NBIAS", [P, R], F32)
        SUMS = sb("SUMS", [P, R], F32)
        REC = sb("REC", [P, R], F32)
        COEF = sb("COEF", [P, R], F32)
        OSUM = sb("OSUM", [P, R, 2], F32)
        SQ = sb("SQ", [P, R], F32)
        SM = sb("SM", [P, R], F32)
        MSQ = sb("MSQ", [P, R], F32)
        MEAN = sb("MEAN", [P, 3, R], F32)
        VAR = sb("VAR", [P, R], F32)
        WV = sb("WV", [P, 2, R], F32)
        RR = sb("RR", [P, 2, R], F32)
        NMR = sb("NMR", [P, R], F32)
        MR = sb("MR", [P, R], F32)
        YA = sb("YA", [P, R], F32)
        YC = sb("YC", [P, R], F32)
        IR = sb("IR", [P, R], F32)
        YS = sb("YS", [P, 3, R], F32)
        R1 = sb("R1", [P, R], F32)
        WL = sb("WL", [P, R], F32)
        KEY = sb("KEY", [P, R, NT], F32)
        KMAX = sb("KMAX", [P, R], F32)
        KINT = sb("KINT", [P, R], I32)
        KBITS = sb("KBITS", [P, R, 6], I32)
        BITS = sb("BITS", [P, 6], I32)
        LOOK = sb("LOOK", [P, R, LW], F32)
        XS = sb("XS", [P, R, DS], F32)
        E1 = sb("E1", [P, R, DS], F32)
        Y1 = sb("Y1", [P, R, DS], F32)
        V = sb("V", [P, 2, R], F32)

        IDENT = sb("IDENT", [P, P], F32)
        IDENTB = sb("IDENTB", [P, P], BF16)
        ONES = sb("ONES", [P, P], F32)
        HALFNEG = sb("HALFNEG", [P, 2 * R], F32)
        MASKW = SG[0:NB, NC - 1, :].bitcast(I32)[:, 0:KEYS // 4]
        MASKU = MASKW.bitcast(U8)
        SLOPE = sb("SLOPE", [P, NC, GRID], F32)
        SSUM = sb("SSUM", [P, NC], F32)
        SIGN = sb("SIGN", [P, NC], F32)
        GB = sb("GB", [P, 2 * NC], F32)
        KW = sb("KW", [P, TC], F32)
        KWS = sb("KWS", [P, NC, TC], F16)
        KCI = JUNK[:, 0:2 * NT].bitcast(I32)
        KC = sb("KC", [P, NT], F32)
        IDX = sb("IDX", [P, TT], I32)
        TOKI = IDX
        TOK = sb("TOK", [P, TT], F32)
        MT = sb("MT", [P, KB, NB], F32)
        MBIAS = sb("MBIAS", [P, NB], F32)
        CNT = sb("CNT", [P, NB], F32)
        HASBIG = sb("HASBIG", [P, NB], F32)
        HASLAST = sb("HASLAST", [P, NB], F32)
        OTHER = sb("OTHER", [P, 1], F32)
        FLAG = sb("FLAG", [P, 1], I32)
        G1 = sb("G1", [P, 1], F32)
        G2 = sb("G2", [P, 1], F32)
        TG1 = sb("TG1", [P, 1], F32)
        TG2 = sb("TG2", [P, 1], F32)
        NTG2 = sb("NTG2", [P, 1], F32)
        TGV = sb("TGV", [P, NB], F32)
        LT = sb("LT", [NT, LW], F32)
        LTR = sb("LTR", [NT, LW], F32)
        LTI = sb("LTI", [NT, 1], I32)
        LTP = sb("LTP", [NT, 3, LW], BF16)
        OSC = sb("OSC", [NT, 1], F32)
        SPA = sb("SPA", [P, NT // 4 * GRID * 2], BF16)
        SPB = sb("SPB", [NT, DS * GRID * 2], BF16)
        MM = sb("MM", [NT, 2], F32)
        M2 = sb("M2", [NT, 2], F32)
        M2R = sb("M2R", [NT, 2], F32)
        M2P = sb("M2P", [NT, 3, 2], BF16)
        RUN2 = sb("RUN2", [P, 2, NT], F32)

        GX = X1[:, 0]
        GCTX = X1[:, 1]
        GC = X1[:, 2]
        GXT = XH[:, :, :].rearrange("p i d -> p (i d)").rearrange("p (c n) -> p c n", n=S)
        GCT = OHT[:, :].bitcast(F32).rearrange("p (c k) -> p c k", k=KEYS)
        GMASKW = SG[:, 0, :].bitcast(I32)[:, 0:KEYS // 4]
        GMASKU = GMASKW.bitcast(U8)
        GMB = SG[:, 2:4, :].rearrange("p a b -> p (a b)").bitcast(F32)
        GS = XT[:, 0, :]
        GE = XT[:, 1, :]
        GPT = XT[:, 2, :]
        GVX = ST[:, 0:2 * R].rearrange("p (i w) -> p i w", w=2)
        GVC = ST[:, 16:16 + 2 * KB].rearrange("p (i w) -> p i w", w=2)
        GVE = ST[:, 24:24 + R]
        GSTATS = ST[:, 32:32 + 48].rearrange("p (i h w) -> p i h w", h=2, w=6)
        x1_dram = nc.dram_tensor("x1_scratch", [NB, P, R * D], F32).ap()

        MASKF = XH[:, 0, 0:KEYS]
        GBPAD = XH[:, 1, 0:P]
        GBROW = GBPAD
        SPRAW = [XH[0:NT, 2, 0:DS * GRID], XH[0:NT, 2, 512:512 + DS * GRID]]
        SPS = XH[0:NT, 3, 0:512]
        SPR = XH[0:NT, 3, 512:1024]
        U = X[:, 0, 0, :].rearrange("p (t j) -> p t j", j=DS)
        U2 = X[:, 0, 1, :].rearrange("p (t j) -> p t j", j=DS)
        VFRAC = X[:, 0, 2, :]
        FIN = X[:, 0, 3, :].rearrange("p (t j) -> p t j", j=DS)
        BIT = [X[:, 1, 0, 256 * n:256 * (n + 1)].bitcast(U8) for n in range(4)]
        SEL = [X[:, 1, 1 + n, :].rearrange("p (a c) -> p a c", c=DS) for n in range(2)]
        FT = [X[:, 2, n, 0:64] for n in range(2)]
        FT2 = [X[:, 2, n, 64:128] for n in range(2)]

        PS = es.enter_context(nc.psum_tensor("PS", [P, 8, 512], F32))
        TB = [PS[:, n, :] for n in range(3)]
        SC = PS[:, 3, :]
        SN = PS[:, 4, :].rearrange("p (i k) -> p i k", i=R)
        OB = [PS[:, 5 + n, :] for n in range(2)]
        KEYP = PS[:, 7, 0:R * NT].rearrange("p (i t) -> p i t", i=R)
        CNTP = PS[:, 7, 0:KB * NB]

        x_in = [sem(f"x_in{n}") for n in range(3)]
        ctx_in = [sem(f"ctx_in{n}") for n in range(3)]
        y_out = [sem(f"y_out{n}") for n in range(3)]
        params_in = sem("params_in")
        mask_in = sem("mask_in")
        gb_in = sem("gb_in")
        padded = sem("padded")
        consts = sem("consts")
        mask_f32 = sem("mask_f32")
        setup_t = sem("setup_t")
        mask_t = sem("mask_t")
        tanh_done = sem("tanh_done")
        setup_done = sem("setup_done")
        identb = sem("identb")
        bank_full = sem("bank_full")
        bank_free = sem("bank_free")
        centred = sem("centred")
        scores_full = sem("scores_full")
        scores_sb = sem("scores_sb")
        turned = sem("turned")
        bias_ready = sem("bias_ready")
        exps = sem("exps")
        o_full = sem("o_full")
        x1_half = sem("x1_half")
        squares = sem("squares")
        var_x = sem("var_x")
        rstd_x = sem("rstd_x")
        var_x1 = sem("var_x1")
        ys_ready = sem("ys_ready")
        normed = sem("normed")
        keys_full = sem("keys_full")
        onehot = sem("onehot")
        gathered = sem("gathered")
        y0_ready = sem("y0_ready")
        ctx_mean = sem("ctx_mean")
        slice_done = sem("slice_done")
        cand_ready = sem("cand_ready")
        ran = sem("ran")
        v_chain = sem("v_chain")
        p_chain = sem("p_chain")
        v_apart = sem("v_apart")
        p_apart = sem("p_apart")
        flag_ready = sem("flag_ready")
        g_in = sem("g_in")
        g_var = sem("g_var")
        g_rstd = sem("g_rstd")
        g_centred = sem("g_centred")
        g_full = sem("g_full")
        g_free = sem("g_free")
        g_scores = sem("g_scores")
        g_bias = sem("g_bias")
        g_exp = sem("g_exp")
        g_o = sem("g_o")
        g_x1 = sem("g_x1")
        g_out = sem("g_out")
        g_again = sem("g_again")
        g_chain = sem("g_chain")
        no_readout = sem("no_readout")
        g_apart = sem("g_apart")
        run_t = sem("run_t")
        run_sb = sem("run_sb")
        table_ready = sem("table_ready")
        range_full = sem("range_full")
        bits_ready = sem("bits_ready")
        idx_ready = sem("idx_ready")
        group_full = sem("group_full")
        lows_sb = sem("lows_sb")
        group_taken = sem("group_taken")
        fin_ready = sem("fin_ready")
        scattered = sem("scattered")

        ORDER = [(0, "ctx0"), (0, "ctx1"), (0, "x0"), (0, "x1"), (0, "x2"), (1, "pt"), (0, "x3"),
                 (0, "x4"), (3, "oht"), (0, "x5"), (0, "x6"), (3, "look"), (0, "x7"), (2, "h0"),
                 (2, "h1"), (2, "h2"), (2, "h3"), (2, "h4"), (2, "h5"), (2, "h6"), (2, "h7")]
        bank_uses = Counts({n: sum(lag == n for lag, _ in ORDER) for n in range(STAGES)}, NB)

        def bank(step, what):
            names = [name for lag, name in ORDER if step.on(lag)]
            at = names.index(what)
            if step.static:
                n = bank_uses.before(step) + at
                return n % 3, n + 1
            fixed = bank_uses.before(Step(1, 1, NB))
            u = step.u - (STAGES - 1)
            return (fixed + u * len(names) + at) % 3, bank_uses.before(step) + at + 1

        def steps(engine, step):
            first = STAGES - 1
            turns = (NB - first) // 3
            for s in range(first):
                step(Step(s // 3, s % 3, NB))
            with engine.Fori(0, turns - 1) as i:
                for u in range(first, first + 3):
                    step(Step(i, u, NB))
            for s in range(first + 3 * (turns - 1), NB + first):
                step(Step(s // 3, s % 3, NB))

        block = es.enter_context(nc.Block())

        def general_flag(engine):
            engine.wait_ge(flag_ready, 1)
            return engine.value_load(FLAG[0:1, 0:1], min_val=0, max_val=1)

        @block.sync
        def _(sp):
            def load(source, slot, batch):
                sp.dma_start(X[:, slot].rearrange("p i d -> p (i d)"), source[batch]).then_inc(x_in[slot], 16)
                sp.dma_start(CTX[:, slot, :], ctx[batch, KEYS - P:KEYS, :]).then_inc(ctx_in[slot], 16)

            sp.dma_start(MASKW, mask).then_inc(mask_in, 16)
            sp.dma_start(CTX[:, 0, :], ctx[0, KEYS - P:KEYS, :]).then_inc(ctx_in[0], 16)
            sp.dma_start(X[:, 0].rearrange("p i d -> p (i d)"), xv[0]).then_inc(x_in[0], 16)
            load(xv, 1, 1)
            load(xv, 2, 2)

            def step(st, source):
                if st.on(2):
                    slot = st.slot(2)
                    for i in range(R):
                        sp.wait_ge(y0_ready, R * st.batch(2) + i + 1)
                        sp.dma_start(outv[st.batch(2), :, i, :], X1[:, slot, i, :]).then_inc(y_out[slot], 16)
                if st.on(1) and st.on(-2):
                    sp.wait_ge(x1_half, 2 * R * (st.batch(1) + 1))
                    load(source, st.slot(1), st.batch(-2))

            def general():
                sp.wait_ge(flag_ready, 1).then_inc(g_out, 16)
                with sp.Fori(0, NB) as b:
                    sp.wait_ge(g_out, 16 * b + 16)
                    sp.dma_start(GX.rearrange("p i d -> p (i d)"), xv[b]).then_inc(g_in, 16)
                    sp.dma_start(GCTX, ctx[b].rearrange("(k p) d -> p k d", p=P)).then_inc(g_in, 16)
                    sp.dma_start(GMASKW, mask[bass.ds(b, 1), :].to_broadcast([P, KEYS // 4])).then_inc(g_in, 16)
                    sp.wait_ge(g_x1, 2 * R * b + 2 * R + 1)
                    sp.dma_start(x1_dram[b], GX.rearrange("p i d -> p (i d)")).then_inc(g_out, 16)
                sp.wait_ge(g_out, 16 * NB + 16)
                for n in range(3):
                    sp.wait_ge(x_in[n], 16)
                    sp.dma_start(X[:, n].rearrange("p i d -> p (i d)"), x1_dram[n]).then_inc(g_again, 16)

            with sp.If(general_flag(sp)):
                general()
                steps(sp, lambda st: step(st, x1_dram))
            with sp.Else():
                steps(sp, lambda st: step(st, xv))
            for n in range(3):
                sp.wait_ge(y_out[n], 16 * R * len(range(n, NB, 3)))

        @block.gpsimd
        def _(pool):
            nc.gpsimd.memset(IDENT[:, :], 0.0).then_inc(consts, 1)
            nc.gpsimd.memset(ONES[:, :], 1.0).then_inc(consts, 1)
            nc.gpsimd.memset(HALFNEG[:, :], -0.5).then_inc(consts, 1)
            nc.gpsimd.memset(KW[:, :], 4104.0).then_inc(consts, 1)
            pool.wait_ge(consts, 4)
            nc.gpsimd.affine_select(out=IDENT[:, :], in_=IDENT[:, :], compare_op=ALU.not_equal, fill=1.0,
                                    base=0, pattern=[[-1, P]], channel_multiplier=1).then_inc(consts, 1)
            nc.gpsimd.affine_select(out=KW[:, :], in_=KW[:, :], compare_op=ALU.is_ge, fill=4096.0,
                                    base=0, pattern=[[-DS, TC]], channel_multiplier=1).then_inc(consts, 1)
            pool.wait_ge(consts, 6)
            nc.gpsimd.affine_select(out=KW[:, :], in_=KW[:, :], compare_op=ALU.is_ge, fill=4096.0,
                                    base=DS - 1, pattern=[[DS, TC]], channel_multiplier=-1).then_inc(consts, 1)
            nc.gpsimd.iota(KCI, pattern=[[-512, NC], [-1, TC]], base=512 * (NC - 1) + TC - 1,
                           channel_multiplier=0).then_inc(consts, 1)
            nc.gpsimd.iota(TOKI[:, :], pattern=[[S, NB], [1, R]], base=0,
                           channel_multiplier=R).then_inc(consts, 1)
            nc.gpsimd.iota(LTI[:, :], pattern=[[0, 1]], base=0, channel_multiplier=1).then_inc(consts, 1)
            for n, bit in enumerate((2048, 1024, 512, 4, 2, 1)):
                nc.gpsimd.memset(BITS[:, n:n + 1], bit).then_inc(consts, 1)
            chain = Chain(pool, p_chain, {0: 1, 2: 7, 4: 3}, NB, 0, p_apart, always_apart=True)

            def centre(batch, slot, n):
                wait_apart(pool, ctx_mean, n + 1, p_apart)
                nc.gpsimd.tensor_scalar(CC[:, :], CTX[:, slot, :], 1.0, NMC[:, 0:1], ALU.mult,
                                        ALU.add).then_inc(centred, 1)

            centre(0, 0, 0)
            with pool.If(general_flag(pool)):
                with pool.Fori(0, NB) as b:
                    wait_apart(pool, g_var, b + 1, g_apart)
                    nc.gpsimd.tensor_tensor(R1[:, :], GVE, HALFNEG[:, 0:R], ALU.pow).then_inc(g_rstd, 1)
                pool.wait_ge(g_again, 48)
            with pool.Else():
                pool.wait_ge(flag_ready, 1)

            def step(st):
                chain.begin(st)
                if st.static and st.number() == 2:
                    pool.wait_ge(setup_done, 1)
                if st.on(2):
                    k = st.slot(2)
                    wait_apart(pool, var_x1, st.batch(2) + 1, p_apart)
                    chain.link(nc.gpsimd.tensor_tensor(RR[:, :, :].rearrange("p a i -> p (a i)"),
                                                       WV[:, :, :].rearrange("p a i -> p (a i)"),
                                                       HALFNEG[:, :], ALU.pow))
                    chain.mark(nc.gpsimd.tensor_tensor(MR[:, :], RR[:, 1, :], MEAN[:, k, :], ALU.mult))
                    chain.link(nc.gpsimd.tensor_scalar(YA[:, :], RR[:, 0, :], TG2[:, 0:1], 1.0, ALU.mult, ALU.add))
                    chain.link(nc.gpsimd.tensor_scalar(NMR[:, :], MR[:, :], -1.0, 0.0, ALU.mult, ALU.add))
                if st.on(4):
                    k = st.slot(4)
                    wait_apart(pool, slice_done, st.batch(4) + 1, p_apart)
                    chain.link(nc.gpsimd.tensor_scalar(PEN[:, :, :], OH[:, k, :, 0, :], -1.0, BIG,
                                                       ALU.add, ALU.mult))
                    wait_apart(pool, ran, st.batch(4) + 1, p_apart)
                    for w in range(2):
                        chain.mark(nc.gpsimd.tensor_tensor(
                            CAND[:, w, :, :], OH[:, k, :, 0, :],
                            V[:, w, :].unsqueeze(2).to_broadcast([P, R, NT]), ALU.mult))
                    chain.wait()
                    for w in range(2):
                        nc.gpsimd.tensor_tensor(CAND[:, w, :, :], CAND[:, w, :, :], PEN[:, :, :],
                                                ALU.add).then_inc(cand_ready, 1)
                if st.on(2):
                    k = st.slot(2)
                    if st.after(2, 1):
                        wait_apart(pool, gathered, st.batch(2), p_apart)
                    for i in range(R):
                        nc.gpsimd.tensor_scalar(XH[:, i, :], X1[:, k, i, :], RR[:, 1, i:i + 1],
                                                NMR[:, i:i + 1], ALU.mult, ALU.add).then_inc(normed, 1)
                    chain.mark(nc.gpsimd.tensor_tensor(IR[:, :], WV[:, 1, :], RR[:, 1, :], ALU.mult))
                    chain.link(nc.gpsimd.tensor_tensor(MR[:, :], RR[:, 0, :], MEAN[:, k, :], ALU.mult))
                    nc.gpsimd.tensor_tensor(YS[:, k, :], IR[:, :], YA[:, :], ALU.mult).then_inc(ys_ready, 1)
                    chain.link(nc.gpsimd.tensor_scalar(YC[:, :], MR[:, :], NTG2[:, 0:1], 0.0, ALU.mult, ALU.add))
                    for i in range(R):
                        if i == 0:
                            wait_apart(pool, normed, R * (st.batch(2) + 1), p_apart)
                        nc.gpsimd.tensor_scalar(X1[:, k, i, :], X1[:, k, i, :], YA[:, i:i + 1],
                                                YC[:, i:i + 1], ALU.mult, ALU.add).then_inc(y0_ready, 1)
                if st.on(-1):
                    wait_apart(pool, bank_free, bank(st, "ctx1")[1], p_apart)
                    centre(None, st.slot(-1), st.number() + 1)
                if st.on(0):
                    wait_apart(pool, var_x, st.batch(0) + 1, p_apart)
                    chain.link(nc.gpsimd.tensor_scalar(WL[:, :], MV1[:, :, 1], EPS, None, ALU.add))
                    nc.gpsimd.tensor_tensor(RX[:, st.slot(0), :], WL[:, :], HALFNEG[:, 0:R],
                                            ALU.pow).then_inc(rstd_x, 1)
                chain.end(st)

            steps(pool, step)

            pool.wait_ge(idx_ready, 1)
            for n in range(3):
                pool.wait_ge(y_out[n], 16 * R * len(range(n, NB, 3)))
            for t in range(TT):
                pool.wait_ge(fin_ready, t // 4 + 1)
                nc.gpsimd.indirect_dma_start(
                    out_rows, bass.IndirectOffsetOnAxis(ap=IDX[:, t:t + 1], axis=0),
                    FIN[:, t, :], None).then_inc(scattered, 16)
            pool.wait_ge(scattered, 16 * TT)

        @block.scalar
        def _(act):
            act.wait_ge(padded, 2)
            act.dma_start(GBROW[NC:2 * NC, :], beta.rearrange("(c p) -> c p", p=P)).then_inc(gb_in, 16)
            act.dma_start(GBROW[0:NC, :], gamma.rearrange("(c p) -> c p", p=P)).then_inc(gb_in, 16)
            act.dma_start(G1[:, :], g_xattn.unsqueeze(0).to_broadcast([P, 1])).then_inc(params_in, 16)
            act.dma_start(G2[:, :], g_ffn.unsqueeze(0).to_broadcast([P, 1])).then_inc(params_in, 16)
            act.dma_start(SLOPE[:, :, :], slopes.rearrange("t j g -> (t j) g").rearrange(
                "(c p) g -> p c g", p=P)).then_inc(params_in, 16)
            act.dma_start(LT[:, 0:DS], gamma.rearrange("(t j) -> t j", j=DS)).then_inc(params_in, 16)
            act.dma_start(LT[:, DS:2 * DS], beta.rearrange("(t j) -> t j", j=DS)).then_inc(params_in, 16)
            act.dma_start(SPRAW[0], bases.rearrange("t j g -> t (j g)")).then_inc(params_in, 16)
            act.dma_start(SPRAW[1], slopes.rearrange("t j g -> t (j g)")).then_inc(params_in, 16)
            act.dma_start(OSC[:, :], out_scale.rearrange("(t a) -> t a", a=1)).then_inc(params_in, 16)
            act.wait_ge(params_in, 16 * 8)
            nc.scalar.activation(TG1[:, :], G1[:, :], ACT.Tanh).then_inc(tanh_done, 1)
            nc.scalar.activation(TG2[:, :], G2[:, :], ACT.Tanh).then_inc(tanh_done, 1)
            with act.If(general_flag(act)):
                act.wait_ge(flag_ready, 1).then_inc(g_free, 1)
                with act.Fori(0, NB) as b:
                    uses = 2 * NC + R
                    for n in range(2 * NC):
                        act.wait_ge(g_full, uses * b + n + 1)
                        dst = GXT[:, n, :] if n < NC else GCT[:, n - NC, :]
                        nc.scalar.activation(dst, OB[n % 2], ACT.Copy).then_inc(g_free, 1)
                    act.wait_ge(g_rstd, b + 1)
                    for i in range(R):
                        act.wait_ge(g_bias, R * b + i + 1)
                        nc.scalar.activation(GE, GS, ACT.Exp, bias=NBIAS[:, i:i + 1], scale=R1[:, i:i + 1],
                                             accum_out=SUMS[:, i:i + 1]).then_inc(g_exp, 1)
                        act.wait_ge(g_full, uses * b + 2 * NC + i + 1)
                        nc.scalar.activation(GPT, OB[0], ACT.Copy).then_inc(g_free, 1)
                act.wait_ge(g_again, 48)
            with act.Else():
                act.wait_ge(flag_ready, 1)

            def take(st, name, out, function=ACT.Copy, width=S, **more):
                n, count = bank(st, name)
                act.wait_ge(bank_full, count)
                source = TB[n][:, 0:width] if name != "oht" else TB[n].bitcast(BF16)[:, 0:S]
                nc.scalar.activation(out, source, function, **more).then_inc(bank_free, 1)

            def take_x(st, c):
                if st.on(0):
                    take(st, f"x{c}", XT[:, c % 4, :])

            def take_h(st, c):
                if st.on(2):
                    take(st, f"h{c}", SG[:, c, :], ACT.Sign, scale=GB[:, c:c + 1], bias=GB[:, NC + c:NC + c + 1])

            def square(st, i):
                if st.on(1):
                    b = st.batch(1)
                    act.wait_ge(x1_half, 2 * R * b + 2 * i + 2)
                    if i == 0 and st.after(1, 1):
                        act.wait_ge(var_x1, b)
                    if i > 0 or st.after(1, 1):
                        act.wait_ge(squares, R * b + i)
                    nc.scalar.activation(JUNK[:, :], X1[:, st.slot(1), i, :], ACT.Square,
                                         accum_out=SQ[:, i:i + 1]).then_inc(squares, 1)

            def step(st):
                if st.static and st.number() == 2:
                    act.wait_ge(setup_done, 1)
                if st.on(0):
                    for n in range(2):
                        take(st, f"ctx{n}", CT[:, 4 * n:4 * n + 4, :].rearrange("p c k -> p (c k)"))
                take_x(st, 0)
                if st.on(1):
                    act.wait_ge(bias_ready, st.batch(1) + 1)
                    for i in range(R):
                        nc.scalar.activation(PR[:, i, :], SN[:, i, :], ACT.Exp, bias=NBIAS[:, i:i + 1],
                                             scale=RX[:, st.slot(1), i:i + 1],
                                             accum_out=SUMS[:, i:i + 1]).then_inc(exps, 1)
                take_x(st, 1)
                take_x(st, 2)
                if st.on(1):
                    take(st, "pt", PT[:, :])
                take_x(st, 3)
                take_x(st, 4)
                if st.on(3):
                    take(st, "oht", OHT[:, bass.ds(S * st.batch(3), S)])
                take_x(st, 5)
                take_x(st, 6)
                if st.on(3):
                    if st.after(3, 1):
                        act.wait_ge(slice_done, st.batch(3))
                    take(st, "look", LOOK[:, :, :].rearrange("p i w -> p (i w)"), width=R * LW)
                take_x(st, 7)
                if st.on(0):
                    act.wait_ge(scores_full, st.batch(0) + 1)
                    nc.scalar.activation(ST[:, :], SC, ACT.Identity, scale=float(D) ** -0.5,
                                         bias=MBIAS[:, bass.ds(st.batch(0), 1)]).then_inc(scores_sb, 1)
                for c in range(NC):
                    take_h(st, c)
                    if c % 2 == 1:
                        square(st, c // 2)

            steps(act, step)

            with act.Fori(0, GROUPS // 2) as i:
                for n in range(2):
                    act.wait_ge(group_full, 2 * i + n + 1)
                    rows = PS[:, 4 * n:4 * n + 4, :].rearrange("p b (j c) -> p (b j) c", c=2 * GRID)
                    act.wait_ge(group_taken, 2 * i + n + 1)
                    nc.scalar.activation(SEL[n][:, :, 0:GRID], rows[:, :, 0:GRID], ACT.Copy).then_inc(lows_sb, 1)

        @block.tensor
        def _(pe):
            pe.wait_ge(consts, 16)
            pe.wait_ge(mask_f32, 1)
            for kb in range(KB):
                last = nc.tensor.transpose(OB[0][:, kb * P:(kb + 1) * P], MASKF[:, kb * P:(kb + 1) * P], IDENT[:, :])
            last.then_inc(setup_t, 1)
            pe.wait_ge(mask_t, 1)
            nc.tensor.matmul(CNTP, ONES[:, :], MT[:, :, :].rearrange("p k b -> p (k b)"), start=True,
                             stop=True).then_inc(setup_t, 1)
            pe.wait_ge(gb_in, 32)
            nc.tensor.transpose(OB[1][:, 0:P], GBROW, IDENT[:, :]).then_inc(setup_t, 1)
            with pe.If(general_flag(pe)):
                pe.wait_ge(setup_done, 1)
                with pe.Fori(0, NB) as b:
                    uses = 2 * NC + R
                    pe.wait_ge(g_in, 48 * b + 48)
                    pe.wait_ge(g_centred, b + 1)
                    for n in range(2 * NC):
                        pe.wait_ge(g_free, uses * b + max(n - 1, 0) + 1)
                        if n == 0:
                            pe.wait_ge(g_x1, 2 * R * b + 1)
                        source, c = (GX, n) if n < NC else (GC, n - NC)
                        for i in range(4):
                            last = nc.tensor.transpose(OB[n % 2][:, i * P:(i + 1) * P],
                                                       source[:, i, c * P:(c + 1) * P], IDENT[:, :])
                        last.then_inc(g_full, 1)
                    pe.wait_ge(g_free, uses * b + 2 * NC + 1)
                    for i in range(R):
                        for c in range(NC):
                            mm = nc.tensor.matmul(SC, GXT[:, c, i * P:(i + 1) * P], GCT[:, c, :], start=(c == 0),
                                                  stop=(c == NC - 1))
                        mm.then_inc(g_scores, 1)
                        pe.wait_ge(g_exp, R * b + i + 1)
                        pe.wait_ge(g_x1, 2 * R * b + 2 * i + 1)
                        for kb in range(KB):
                            last = nc.tensor.transpose(OB[0][:, kb * P:(kb + 1) * P], GE[:, kb * P:(kb + 1) * P],
                                                       IDENT[:, :])
                        last.then_inc(g_full, 1)
                        pe.wait_ge(g_free, uses * b + 2 * NC + i + 2)
                        for h in range(2):
                            for kb in range(KB):
                                mm = nc.tensor.matmul(OB[h], GPT[:, kb * P:(kb + 1) * P],
                                                      GCTX[:, kb, h * HALF:(h + 1) * HALF], start=(kb == 0),
                                                      stop=(kb == KB - 1))
                            mm.then_inc(g_o, 1)
                pe.wait_ge(g_again, 48)
            with pe.Else():
                pe.wait_ge(flag_ready, 1)

            def rotating(st, name):
                n, count = bank(st, name)
                if not st.static or count > 3:
                    pe.wait_ge(bank_free, count - 3)
                return TB[n]

            def turn_x(st, c):
                if st.on(0):
                    dst = rotating(st, f"x{c}")
                    if c == 0:
                        pe.wait_ge(x_in[st.slot(0)], 16 * st.round(0) + 16)
                    for i in range(R):
                        last = nc.tensor.transpose(dst[:, i * P:(i + 1) * P],
                                                   X[:, st.slot(0), i, c * P:(c + 1) * P], IDENT[:, :])
                    last.then_inc(bank_full, 1)

            def score(st, c):
                if st.on(0):
                    pe.wait_ge(bank_free, bank(st, f"x{c}")[1])
                    if c == 0 and st.after(0, 1):
                        pe.wait_ge(scores_sb, st.batch(0))
                    mm = nc.tensor.matmul(SC, CT[:, c, :], XT[:, c % 4, :], start=(c == 0), stop=(c == NC - 1))
                    if c == NC - 1:
                        mm.then_inc(scores_full, 1)

            def turn_h(st, c):
                if st.on(2):
                    dst = rotating(st, f"h{c}")
                    for i in range(R):
                        if c == 0:
                            pe.wait_ge(normed, R * st.batch(2) + i + 1)
                        last = nc.tensor.transpose(dst[:, i * P:(i + 1) * P], XH[:, i, c * P:(c + 1) * P],
                                                   IDENT[:, :])
                    last.then_inc(bank_full, 1)

            def key(st, c):
                if st.on(2):
                    pe.wait_ge(bank_free, bank(st, f"h{c}")[1])
                    if c == 0 and st.after(2, 1):
                        pe.wait_ge(onehot, st.batch(2))
                    for i in range(R):
                        mm = nc.tensor.matmul(KEYP[:, i, TC * c:TC * (c + 1)], SG[:, c, i * P:(i + 1) * P],
                                              KWS[:, c, :], start=True, stop=True)
                    if c == NC - 1:
                        mm.then_inc(keys_full, 1)

            def turn_scores(st):
                if st.on(1):
                    pe.wait_ge(scores_sb, st.batch(1) + 1)
                    if st.after(1, 1):
                        pe.wait_ge(exps, R * st.batch(1))
                    for i in range(R):
                        last = nc.tensor.transpose(SN[:, i, :], ST[:, i * P:(i + 1) * P], IDENT[:, :])
                    last.then_inc(turned, 1)

            def turn_probs(st):
                if st.on(1):
                    dst = rotating(st, "pt")
                    for i in range(R):
                        pe.wait_ge(exps, R * st.batch(1) + i + 1)
                        last = nc.tensor.transpose(dst[:, i * P:(i + 1) * P], PR[:, i, :], IDENT[:, :])
                    last.then_inc(bank_full, 1)

            def readout(st, n):
                if st.on(1):
                    i, h = n // 2, n % 2
                    if n == 0:
                        pe.wait_ge(bank_free, bank(st, "pt")[1])
                    if n >= 2 or st.after(1, 1):
                        pe.wait_ge(x1_half, 2 * R * st.batch(1) + n - 1)
                    nc.tensor.matmul(OB[n % 2], PT[:, i * P:(i + 1) * P],
                                     CTX[:, st.slot(1), h * HALF:(h + 1) * HALF], start=True,
                                     stop=True).then_inc(o_full, 1)

            def turn_onehot(st):
                if st.on(3):
                    dst = rotating(st, "oht").bitcast(BF16)
                    pe.wait_ge(onehot, st.batch(3) + 1)
                    for i in range(R):
                        twice = OH[:, st.slot(3), i, :, :].rearrange("p a t -> p (a t)")
                        last = nc.tensor.transpose(dst[:, i * P:(i + 1) * P], twice, IDENTB[:, :])
                    last.then_inc(bank_full, 1)

            def look_up(st):
                if st.on(3):
                    pe.wait_ge(bank_free, bank(st, "oht")[1])
                    dst = rotating(st, "look")
                    for i in range(R):
                        for part in range(3):
                            mm = nc.tensor.matmul(dst[:, i * LW:(i + 1) * LW],
                                                  OHT[0:NT, bass.ds(S * st.batch(3) + i * P, P)],
                                                  LTP[:, part, :], start=(part == 0), stop=(part == 2))
                    mm.then_inc(bank_full, 1)

            def step(st):
                if st.static and st.number() == 1:
                    pe.wait_ge(setup_done, 1)
                turn_scores(st)
                if st.on(0):
                    pe.wait_ge(centred, st.batch(0) + 1)
                    for n in range(2):
                        dst = rotating(st, f"ctx{n}")
                        for c in range(4):
                            last = nc.tensor.transpose(dst[:, c * P:(c + 1) * P],
                                                       CC[:, (4 * n + c) * P:(4 * n + c + 1) * P], IDENT[:, :])
                        last.then_inc(bank_full, 1)
                turn_x(st, 0)
                turn_x(st, 1)
                score(st, 0)
                turn_x(st, 2)
                score(st, 1)
                turn_probs(st)
                turn_x(st, 3)
                score(st, 2)
                turn_x(st, 4)
                score(st, 3)
                turn_onehot(st)
                turn_x(st, 5)
                score(st, 4)
                turn_x(st, 6)
                score(st, 5)
                look_up(st)
                turn_x(st, 7)
                score(st, 6)
                score(st, 7)
                for c in range(NC):
                    readout(st, c)
                    turn_h(st, c)
                    if c > 0:
                        key(st, c - 1)
                key(st, NC - 1)

            steps(pe, step)

            pe.wait_ge(run_sb, 1)
            for w in range(2):
                last = nc.tensor.transpose(PS[0:NT, 0, w * P:(w + 1) * P], RUN2[:, w, :], IDENT[:, :])
            last.then_inc(run_t, 1)
            pe.wait_ge(table_ready, 1)
            for t in range(TT):
                for part in range(3):
                    mm = nc.tensor.matmul(PS[:, 7, 2 * t:2 * t + 2], OHT[0:NT, t * P:(t + 1) * P], M2P[:, part, :],
                                          start=(part == 0), stop=(part == 2))
            mm.then_inc(range_full, 1)
            with pe.Fori(0, GROUPS // 2) as i:
                for n in range(2):
                    pe.wait_ge(group_taken, 2 * i + n + 1)
                    for r in range(4):
                        tile = bass.ds(P * 4 * (2 * i + n) + P * r, P)
                        nc.tensor.matmul(PS[:, 4 * n + r, :], OHT[:, tile], SPA[:, :], start=True, stop=False)
                        mm = nc.tensor.matmul(PS[:, 4 * n + r, :], OHT[0:NT, tile], SPB[:, :], start=False, stop=True)
                    mm.then_inc(group_full, 1)

        @block.vector
        def _(dve):
            made = [0]

            def link(instruction):
                made[0] += 1
                instruction.then_inc(v_chain, 1)
                dve.wait_ge(v_chain, made[0])

            def context_mean(slot, count, batch, after):
                dve.wait_ge(ctx_in[slot], count)
                if after is not None:
                    dve.wait_ge(centred, after)
                for h in range(2):
                    chain.mark(nc.vector.bn_stats(STC[:, h, :], CTX[:, slot, h * HALF:(h + 1) * HALF]))
                chain.wait(apart=True)
                chain.link(nc.vector.bn_aggr(MVC[:, :], STC[:, :, :]))
                nc.vector.tensor_scalar(NMC[:, :], MVC[:, 0:1], -1.0, None, ALU.mult).then_inc(ctx_mean, 1)

            nc.vector.memset(MASKF, 0.0).then_inc(padded, 1)
            nc.vector.memset(GBPAD, 0.0).then_inc(padded, 1)
            dve.wait_ge(mask_in, 16)
            dve.wait_ge(padded, 2)
            nc.vector.tensor_copy(MASKF[0:NB, :], MASKU).then_inc(mask_f32, 1)
            dve.wait_ge(ctx_in[0], 16)
            link(nc.vector.bn_stats(STC[:, 0, :], CTX[:, 0, 0:HALF]))
            link(nc.vector.bn_stats(STC[:, 1, :], CTX[:, 0, HALF:D]))
            link(nc.vector.bn_aggr(MVC[:, :], STC[:, :, :]))
            nc.vector.tensor_scalar(NMC[:, :], MVC[:, 0:1], -1.0, None, ALU.mult).then_inc(ctx_mean, 1)
            dve.wait_ge(setup_t, 1)
            nc.vector.tensor_copy(MT[:, :, :], OB[0].rearrange("p (k b) -> p k b", k=KB)[:, :, 0:NB]).then_inc(mask_t, 1)
            dve.wait_ge(mask_t, 1)
            dve.wait_ge(setup_t, 2)
            link(nc.vector.tensor_scalar(HASLAST[:, :], CNTP[:, (KB - 1) * NB:KB * NB], 0.0, BIG, ALU.is_gt,
                                         ALU.mult))
            link(nc.vector.tensor_reduce(CNT[:, :], CNTP.rearrange("p (k b) -> p b k", k=KB), AX_X, ALU.add))
            link(nc.vector.tensor_scalar(HASBIG[:, :], CNT[:, :], 0.0, BIG, ALU.is_gt, ALU.mult))
            link(nc.vector.scalar_tensor_tensor(MBIAS[:, :], MT[:, KB - 1, :], -1.0, HASLAST[:, :], ALU.add, ALU.mult))
            link(nc.vector.tensor_reduce(OTHER[:, :], CNTP[:, 0:(KB - 1) * NB], AX_X, ALU.add))
            nc.vector.tensor_scalar(FLAG[:, :], OTHER[:, :], 0.0, None, ALU.is_gt).then_inc(flag_ready, 1)
            dve.wait_ge(consts, 16)
            nc.vector.tensor_copy(KC[:, :], KCI)
            nc.vector.tensor_copy(TOK[:, :], TOKI[:, :])
            nc.vector.tensor_copy(IDENTB[:, :], IDENT[:, :])
            dve.wait_ge(setup_t, 3)
            nc.vector.tensor_copy(GB[:, :], OB[1][:, 0:2 * NC])
            dve.wait_ge(params_in, 16 * 8)
            link(nc.vector.tensor_reduce(SSUM[:, :], SLOPE[:, :, :], AX_X, ALU.add))
            link(nc.vector.tensor_scalar(SIGN[:, :], SSUM[:, :], 0.0, None, ALU.is_gt))
            link(nc.vector.tensor_scalar(SSUM[:, :], SSUM[:, :], 0.0, None, ALU.is_lt))
            link(nc.vector.tensor_tensor(SIGN[:, :], SIGN[:, :], SSUM[:, :], ALU.subtract))
            nc.vector.tensor_tensor(KWS[:, :, :], SIGN[:, :].unsqueeze(2).to_broadcast([P, NC, TC]),
                                    KW[:, :].unsqueeze(1).to_broadcast([P, NC, TC]), ALU.mult)
            link(nc.vector.tensor_copy(LT[:, 2 * DS:LW], LTI[:, :]))

            def split(source, rest, parts):
                link(nc.vector.tensor_copy(parts[0], source))
                link(nc.vector.tensor_tensor(rest, source, parts[0], ALU.subtract))
                link(nc.vector.tensor_copy(parts[1], rest))
                link(nc.vector.tensor_tensor(rest, rest, parts[1], ALU.subtract))
                link(nc.vector.tensor_copy(parts[2], rest))

            split(LT[:, :], LTR[:, :], [LTP[:, n, :] for n in range(3)])
            dve.wait_ge(tanh_done, 2)
            link(nc.vector.tensor_scalar(TGV[:, :], CNT[:, :], 0.0, TG1[:, 0:1], ALU.is_gt, ALU.mult))
            nc.vector.tensor_scalar(NTG2[:, :], TG2[:, :], -1.0, None, ALU.mult)
            table = SPS.rearrange("t (a w) -> t a w", w=2)
            for w in range(2):
                link(nc.vector.tensor_scalar(table[:, :, w], SPRAW[w], OSC[:, 0:1], TG2[0:NT, 0:1],
                                             ALU.mult, ALU.mult))
            link(nc.vector.tensor_copy(SPA[0:NT, :], SPS))
            link(nc.vector.tensor_tensor(SPR, SPS, SPA[0:NT, :], ALU.subtract))
            link(nc.vector.tensor_copy(SPB[:, :], SPR))
            link(nc.vector.tensor_tensor(SPR, SPR, SPB[:, :], ALU.subtract))
            link(nc.vector.tensor_copy(SPA[NT:2 * NT, :], SPB[:, :]))
            link(nc.vector.tensor_copy(SPB[:, :], SPR))
            nc.vector.memset(RUN[:, :, :, :], -BIG).then_inc(ran, 1)
            nc.vector.memset(SUMS[:, :], 0.0).then_inc(setup_done, 1)

            with dve.If(general_flag(dve)):
                dve.wait_ge(setup_done, 1).then_inc(g_x1, 1)
                with dve.Fori(0, NB) as b:
                    made_in_turn = 3 * R + 3 * KB + KB + 4 * R
                    done = [0]

                    def mark(instruction):
                        done[0] += 1
                        instruction.then_inc(g_chain, 1)

                    def wait():
                        wait_apart(dve, g_chain, made_in_turn * b + done[0], g_apart)

                    def g_link(instruction):
                        mark(instruction)
                        wait()

                    def statistics(source, mean_var, rows):
                        for i in range(rows):
                            for h in range(2):
                                mark(nc.vector.bn_stats(GSTATS[:, i, h, :], source[:, i, h * HALF:(h + 1) * HALF]))
                        wait()
                        for i in range(rows):
                            mark(nc.vector.bn_aggr(mean_var[:, i, :], GSTATS[:, i, :, :]))
                        wait()

                    dve.wait_ge(g_in, 48 * b + 48)
                    statistics(GX, GVX, R)
                    nc.vector.tensor_scalar(GVE, GVX[:, :, 1], EPS, None, ALU.add).then_inc(g_var, 1)
                    statistics(GCTX, GVC, KB)
                    for k in range(KB):
                        mark(nc.vector.tensor_scalar(GC[:, k, :], GCTX[:, k, :], GVC[:, k, 0:1], None, ALU.subtract))
                    wait()
                    nc.vector.tensor_scalar(GMB, GMASKU, -1.0, HASBIG[:, bass.ds(b, 1)], ALU.add,
                                            ALU.mult).then_inc(g_centred, 1)
                    dve.wait_ge(g_centred, b + 1)
                    dve.wait_ge(g_rstd, b + 1)
                    for i in range(R):
                        dve.wait_ge(g_scores, R * b + i + 1)
                        g_link(nc.vector.scalar_tensor_tensor(GS, SC, float(D) ** -0.5, GMB, ALU.mult, ALU.add))
                        g_link(nc.vector.tensor_reduce(MX[:, i:i + 1], GS, AX_X, ALU.max))
                        nc.vector.scalar_tensor_tensor(NBIAS[:, i:i + 1], MX[:, i:i + 1], -1.0, R1[:, i:i + 1],
                                                       ALU.mult, ALU.mult).then_inc(g_bias, 1)
                        dve.wait_ge(g_exp, R * b + i + 1)
                        g_link(nc.vector.reciprocal(REC[:, i:i + 1], SUMS[:, i:i + 1]))
                        g_link(nc.vector.tensor_scalar(COEF[:, i:i + 1], REC[:, i:i + 1], TGV[:, bass.ds(b, 1)],
                                                       None, ALU.mult))
                        for h in range(2):
                            dve.wait_ge(g_o, 2 * R * b + 2 * i + h + 1)
                            cols = slice(h * HALF, (h + 1) * HALF)
                            nc.vector.scalar_tensor_tensor(GX[:, i, cols], OB[h], COEF[:, i:i + 1], GX[:, i, cols],
                                                           ALU.mult, ALU.add).then_inc(g_x1, 1)
                    assert done[0] == made_in_turn
                nc.vector.memset(TGV[:, :], 0.0).then_inc(no_readout, 1)
                dve.wait_ge(no_readout, 1)
                dve.wait_ge(g_again, 48)
            with dve.Else():
                dve.wait_ge(flag_ready, 1)

            chain = Chain(dve, v_chain, {-1: 3, 0: 11, 1: 3, 2: 5, 3: 16}, NB, made[0], v_apart)

            def softmax_bias(st):
                if st.on(1):
                    dve.wait_ge(turned, st.batch(1) + 1)
                    chain.link(nc.vector.tensor_reduce(MX[:, :], SN[:, :, :], AX_X, ALU.max))
                    dve.wait_ge(rstd_x, st.batch(1) + 1)
                    nc.vector.scalar_tensor_tensor(NBIAS[:, :], MX[:, :], -1.0, RX[:, st.slot(1), :],
                                                   ALU.mult, ALU.mult).then_inc(bias_ready, 1)

            def coefficient(st):
                if st.on(1):
                    dve.wait_ge(exps, R * (st.batch(1) + 1))
                    chain.link(nc.vector.reciprocal(REC[:, :], SUMS[:, :]))
                    chain.link(nc.vector.tensor_scalar(COEF[:, :], REC[:, :], TGV[:, bass.ds(st.batch(1), 1)],
                                                       None, ALU.mult))

            def add_readout(st, n):
                if st.on(1):
                    i, h, k = n // 2, n % 2, st.slot(1)
                    if n == 0 and st.after(1, 3):
                        dve.wait_ge(y_out[k], 16 * R * st.round(1))
                    dve.wait_ge(o_full, 2 * R * st.batch(1) + n + 1)
                    cols = slice(h * HALF, (h + 1) * HALF)
                    nc.vector.scalar_tensor_tensor(X1[:, k, i, cols], OB[n % 2], COEF[:, i:i + 1],
                                                   X[:, k, i, cols], ALU.mult, ALU.add,
                                                   accum_out=OSUM[:, i, h:h + 1]).then_inc(x1_half, 1)

            def x1_stats(st):
                if st.on(2):
                    k = st.slot(2)
                    dve.wait_ge(squares, R * (st.batch(2) + 1))
                    dve.wait_ge(x1_half, 2 * R * (st.batch(2) + 1))
                    chain.link(nc.vector.tensor_tensor(SM[:, :], OSUM[:, :, 0], OSUM[:, :, 1], ALU.add))
                    chain.link(nc.vector.tensor_scalar(MEAN[:, k, :], SM[:, :], 1.0 / D, None, ALU.mult))
                    chain.link(nc.vector.tensor_tensor(MSQ[:, :], MEAN[:, k, :], MEAN[:, k, :], ALU.mult))
                    chain.link(nc.vector.scalar_tensor_tensor(VAR[:, :], SQ[:, :], 1.0 / D, MSQ[:, :], ALU.mult,
                                                              ALU.subtract))
                    if st.after(2, 1):
                        dve.wait_ge(ys_ready, st.batch(2))
                    chain.link(nc.vector.tensor_scalar(WV[:, 0, :], VAR[:, :], EPS, None, ALU.add))
                    nc.vector.scalar_tensor_tensor(WV[:, 1, :], WV[:, 0, :], EPS, VAR[:, :], ALU.mult,
                                                   ALU.add).then_inc(var_x1, 1)

            def pick_tile(st):
                if st.on(3):
                    dve.wait_ge(keys_full, st.batch(3) + 1)
                    chain.link(nc.vector.tensor_tensor(KEY[:, :, :], KEYP,
                                                       KC[:, :].unsqueeze(1).to_broadcast([P, R, NT]), ALU.add))
                    chain.link(nc.vector.tensor_reduce(KMAX[:, :], KEY[:, :, :], AX_X, ALU.max))
                    nc.vector.tensor_tensor(OH[:, st.slot(3), :, :, :],
                                            KEY[:, :, :].unsqueeze(2).to_broadcast([P, R, 2, NT]),
                                            KMAX[:, :].unsqueeze(2).unsqueeze(3).to_broadcast([P, R, 2, NT]),
                                            ALU.is_equal).then_inc(onehot, 1)

            def gather_slice(st):
                if st.on(3):
                    chain.link(nc.vector.tensor_scalar(KINT[:, :], KMAX[:, :], 256.0, None, ALU.add))
                    chain.link(nc.vector.tensor_tensor(KBITS[:, :, :], KINT[:, :].unsqueeze(2).to_broadcast([P, R, 6]),
                                                       BITS[:, :].unsqueeze(1).to_broadcast([P, R, 6]),
                                                       ALU.bitwise_and), apart=True)
                    width = HALF
                    for n in range(6):
                        chain.link(nc.vector.copy_predicated(
                            XH[:, :, D - width:D], KBITS[:, :, n:n + 1].to_broadcast([P, R, width]),
                            XH[:, :, D - 2 * width:D - width]), apart=n < 5)
                        width //= 2
                    nc.vector.tensor_copy(XS[:, :, :], XH[:, :, D - DS:D]).then_inc(gathered, 1)

            def x_stats(st, i):
                if st.on(0):
                    if i == 0:
                        dve.wait_ge(x_in[st.slot(0)], 16 * st.round(0) + 16)
                        if st.after(0, 1):
                            dve.wait_ge(rstd_x, st.batch(0))
                    for h in range(2):
                        chain.mark(nc.vector.bn_stats(ST1[:, i, h, :],
                                                      X[:, st.slot(0), i, h * HALF:(h + 1) * HALF]))
                    if i == R - 1:
                        chain.wait(apart=True)
                        for n in range(R):
                            ins = nc.vector.bn_aggr(MV1[:, n, :], ST1[:, n, :, :])
                            if n < R - 1:
                                chain.mark(ins)
                            else:
                                ins.then_inc(var_x, 1)

            def slices(st):
                if st.on(3):
                    k, b = st.slot(3), st.batch(3)
                    rows = bass.ds(R * b, R)

                    def wide(values):
                        return values.unsqueeze(2).to_broadcast([P, R, DS])

                    dve.wait_ge(gathered, b + 1)
                    dve.wait_ge(ys_ready, b + 1)
                    chain.mark(nc.vector.tensor_tensor(Y1[:, :, :], XS[:, :, :], wide(YS[:, k, :]), ALU.mult))
                    dve.wait_ge(bank_free, bank(st, "look")[1])
                    chain.link(nc.vector.tensor_tensor(E1[:, :, :], XS[:, :, :], LOOK[:, :, 0:DS], ALU.mult))
                    chain.mark(nc.vector.tensor_tensor(XN[:, rows, :], E1[:, :, :], LOOK[:, :, DS:2 * DS], ALU.add))
                    chain.mark(nc.vector.tensor_tensor(Y0S[:, rows, :], Y1[:, :, :], wide(MEAN[:, k, :]), ALU.add))
                    chain.link(nc.vector.tensor_copy(TK[:, rows], LOOK[:, :, 2 * DS]), apart=True)
                    if st.after(3, 1):
                        wait_apart(dve, cand_ready, 2 * b, v_apart)
                    chain.mark(nc.vector.tensor_reduce(V[:, 0, :], XN[:, rows, :], AX_X, ALU.max))
                    nc.vector.tensor_reduce(V[:, 1, :], XN[:, rows, :], AX_X, ALU.min,
                                            negate=True).then_inc(slice_done, 1)

            def take_candidates(st):
                if st.on(4):
                    dve.wait_ge(cand_ready, 2 * (st.batch(4) + 1))
                    dve.wait_ge(ran, st.batch(4) + 1)
                    nc.vector.tensor_tensor(RUN[:, :, :, :].rearrange("p w i t -> p (w i t)"),
                                            RUN[:, :, :, :].rearrange("p w i t -> p (w i t)"),
                                            CAND[:, :, :, :].rearrange("p w i t -> p (w i t)"),
                                            ALU.max).then_inc(ran, 1)

            def step(st):
                chain.begin(st)
                x1_stats(st)
                softmax_bias(st)
                pick_tile(st)
                gather_slice(st)
                coefficient(st)
                take_candidates(st)
                if st.on(-1):
                    context_mean(st.slot(-1), 16 * st.round(-1) + 16, None, st.batch(0) + 1)
                slices(st)
                for n in range(2 * R):
                    add_readout(st, n)
                    if n % 2 == 1:
                        x_stats(st, n // 2)
                chain.end(st)

            steps(dve, step)

            made[0] += sum(chain.counts.of(s) for s in range(NB + STAGES - 1))
            dve.wait_ge(ran, NB + 1)
            nc.vector.tensor_reduce(RUN2[:, :, :], RUN[:, :, :, :].rearrange("p w i t -> p w t i"), AX_X,
                                    ALU.max).then_inc(run_sb, 1)
            nc.vector.scalar_tensor_tensor(IDX[:, :], TOK[:, :], float(NT), TK[:, :], ALU.mult,
                                           ALU.add).then_inc(idx_ready, 1)
            dve.wait_ge(run_t, 1)
            link(nc.vector.tensor_reduce(MM[:, :], PS[0:NT, 0, 0:2 * P].rearrange("p (w n) -> p w n", w=2), AX_X,
                                         ALU.max))
            link(nc.vector.tensor_copy(M2[:, 0:1], MM[:, 1:2]))
            link(nc.vector.tensor_tensor(MM[:, 0:1], MM[:, 0:1], MM[:, 1:2], ALU.add))
            link(nc.vector.tensor_scalar(MM[:, 0:1], MM[:, 0:1], 1e-8, None, ALU.add))
            link(nc.vector.reciprocal(MM[:, 1:2], MM[:, 0:1]))
            link(nc.vector.tensor_scalar(M2[:, 1:2], MM[:, 1:2], float(GRID), None, ALU.mult))
            split(M2[:, :], M2R[:, :], [M2P[:, n, :] for n in range(3)])
            nc.vector.memset(FT[0], 0.0).then_inc(table_ready, 1)
            dve.wait_ge(range_full, 1)
            ranges = PS[:, 7, 0:2 * TT].rearrange("p (t w) -> p t w", w=2)
            link(nc.vector.tensor_tensor(U, XN[:, :, :], ranges[:, :, 0:1].to_broadcast([P, TT, DS]), ALU.add))
            link(nc.vector.tensor_tensor(U2, U, ranges[:, :, 1:2].to_broadcast([P, TT, DS]), ALU.mult))
            top = 0.9999989867210388 * GRID
            vf = VFRAC
            link(nc.vector.tensor_scalar(vf, U2.rearrange("p t j -> p (t j)"), 0.0, top, ALU.max, ALU.min))
            nc.vector.memset(FT[1], 0.0).then_inc(group_taken, 1)
            nc.vector.memset(FT[0], 0.0).then_inc(group_taken, 1)
            for n in range(4):
                link(nc.vector.tensor_scalar(BIT[n], vf, float(8 >> n), None, ALU.is_ge))
                link(nc.vector.scalar_tensor_tensor(vf, BIT[n], -float(8 >> n), vf, ALU.mult, ALU.add))
            y0f = Y0S[:, :, :].rearrange("p t j -> p (t j)")
            finf = FIN.rearrange("p t j -> p (t j)")
            for g in range(GROUPS):
                n = g % 2
                at = slice(64 * g, 64 * (g + 1))
                dve.wait_ge(lows_sb, g + 1)
                rows = PS[:, 4 * n:4 * n + 4, :].rearrange("p b (j c) -> p (b j) c", c=2 * GRID)
                width = GRID
                for level in range(4):
                    bit = BIT[level][:, at].unsqueeze(2).to_broadcast([P, 64, width])
                    upper = rows[:, :, width:2 * width] if level == 0 else SEL[n][:, :, width:2 * width]
                    link(nc.vector.copy_predicated(SEL[n][:, :, 0:width], bit, upper))
                    width //= 2
                link(nc.vector.tensor_tensor(FT[n], SEL[n][:, :, 1], vf[:, at], ALU.mult))
                link(nc.vector.tensor_tensor(FT2[n], SEL[n][:, :, 0], y0f[:, at], ALU.add))
                link(nc.vector.tensor_tensor(finf[:, at], FT[n], FT2[n], ALU.add))
                nc.vector.tensor_copy(FT2[n][:, 0:1], FT[n][:, 0:1]).then_inc(fin_ready, 1)
                nc.vector.tensor_copy(FT2[n][:, 1:2], FT[n][:, 1:2]).then_inc(group_taken, 1)


_INS = ["x", "ctx_2048", "mask_BxS2_bk0", "g_xattn", "g_ffn", "L0_ffn_ln_gamma", "L0_ffn_ln_beta",
        "L0_ffn_spline_bases", "L0_ffn_spline_slopes", "L0_ffn_output_scale"]


def kernel(**inputs):
    import numpy as _np
    import concourse.bacc as _bacc
    from concourse import mybir as _mybir
    from concourse.bass_utils import run_bass_kernel_spmd as _run

    nc = _bacc.Bacc("TRN2", target_bir_lowering=False, num_devices=1)
    arrays, args = {}, []
    for name in _INS:
        a = _np.ascontiguousarray(inputs[name])
        if a.dtype.kind == "b":
            a = a.view(_np.int32)
        arrays[f"in_{name}_dram"] = a
        args.append(nc.dram_tensor(f"in_{name}_dram", a.shape, _mybir.dt.from_np(a.dtype), kind="ExternalInput").ap())
    args.append(nc.dram_tensor("out_0_dram", (16, 512, 1024), _mybir.dt.float32, kind="ExternalOutput").ap())
    build_kernel(nc, *args)
    r = _run(nc, [arrays], core_ids=[0])
    return r.results[0]["out_0_dram"]
```

```python
from contextlib import ExitStack

import concourse.bass as bass
from concourse import mybir

ALU = mybir.AluOpType
ACT = mybir.ActivationFunctionType
AX_X = mybir.AxisListType.X
F32 = mybir.dt.float32
F16 = mybir.dt.float16
BF16 = mybir.dt.bfloat16
F32R = mybir.dt.float32r
U8 = mybir.dt.uint8
I32 = mybir.dt.int32

P = 128
BIG = 1e30
EPS = 1e-5
LAGS = range(-1, 5)


class Step:

    def __init__(self, q, u, batches):
        self.q, self.u, self.batches = q, u, batches
        self.static = isinstance(q, int)

    def previous(self):
        return Step((3 * self.q + self.u - 1) // 3, (self.u - 1) % 3, self.batches) if self.static else \
            Step(self.q, self.u - 1, self.batches)

    def number(self):
        return 3 * self.q + self.u

    def batch(self, lag):
        return 3 * self.q + (self.u - lag)

    def slot(self, lag):
        return (self.u - lag) % 3

    def round(self, lag):
        return self.q + (self.u - lag) // 3

    def on(self, lag):
        return not self.static or 0 <= self.batch(lag) < self.batches

    def after(self, lag, n):
        return not self.static or self.batch(lag) >= n


def wait_apart(engine, sem, value, apart):
    engine.wait_ge(sem, value).then_inc(apart, 1)


class Counts:

    def __init__(self, per_stage, batches):
        self.per_stage, self.batches = per_stage, batches

    def before(self, step):
        first = LAGS[-1]
        upto = step.number() if step.static else first
        total = sum(self.of(s) for s in range(LAGS[0], upto))
        if not step.static:
            total = total + self.of(first) * (step.number() - first)
        return total

    def of(self, s):
        return sum(n for lag, n in self.per_stage.items() if 0 <= s - lag < self.batches)


class Chain:

    def __init__(self, engine, sem, per_stage, batches, start, apart, always_apart=False):
        self.engine, self.sem, self.start = engine, sem, start
        self.apart, self.always_apart = apart, always_apart
        self.counts = Counts(per_stage, batches)

    def begin(self, step):
        self.base = self.counts.before(step) + self.start
        self.local = 0

    def mark(self, instruction):
        instruction.then_inc(self.sem, 1)
        self.local += 1

    def wait(self, apart=False, value=None):
        value = self.base + (self.local if value is None else value)
        if apart or self.always_apart:
            wait_apart(self.engine, self.sem, value, self.apart)
        else:
            self.engine.wait_ge(self.sem, value)

    def link(self, instruction, apart=False):
        self.mark(instruction)
        self.wait(apart)

    def end(self, step):
        if step.static:
            assert self.local == self.counts.of(step.number()), (self.local, step.number())
        else:
            assert self.local == self.counts.of(LAGS[-1]), self.local


def build_kernel(nc, x, ctx, mask, g_xattn, g_ffn, gamma, beta, bases, slopes, out_scale, out):
    NB, S, D = x.shape
    NT, DS, GRID = bases.shape
    R = S // P
    NC = D // P
    TC = P // DS
    KEYS = ctx.shape[1]
    KB = KEYS // P
    TT = NB * R
    HALF = D // 2
    LW = 2 * DS + 1
    GROUPS = TT // 4
    assert NC * TC == NT and S == 512 and R == 4 and KB == 4 and NC == 8

    xv = x.rearrange("b (p i) d -> b p (i d)", i=R)
    outv = out.rearrange("b (p i) d -> b p i d", i=R)
    out_rows = out.rearrange("b s (t j) -> (b s t) j", j=DS)

    es = ExitStack()
    with es:
        def sb(name, shape, dt):
            return es.enter_context(nc.sbuf_tensor(name, shape, dt))

        def sem(name):
            return es.enter_context(nc.semaphore(name))

        X = sb("X", [P, 3, R, D], F32)
        X1 = sb("X1", [P, 3, R, D], F32)
        XH = sb("XH", [P, R, D], F32)
        CTX = sb("CTX", [P, 3, D], F32)
        CC = sb("CC", [P, D], F32)
        CT = sb("CT", [P, NC, P], F32)
        XT = sb("XT", [P, 4, S], F32)
        ST = sb("ST", [P, S], F32)
        PR = sb("PR", [P, R, P], F32)
        PT = PR[:, :, :].rearrange("p i k -> p (i k)")
        PTH = sb("PTH", [P, S], F32R)
        PTL = sb("PTL", [P, S], F32R)
        CTXH = sb("CTXH", [P, D], F32R)
        CTXL = sb("CTXL", [P, D], F32R)
        SG = sb("SG", [P, NC, S], F16)
        JUNK = sb("JUNK", [P, D], BF16)
        OH = sb("OH", [P, 3, R, 2, NT], BF16)
        OHT = sb("OHT", [P, TT * P], BF16)
        XN = sb("XN", [P, TT, DS], F32)
        Y0S = sb("Y0S", [P, TT, DS], F32)
        TK = sb("TK", [P, TT], F32)
        CAND = sb("CAND", [P, 2, R, NT], F32)
        RUN = sb("RUN", [P, 2, R, NT], F32)
        PEN = sb("PEN", [P, R, NT], F32)

        ST1 = sb("ST1", [P, R, 2, 6], F32)
        MV1 = sb("MV1", [P, R, 2], F32)
        RX = sb("RX", [P, 3, R], F32)
        NMC = sb("NMC", [P, 1], F32)
        MX = sb("MX", [P, R], F32)
        NBIAS = sb("NBIAS", [P, R], F32)
        SUMS = sb("SUMS", [P, R], F32)
        REC = sb("REC", [P, R], F32)
        COEF = sb("COEF", [P, R], F32)
        OSUM = sb("OSUM", [P, R, 2], F32)
        SQ = sb("SQ", [P, R], F32)
        SM = sb("SM", [P, R], F32)
        MSQ = sb("MSQ", [P, R], F32)
        MEAN = sb("MEAN", [P, 3, R], F32)
        VAR = sb("VAR", [P, R], F32)
        WV = sb("WV", [P, 2, R], F32)
        RR = sb("RR", [P, 2, R], F32)
        NMR = sb("NMR", [P, R], F32)
        MR = sb("MR", [P, R], F32)
        YA = sb("YA", [P, R], F32)
        YC = sb("YC", [P, R], F32)
        IR = sb("IR", [P, R], F32)
        YS = sb("YS", [P, 3, R], F32)
        R1 = sb("R1", [P, R], F32)
        WL = sb("WL", [P, R], F32)
        KMAX = sb("KMAX", [P, R], F32)
        KINT = sb("KINT", [P, R], I32)
        KBITS = sb("KBITS", [P, R, 6], I32)
        BITS = sb("BITS", [P, 6], I32)
        LOOK = sb("LOOK", [P, R, LW], F32)
        XS = sb("XS", [P, R, DS], F32)
        E1 = sb("E1", [P, R, DS], F32)
        Y1 = sb("Y1", [P, R, DS], F32)
        V = sb("V", [P, 2, R], F32)

        IDENT = sb("IDENT", [P, P], F32)
        IDENTB = sb("IDENTB", [P, P], BF16)
        HALFNEG = sb("HALFNEG", [P, 2 * R], F32)
        MASKW = SG[0:NB, NC - 1, :].bitcast(I32)[:, 0:KEYS // 4]
        MASKU = MASKW.bitcast(U8)
        SLOPE = sb("SLOPE", [P, NC, GRID], F32)
        SSUM = sb("SSUM", [P, NC], F32)
        SIGN = sb("SIGN", [P, NC], F32)
        GB = sb("GB", [P, 2 * NC], F32)
        KW = sb("KW", [P, TC], F32)
        KWS = sb("KWS", [P, NC, TC], F16)
        KCI = [PT[0:1, 256 * n:256 * (n + 1)].bitcast(I32) for n in range(2)]
        KC = sb("KC", [1, 2, R * NT], F16)
        KONE = sb("KONE", [1, P], F16)
        IDX = sb("IDX", [P, TT], I32)
        TOKI = IDX
        TOK = sb("TOK", [P, TT], F32)
        MT = sb("MT", [P, KB, NB], F32)
        MBIAS = sb("MBIAS", [P, NB], F32)
        CNT = sb("CNT", [P, NB], F32)
        HASBIG = sb("HASBIG", [P, NB], F32)
        HASLAST = sb("HASLAST", [P, NB], F32)
        OTHER = sb("OTHER", [P, 1], F32)
        FLAG = sb("FLAG", [P, 1], I32)
        G1 = sb("G1", [P, 1], F32)
        G2 = sb("G2", [P, 1], F32)
        TG1 = sb("TG1", [P, 1], F32)
        TG2 = sb("TG2", [P, 1], F32)
        NTG2 = sb("NTG2", [P, 1], F32)
        TGV = sb("TGV", [P, NB], F32)
        LT = sb("LT", [NT, LW], F32)
        LTR = sb("LTR", [NT, LW], F32)
        LTI = sb("LTI", [NT, 1], I32)
        LTA = sb("LTA", [P, LW], BF16)
        LTB = sb("LTB", [NT, LW], BF16)
        OSC = sb("OSC", [NT, 1], F32)
        SPA = sb("SPA", [P, NT // 4 * GRID * 2], BF16)
        SPB = sb("SPB", [NT, DS * GRID * 2], BF16)
        MM = sb("MM", [NT, 2], F32)
        M2 = sb("M2", [NT, 2], F32)
        M2R = sb("M2R", [NT, 2], F32)
        M2A = sb("M2A", [P, 2], BF16)
        M2B = sb("M2B", [NT, 2], BF16)

        GX = X1[:, 0]
        GCTX = X1[:, 1]
        GC = X1[:, 2]
        GXT = XH[:, :, :].rearrange("p i d -> p (i d)").rearrange("p (c n) -> p c n", n=S)
        GCT = OHT[:, :].bitcast(F32).rearrange("p (c k) -> p c k", k=KEYS)
        GMASKW = SG[:, 0, :].bitcast(I32)[:, 0:KEYS // 4]
        GMASKU = GMASKW.bitcast(U8)
        GMB = SG[:, 2:4, :].rearrange("p a b -> p (a b)").bitcast(F32)
        GS = XT[:, 0, :]
        GE = XT[:, 1, :]
        GPT = XT[:, 2, :]
        GVX = ST[:, 0:2 * R].rearrange("p (i w) -> p i w", w=2)
        GVC = ST[:, 16:16 + 2 * KB].rearrange("p (i w) -> p i w", w=2)
        GVE = ST[:, 24:24 + R]
        GSTATS = ST[:, 32:32 + 48].rearrange("p (i h w) -> p i h w", h=2, w=6)
        x1_dram = nc.dram_tensor("x1_scratch", [NB, P, R * D], F32).ap()

        MASKF = XH[:, 0, 0:KEYS]
        ONES = XH[:, 0, KEYS:KEYS + P]
        RUN2 = CAND[:, 0, 0:2, :]
        XN_flat, Y0S_flat = (buffer[0:NT, :, :].rearrange("p t j -> p (t j)") for buffer in (XN, Y0S))
        SPRAW = [XN_flat[:, 0:DS * GRID], XN_flat[:, 512:512 + DS * GRID]]
        SPS = Y0S_flat[:, 0:512]
        SPR = Y0S_flat[:, 512:1024]
        U = X[:, 0, 0, :]
        U2 = X[:, 0, 1, :]
        VFRAC = X[:, 0, 2, :]
        FIN = X[:, 0, 3, :].rearrange("p (t j) -> p t j", j=DS)
        BIT = [X[:, 1, 0, 256 * n:256 * (n + 1)].bitcast(U8) for n in range(4)]
        SEL = [X[:, 1 + n // 3, (n + 1) % 4, :].rearrange("p (a c) -> p a c", c=DS) for n in range(4)]
        FT = [X[:, 2, 1, 64 * n:64 * (n + 1)] for n in range(2)]
        FT2 = [X[:, 2, 2, 64 * n:64 * (n + 1)] for n in range(2)]
        RANGE = X[:, 2, 3, 0:2 * TT].rearrange("p (t w) -> p t w", w=2)

        RANGE_PARTS = [range(0, 16), range(16, TT)]

        PS = es.enter_context(nc.psum_tensor("PS", [P, 8, 512], F32))
        TB = [PS[:, n, :] for n in range(3)]
        SC = PS[:, 3, :]
        SN = PS[:, 4, :].rearrange("p (i k) -> p i k", i=R)
        OB = [PS[:, 5 + n, :] for n in range(2)]
        KEYP = PS[:, 7, 0:R * NT].rearrange("p (i t) -> p i t", i=R)
        CNTP = PS[:, 7, 0:KB * NB]

        x_in = [sem(f"x_in{n}") for n in range(3)]
        ctx_in = [sem(f"ctx_in{n}") for n in range(3)]
        y_out = [sem(f"y_out{n}") for n in range(3)]
        params_in = sem("params_in")
        mask_in = sem("mask_in")
        gates_in = sem("gates_in")
        padded = sem("padded")
        consts = sem("consts")
        mask_f32 = sem("mask_f32")
        setup_t = sem("setup_t")
        mask_t = sem("mask_t")
        tanh_done = sem("tanh_done")
        gates_ready = sem("gates_ready")
        setup_done = sem("setup_done")
        bank_full = sem("bank_full")
        bank_free = sem("bank_free")
        centred = sem("centred")
        scores_full = sem("scores_full")
        scores_sb = sem("scores_sb")
        turned = sem("turned")
        bias_ready = sem("bias_ready")
        exps = sem("exps")
        ctx_high = sem("ctx_high")
        ctx_low = sem("ctx_low")
        pt_low = sem("pt_low")
        o_full = sem("o_full")
        x1_half = sem("x1_half")
        squares = sem("squares")
        var_x = sem("var_x")
        rstd_x = sem("rstd_x")
        var_x1 = sem("var_x1")
        ys_ready = sem("ys_ready")
        factors = sem("factors")
        normed = sem("normed")
        normed_third = sem("normed_third")
        normed_last = sem("normed_last")
        keys_full = sem("keys_full")
        onehot = sem("onehot")
        gathered = sem("gathered")
        y0_ready = sem("y0_ready")
        ctx_mean = sem("ctx_mean")
        slice_done = sem("slice_done")
        cand_ready = sem("cand_ready")
        ran = sem("ran")
        v_chain = sem("v_chain")
        tables_chain = sem("tables_chain")
        p_chain = sem("p_chain")
        v_apart = sem("v_apart")
        p_apart = sem("p_apart")
        flag_ready = sem("flag_ready")
        g_in = sem("g_in")
        g_var = sem("g_var")
        g_rstd = sem("g_rstd")
        g_centred = sem("g_centred")
        g_full = sem("g_full")
        g_free = sem("g_free")
        g_scores = sem("g_scores")
        g_bias = sem("g_bias")
        g_exp = sem("g_exp")
        g_o = sem("g_o")
        g_x1 = sem("g_x1")
        g_out = sem("g_out")
        g_again = sem("g_again")
        g_chain = sem("g_chain")
        no_readout = sem("no_readout")
        g_apart = sem("g_apart")
        run_t = sem("run_t")
        run_sb = sem("run_sb")
        table_ready = sem("table_ready")
        range_full = sem("range_full")
        idx_ready = sem("idx_ready")
        group_full = sem("group_full")
        lows_sb = sem("lows_sb")
        range_sb = sem("range_sb")
        rows_used = sem("rows_used")
        fin_ready = sem("fin_ready")
        scattered = sem("scattered")

        ORDER = [(0, "x2"), (0, "x3"), (0, "x4"), (1, "pt"), (3, "oht"),
                 (0, "x5"), (0, "x6"), (3, "look"), (0, "x7"), (2, "h0"), (2, "h1"), (2, "h2"),
                 (2, "h3"), (-1, "ctx0"), (2, "h4"), (2, "h5"), (-1, "ctx1"), (2, "h6"),
                 (-1, "x0"), (2, "h7"), (-1, "x1")]
        bank_uses = Counts({n: sum(lag == n for lag, _ in ORDER) for n in LAGS}, NB)

        def last_at(step, lag):
            return step.static and step.batch(lag) == NB - 1

        def bank(step, what):
            names = [name for lag, name in ORDER if step.on(lag)]
            if last_at(step, 2):
                names.sort(key=lambda name: name[0] != "h")
            at = names.index(what)
            if step.static:
                n = bank_uses.before(step) + at
                return n % 3, n + 1
            fixed = bank_uses.before(Step(1, 1, NB))
            u = step.u - LAGS[-1]
            return (fixed + u * len(names) + at) % 3, bank_uses.before(step) + at + 1

        def steps(engine, step):
            first = LAGS[-1]
            turns = (NB - first) // 3
            for s in range(LAGS[0], first):
                step(Step(s // 3, s % 3, NB))
            with engine.Fori(0, turns - 1) as i:
                for u in range(first, first + 3):
                    step(Step(i, u, NB))
            for s in range(first + 3 * (turns - 1), NB + first):
                step(Step(s // 3, s % 3, NB))

        def normed_rows(st, lag):
            return X[:, (NB - 1) % 3] if last_at(st, lag) else XH

        def needs_gathered(st):
            return st.after(2, 1) and not last_at(st, 2)

        block = es.enter_context(nc.Block())

        def general_flag(engine):
            engine.wait_ge(flag_ready, 1)
            return engine.value_load(FLAG[0:1, 0:1], min_val=0, max_val=1)

        @block.sync
        def _(sp):
            def load(source, slot, batch):
                sp.dma_start(CTX[:, slot, :], ctx[batch, KEYS - P:KEYS, :]).then_inc(ctx_in[slot], 16)
                sp.dma_start(X[:, slot].rearrange("p i d -> p (i d)"), source[batch]).then_inc(x_in[slot], 16)

            sp.dma_start(MASKW, mask).then_inc(mask_in, 16)
            sp.dma_start(CTX[:, 0, :], ctx[0, KEYS - P:KEYS, :]).then_inc(ctx_in[0], 16)
            sp.dma_start(X[:, 0].rearrange("p i d -> p (i d)"), xv[0]).then_inc(x_in[0], 16)
            load(xv, 1, 1)
            load(xv, 2, 2)

            def step(st, source):
                if st.on(2):
                    slot = st.slot(2)
                    for i in range(R):
                        sp.wait_ge(y0_ready, R * st.batch(2) + i + 1)
                        sp.dma_start(outv[st.batch(2), :, i, :], X1[:, slot, i, :]).then_inc(y_out[slot], 16)
                if st.on(1) and st.on(-2):
                    sp.wait_ge(x1_half, 2 * R * (st.batch(1) + 1))
                    load(source, st.slot(1), st.batch(-2))

            def general():
                sp.wait_ge(flag_ready, 1).then_inc(g_out, 16)
                with sp.Fori(0, NB) as b:
                    sp.wait_ge(g_out, 16 * b + 16)
                    sp.dma_start(GX.rearrange("p i d -> p (i d)"), xv[b]).then_inc(g_in, 16)
                    sp.dma_start(GCTX, ctx[b].rearrange("(k p) d -> p k d", p=P)).then_inc(g_in, 16)
                    sp.dma_start(GMASKW, mask[bass.ds(b, 1), :].to_broadcast([P, KEYS // 4])).then_inc(g_in, 16)
                    sp.wait_ge(g_x1, 2 * R * b + 2 * R + 1)
                    sp.dma_start(x1_dram[b], GX.rearrange("p i d -> p (i d)")).then_inc(g_out, 16)
                sp.wait_ge(g_out, 16 * NB + 16)
                for n in range(3):
                    sp.wait_ge(x_in[n], 16)
                    sp.dma_start(X[:, n].rearrange("p i d -> p (i d)"), x1_dram[n]).then_inc(g_again, 16)

            with sp.If(general_flag(sp)):
                general()
                steps(sp, lambda st: step(st, x1_dram))
            with sp.Else():
                steps(sp, lambda st: step(st, xv))
            for n in range(3):
                sp.wait_ge(y_out[n], 16 * R * len(range(n, NB, 3)))

        @block.gpsimd
        def _(pool):
            nc.gpsimd.memset(IDENT[:, :], 0.0).then_inc(consts, 1)
            nc.gpsimd.memset(ONES[:, :], 1.0).then_inc(consts, 1)
            nc.gpsimd.memset(HALFNEG[:, :], -0.5).then_inc(consts, 1)
            nc.gpsimd.memset(KW[:, :], 4104.0).then_inc(consts, 1)
            pool.wait_ge(consts, 4)
            nc.gpsimd.affine_select(out=IDENT[:, :], in_=IDENT[:, :], compare_op=ALU.not_equal, fill=1.0,
                                    base=0, pattern=[[-1, P]], channel_multiplier=1).then_inc(consts, 1)
            nc.gpsimd.affine_select(out=KW[:, :], in_=KW[:, :], compare_op=ALU.is_ge, fill=4096.0,
                                    base=0, pattern=[[-DS, TC]], channel_multiplier=1).then_inc(consts, 1)
            pool.wait_ge(consts, 6)
            nc.gpsimd.affine_select(out=KW[:, :], in_=KW[:, :], compare_op=ALU.is_ge, fill=4096.0,
                                    base=DS - 1, pattern=[[DS, TC]], channel_multiplier=-1).then_inc(consts, 1)
            nc.gpsimd.iota(KCI[0], pattern=[[0, R], [-512, NC], [0, TC]], base=512 * (NC - 1) + 256,
                           channel_multiplier=0).then_inc(consts, 1)
            nc.gpsimd.iota(KCI[1], pattern=[[0, R * NC], [-1, TC]], base=TC - 1,
                           channel_multiplier=0).then_inc(consts, 1)
            nc.gpsimd.iota(TOKI[:, :], pattern=[[S, NB], [1, R]], base=0,
                           channel_multiplier=R).then_inc(consts, 1)
            nc.gpsimd.iota(LTI[:, :], pattern=[[0, 1]], base=0, channel_multiplier=1).then_inc(consts, 1)
            for n, bit in enumerate((2048, 1024, 512, 4, 2, 1)):
                nc.gpsimd.memset(BITS[:, n:n + 1], bit).then_inc(consts, 1)
            chain = Chain(pool, p_chain, {0: 1, 2: 6, 4: 3}, NB, 0, p_apart, always_apart=True)

            with pool.If(general_flag(pool)):
                with pool.Fori(0, NB) as b:
                    wait_apart(pool, g_var, b + 1, g_apart)
                    nc.gpsimd.tensor_tensor(R1[:, :], GVE, HALFNEG[:, 0:R], ALU.pow).then_inc(g_rstd, 1)
                pool.wait_ge(g_again, 48)
            with pool.Else():
                pool.wait_ge(flag_ready, 1)

            def step(st):
                chain.begin(st)
                if st.static and st.number() == 2:
                    pool.wait_ge(gates_ready, 1)
                if st.on(4):
                    k = st.slot(4)
                    wait_apart(pool, slice_done, st.batch(4) + 1, p_apart)
                    chain.link(nc.gpsimd.tensor_scalar(PEN[:, :, :], OH[:, k, :, 0, :], -1.0, BIG,
                                                       ALU.add, ALU.mult))
                    wait_apart(pool, ran, st.batch(4) + 1, p_apart)
                    for w in range(2):
                        chain.mark(nc.gpsimd.tensor_tensor(
                            CAND[:, w, :, :], OH[:, k, :, 0, :],
                            V[:, w, :].unsqueeze(2).to_broadcast([P, R, NT]), ALU.mult))
                    chain.wait()
                    for w in range(2):
                        nc.gpsimd.tensor_tensor(CAND[:, w, :, :], CAND[:, w, :, :], PEN[:, :, :],
                                                ALU.add).then_inc(cand_ready, 1)
                if st.on(1):
                    context = CTX[:, st.slot(1), :]
                    if st.after(1, 1):
                        wait_apart(pool, o_full, 2 * R * st.batch(1), p_apart)
                    nc.gpsimd.tensor_scalar(CTXH[:, :], context, 1.0, 0.0, ALU.mult, ALU.add).then_inc(ctx_high, 1)
                    wait_apart(pool, ctx_high, st.batch(1) + 1, p_apart)
                    nc.gpsimd.tensor_tensor(CTXL[:, :], context, CTXH[:, :].bitcast(F32),
                                            ALU.subtract).then_inc(ctx_low, 1)
                if st.on(2):
                    k = st.slot(2)
                    wait_apart(pool, var_x1, st.batch(2) + 1, p_apart)
                    chain.link(nc.gpsimd.tensor_tensor(RR[:, :, :].rearrange("p a i -> p (a i)"),
                                                       WV[:, :, :].rearrange("p a i -> p (a i)"),
                                                       HALFNEG[:, :], ALU.pow))
                    chain.mark(nc.gpsimd.tensor_tensor(MR[:, :], RR[:, 1, :], MEAN[:, k, :], ALU.mult))
                    chain.link(nc.gpsimd.tensor_scalar(YA[:, :], RR[:, 0, :], TG2[:, 0:1], 1.0, ALU.mult, ALU.add))
                    nc.gpsimd.tensor_scalar(NMR[:, :], MR[:, :], -1.0, 0.0, ALU.mult, ALU.add).then_inc(factors, 1)
                if st.on(2):
                    k = st.slot(2)
                    if needs_gathered(st):
                        wait_apart(pool, gathered, st.batch(2), p_apart)
                    wait_apart(pool, factors, st.batch(2) + 1, p_apart)
                    for i in range(R - 2):
                        nc.gpsimd.tensor_scalar(normed_rows(st, 2)[:, i, :], X1[:, k, i, :], RR[:, 1, i:i + 1],
                                                NMR[:, i:i + 1], ALU.mult, ALU.add).then_inc(normed, 1)
                if st.on(-1):
                    wait_apart(pool, ctx_mean, st.batch(-1) + 1, p_apart)
                    if st.after(-1, 1):
                        wait_apart(pool, bank_free, bank(st.previous(), "ctx1")[1], p_apart)
                    nc.gpsimd.tensor_scalar(CC[:, :], CTX[:, st.slot(-1), :], 1.0, NMC[:, 0:1], ALU.mult,
                                            ALU.add).then_inc(centred, 1)
                if st.on(2):
                    chain.mark(nc.gpsimd.tensor_tensor(IR[:, :], WV[:, 1, :], RR[:, 1, :], ALU.mult))
                    chain.link(nc.gpsimd.tensor_tensor(MR[:, :], RR[:, 0, :], MEAN[:, k, :], ALU.mult))
                    nc.gpsimd.tensor_tensor(YS[:, k, :], IR[:, :], YA[:, :], ALU.mult).then_inc(ys_ready, 1)
                    chain.link(nc.gpsimd.tensor_scalar(YC[:, :], MR[:, :], NTG2[:, 0:1], 0.0, ALU.mult, ALU.add))
                    for i in range(R):
                        if i == 0:
                            wait_apart(pool, normed, (R - 2) * (st.batch(2) + 1), p_apart)
                        if i == R - 2:
                            wait_apart(pool, normed_third, st.batch(2) + 1, p_apart)
                        if i == R - 1:
                            wait_apart(pool, normed_last, st.batch(2) + 1, p_apart)
                        nc.gpsimd.tensor_scalar(X1[:, k, i, :], X1[:, k, i, :], YA[:, i:i + 1],
                                                YC[:, i:i + 1], ALU.mult, ALU.add).then_inc(y0_ready, 1)
                if st.on(0):
                    wait_apart(pool, var_x, st.batch(0) + 1, p_apart)
                    chain.link(nc.gpsimd.tensor_scalar(WL[:, :], MV1[:, :, 1], EPS, None, ALU.add))
                    nc.gpsimd.tensor_tensor(RX[:, st.slot(0), :], WL[:, :], HALFNEG[:, 0:R],
                                            ALU.pow).then_inc(rstd_x, 1)
                chain.end(st)

            steps(pool, step)

            pool.wait_ge(idx_ready, 1)
            for n in range(3):
                pool.wait_ge(y_out[n], 16 * R * len(range(n, NB, 3)))
            for t in range(TT):
                pool.wait_ge(fin_ready, t // 4 + 1)
                nc.gpsimd.indirect_dma_start(
                    out_rows, bass.IndirectOffsetOnAxis(ap=IDX[:, t:t + 1], axis=0),
                    FIN[:, t, :], None).then_inc(scattered, 16)
            pool.wait_ge(scattered, 16 * TT)

        @block.scalar
        def _(act):
            act.dma_start(G1[:, :], g_xattn.unsqueeze(0).to_broadcast([P, 1])).then_inc(gates_in, 16)
            act.dma_start(G2[:, :], g_ffn.unsqueeze(0).to_broadcast([P, 1])).then_inc(gates_in, 16)
            act.dma_start(GB[:, 0:NC], gamma.rearrange("(c p) -> p c", p=P),
                          allow_slow_non_contiguous=True).then_inc(params_in, 16)
            act.dma_start(GB[:, NC:2 * NC], beta.rearrange("(c p) -> p c", p=P),
                          allow_slow_non_contiguous=True).then_inc(params_in, 16)
            act.dma_start(SLOPE[:, :, :], slopes.rearrange("t j g -> (t j) g").rearrange(
                "(c p) g -> p c g", p=P),
                          allow_slow_non_contiguous=True).then_inc(params_in, 16)
            act.dma_start(LT[:, 0:DS], gamma.rearrange("(t j) -> t j", j=DS)).then_inc(params_in, 16)
            act.dma_start(LT[:, DS:2 * DS], beta.rearrange("(t j) -> t j", j=DS)).then_inc(params_in, 16)
            act.dma_start(SPRAW[0], bases.rearrange("t j g -> t (j g)")).then_inc(params_in, 16)
            act.dma_start(SPRAW[1], slopes.rearrange("t j g -> t (j g)")).then_inc(params_in, 16)
            act.dma_start(OSC[:, :], out_scale.rearrange("(t a) -> t a", a=1)).then_inc(params_in, 16)
            act.wait_ge(gates_in, 32)
            nc.scalar.activation(TG1[:, :], G1[:, :], ACT.Tanh).then_inc(tanh_done, 1)
            nc.scalar.activation(TG2[:, :], G2[:, :], ACT.Tanh).then_inc(tanh_done, 1)
            with act.If(general_flag(act)):
                act.wait_ge(flag_ready, 1).then_inc(g_free, 1)
                with act.Fori(0, NB) as b:
                    uses = 2 * NC + R
                    for n in range(2 * NC):
                        act.wait_ge(g_full, uses * b + n + 1)
                        dst = GXT[:, n, :] if n < NC else GCT[:, n - NC, :]
                        nc.scalar.activation(dst, OB[n % 2], ACT.Copy).then_inc(g_free, 1)
                    act.wait_ge(g_rstd, b + 1)
                    for i in range(R):
                        act.wait_ge(g_bias, R * b + i + 1)
                        nc.scalar.activation(GE, GS, ACT.Exp, bias=NBIAS[:, i:i + 1], scale=R1[:, i:i + 1],
                                             accum_out=SUMS[:, i:i + 1]).then_inc(g_exp, 1)
                        act.wait_ge(g_full, uses * b + 2 * NC + i + 1)
                        nc.scalar.activation(GPT, OB[0], ACT.Copy).then_inc(g_free, 1)
                act.wait_ge(g_again, 48)
            with act.Else():
                act.wait_ge(flag_ready, 1)

            def take(st, name, out, function=ACT.Copy, width=S, **more):
                n, count = bank(st, name)
                act.wait_ge(bank_full, count)
                source = TB[n][:, 0:width] if name != "oht" else TB[n].bitcast(BF16)[:, 0:S]
                nc.scalar.activation(out, source, function, **more).then_inc(bank_free, 1)

            def take_x(st, c, lag=0):
                if st.on(lag):
                    take(st, f"x{c}", XT[:, c % 4, :])

            def take_h(st, c):
                if st.on(2):
                    if st.static and st.number() == 2 and c == 0:
                        act.wait_ge(setup_done, 1)
                    take(st, f"h{c}", SG[:, c, :], ACT.Sign, scale=GB[:, c:c + 1], bias=GB[:, NC + c:NC + c + 1])

            def context_mean(st):
                if st.on(-1):
                    act.wait_ge(ctx_in[st.slot(-1)], 16 * st.round(-1) + 16)
                    if st.after(-1, 1):
                        act.wait_ge(centred, st.batch(-1))
                        act.wait_ge(ctx_mean, st.batch(-1))
                    if st.on(2):
                        act.wait_ge(squares, R * (st.batch(2) + 1))
                    nc.scalar.activation(JUNK[:, :], CTX[:, st.slot(-1), :], ACT.Identity, scale=-1.0 / D,
                                         accum_out=NMC[:, 0:1]).then_inc(ctx_mean, 1)

            def third_row(st):
                if st.on(2):
                    i = R - 2
                    act.wait_ge(factors, st.batch(2) + 1)
                    if needs_gathered(st):
                        act.wait_ge(gathered, st.batch(2))
                    nc.scalar.activation(normed_rows(st, 2)[:, i, :], X1[:, st.slot(2), i, :], ACT.Identity,
                                         bias=NMR[:, i:i + 1], scale=RR[:, 1, i:i + 1]).then_inc(normed_third, 1)

            def take_onehots(st):
                if st.on(3):
                    take(st, "oht", OHT[:, bass.ds(S * st.batch(3), S)])

            def take_look(st):
                if st.on(3):
                    if st.after(3, 1):
                        act.wait_ge(slice_done, st.batch(3))
                    take(st, "look", LOOK[:, :, :].rearrange("p i w -> p (i w)"), width=R * LW)

            def square(st, i, lag):
                if st.on(lag):
                    b = st.batch(lag)
                    act.wait_ge(x1_half, 2 * R * b + 2 * i + 2)
                    if i == 0 and st.on(-1):
                        act.wait_ge(ctx_mean, st.batch(-1) + 1)
                    if i == 0 and st.after(lag, 1):
                        act.wait_ge(var_x1, b)
                    if i > 0 or st.after(lag, 1):
                        act.wait_ge(squares, R * b + i)
                    nc.scalar.activation(JUNK[:, :], X1[:, st.slot(lag), i, :], ACT.Square,
                                         accum_out=SQ[:, i:i + 1]).then_inc(squares, 1)

            def step(st):
                take_x(st, 2)
                if not last_at(st, 2):
                    square(st, R - 1, 2)
                if st.on(1):
                    act.wait_ge(bias_ready, st.batch(1) + 1)
                    if st.after(1, 1):
                        act.wait_ge(pt_low, st.batch(1))
                    for i in range(R):
                        nc.scalar.activation(PR[:, i, :], SN[:, i, :], ACT.Exp, bias=NBIAS[:, i:i + 1],
                                             scale=RX[:, st.slot(1), i:i + 1],
                                             accum_out=SUMS[:, i:i + 1]).then_inc(exps, 1)
                take_x(st, 3)
                take_x(st, 4)
                if st.on(1):
                    if st.after(1, 1):
                        act.wait_ge(o_full, 2 * R * st.batch(1))
                    n, count = bank(st, "pt")
                    act.wait_ge(bank_full, count)
                    nc.scalar.activation(PTH[:, :], TB[n], ACT.Copy)
                    nc.scalar.activation(PT, TB[n], ACT.Copy).then_inc(bank_free, 1)
                if not last_at(st, 2):
                    take_onehots(st)
                take_x(st, 5)
                context_mean(st)
                take_x(st, 6)
                if not last_at(st, 2):
                    take_look(st)
                take_x(st, 7)
                third_row(st)
                if st.on(0):
                    act.wait_ge(scores_full, st.batch(0) + 1)
                    nc.scalar.activation(ST[:, :], SC, ACT.Identity, scale=float(D) ** -0.5,
                                         bias=MBIAS[:, bass.ds(st.batch(0), 1)]).then_inc(scores_sb, 1)
                if last_at(st, 1):
                    for i in range(R):
                        square(st, i, 1)
                for c in range(NC):
                    take_h(st, c)
                    if c % 2 == 1 and c < NC - 1 and not last_at(st, 1):
                        square(st, c // 2, 1)
                    if c >= NC - 2:
                        take_x(st, c - (NC - 2), -1)
                    if c in (3, 5) and st.on(-1):
                        n = (c - 3) // 2
                        take(st, f"ctx{n}", CT[:, 4 * n:4 * n + 4, :].rearrange("p c k -> p (c k)"))
                if last_at(st, 2):
                    take_onehots(st)
                    take_look(st)

            steps(act, step)

            def take_ranges(n):
                act.wait_ge(range_full, n + 1)
                tiles = RANGE_PARTS[n]
                source = PS[:, 7, 0:2 * len(tiles)].rearrange("p (t w) -> p t w", w=2)
                nc.scalar.activation(RANGE[:, tiles[0]:tiles[-1] + 1, :], source, ACT.Copy).then_inc(range_sb, 1)

            take_ranges(0)
            for g in range(GROUPS):
                n = g % 2
                act.wait_ge(group_full, g + 1)
                rows = PS[:, 4 * n:4 * n + 4, :].rearrange("p b (j c) -> p (b j) c", c=2 * GRID)
                if g >= 4:
                    act.wait_ge(fin_ready, g - 3)
                nc.scalar.activation(SEL[g % 4][:, :, 0:GRID], rows[:, :, 0:GRID], ACT.Copy).then_inc(lows_sb, 1)
                if g == 0:
                    take_ranges(1)

        @block.tensor
        def _(pe):
            pe.wait_ge(consts, 7)
            pe.wait_ge(mask_f32, 1)
            for kb in range(KB):
                last = nc.tensor.transpose(OB[0][:, kb * P:(kb + 1) * P], MASKF[:, kb * P:(kb + 1) * P], IDENT[:, :])
            last.then_inc(setup_t, 1)
            pe.wait_ge(mask_t, 1)
            nc.tensor.matmul(CNTP, ONES[:, :], MT[:, :, :].rearrange("p k b -> p (k b)"), start=True,
                             stop=True).then_inc(setup_t, 1)
            with pe.If(general_flag(pe)):
                with pe.Fori(0, NB) as b:
                    uses = 2 * NC + R
                    pe.wait_ge(g_in, 48 * b + 48)
                    pe.wait_ge(g_centred, b + 1)
                    for n in range(2 * NC):
                        pe.wait_ge(g_free, uses * b + max(n - 1, 0) + 1)
                        if n == 0:
                            pe.wait_ge(g_x1, 2 * R * b + 1)
                        source, c = (GX, n) if n < NC else (GC, n - NC)
                        for i in range(4):
                            last = nc.tensor.transpose(OB[n % 2][:, i * P:(i + 1) * P],
                                                       source[:, i, c * P:(c + 1) * P], IDENT[:, :])
                        last.then_inc(g_full, 1)
                    pe.wait_ge(g_free, uses * b + 2 * NC + 1)
                    for i in range(R):
                        for c in range(NC):
                            mm = nc.tensor.matmul(SC, GXT[:, c, i * P:(i + 1) * P], GCT[:, c, :], start=(c == 0),
                                                  stop=(c == NC - 1))
                        mm.then_inc(g_scores, 1)
                        pe.wait_ge(g_exp, R * b + i + 1)
                        pe.wait_ge(g_x1, 2 * R * b + 2 * i + 1)
                        for kb in range(KB):
                            last = nc.tensor.transpose(OB[0][:, kb * P:(kb + 1) * P], GE[:, kb * P:(kb + 1) * P],
                                                       IDENT[:, :])
                        last.then_inc(g_full, 1)
                        pe.wait_ge(g_free, uses * b + 2 * NC + i + 2)
                        for h in range(2):
                            for kb in range(KB):
                                mm = nc.tensor.matmul(OB[h], GPT[:, kb * P:(kb + 1) * P],
                                                      GCTX[:, kb, h * HALF:(h + 1) * HALF], start=(kb == 0),
                                                      stop=(kb == KB - 1))
                            mm.then_inc(g_o, 1)
                pe.wait_ge(g_again, 48)
            with pe.Else():
                pe.wait_ge(flag_ready, 1)

            def rotating(st, name):
                n, count = bank(st, name)
                if not st.static or count > 3:
                    pe.wait_ge(bank_free, count - 3)
                return TB[n]

            def turn_x(st, c, lag=0):
                if st.on(lag):
                    dst = rotating(st, f"x{c}")
                    if c == 0:
                        pe.wait_ge(x_in[st.slot(lag)], 16 * st.round(lag) + 16)
                    for i in range(R):
                        last = nc.tensor.transpose(dst[:, i * P:(i + 1) * P],
                                                   X[:, st.slot(lag), i, c * P:(c + 1) * P], IDENT[:, :])
                    last.then_inc(bank_full, 1)

            def score(st, c):
                if st.on(0):
                    pe.wait_ge(bank_free, bank(st.previous() if c < 2 else st, f"x{c}")[1])
                    if c == 0 and st.after(0, 1):
                        pe.wait_ge(scores_sb, st.batch(0))
                    mm = nc.tensor.matmul(SC, CT[:, c, :], XT[:, c % 4, :], start=(c == 0), stop=(c == NC - 1))
                    if c == NC - 1:
                        mm.then_inc(scores_full, 1)

            def turn_h(st, c):
                if st.on(2):
                    dst = rotating(st, f"h{c}")
                    if c == 0:
                        pe.wait_ge(normed, (R - 2) * (st.batch(2) + 1))
                        pe.wait_ge(normed_third, st.batch(2) + 1)
                        pe.wait_ge(normed_last, st.batch(2) + 1)
                    for i in range(R):
                        last = nc.tensor.transpose(dst[:, i * P:(i + 1) * P],
                                                   normed_rows(st, 2)[:, i, c * P:(c + 1) * P], IDENT[:, :])
                    last.then_inc(bank_full, 1)

            def key(st, c):
                if st.on(2):
                    pe.wait_ge(bank_free, bank(st, f"h{c}")[1])
                    if c == 0 and st.after(2, 1):
                        pe.wait_ge(onehot, st.batch(2))
                    if st.static and st.number() == 2 and c == 0:
                        pe.wait_ge(setup_done, 1)
                    if c == 0:
                        for n in range(2):
                            nc.tensor.matmul(PS[:, 7, 0:R * NT], KONE[:, :], KC[:, n, :], start=(n == 0), stop=False)
                    for i in range(R):
                        mm = nc.tensor.matmul(KEYP[:, i, TC * c:TC * (c + 1)], SG[:, c, i * P:(i + 1) * P],
                                              KWS[:, c, :], start=False,
                                              stop=(c == NC - 1 and i == R - 1))
                    if c == NC - 1:
                        mm.then_inc(keys_full, 1)

            def turn_scores(st):
                if st.on(0):
                    pe.wait_ge(scores_sb, st.batch(0) + 1)
                    if st.after(0, 1):
                        pe.wait_ge(exps, R * st.batch(0))
                    for i in range(R):
                        last = nc.tensor.transpose(SN[:, i, :], ST[:, i * P:(i + 1) * P], IDENT[:, :])
                    last.then_inc(turned, 1)

            def turn_context(st, n):
                if st.on(-1):
                    pe.wait_ge(centred, st.batch(-1) + 1)
                    dst = rotating(st, f"ctx{n}")
                    for c in range(4):
                        last = nc.tensor.transpose(dst[:, c * P:(c + 1) * P],
                                                   CC[:, (4 * n + c) * P:(4 * n + c + 1) * P], IDENT[:, :])
                    last.then_inc(bank_full, 1)

            def turn_probs(st):
                if st.on(1):
                    dst = rotating(st, "pt")
                    for i in range(R):
                        pe.wait_ge(exps, R * st.batch(1) + i + 1)
                        last = nc.tensor.transpose(dst[:, i * P:(i + 1) * P], PR[:, i, :], IDENT[:, :])
                    last.then_inc(bank_full, 1)

            def readout(st, n):
                if st.on(1):
                    i, h = n // 2, n % 2
                    if n == 0:
                        pe.wait_ge(pt_low, st.batch(1) + 1)
                        pe.wait_ge(ctx_low, st.batch(1) + 1)
                    if n >= 2 or st.after(1, 1):
                        pe.wait_ge(x1_half, 2 * R * st.batch(1) + n - 1)
                    rows, cols = slice(i * P, (i + 1) * P), slice(h * HALF, (h + 1) * HALF)
                    nc.tensor.matmul(OB[n % 2], PTH[:, rows], CTXH[:, cols], start=True, stop=False)
                    nc.tensor.matmul(OB[n % 2], PTH[:, rows], CTXL[:, cols], start=False, stop=False)
                    nc.tensor.matmul(OB[n % 2], PTL[:, rows], CTXH[:, cols], start=False,
                                     stop=True).then_inc(o_full, 1)

            def turn_onehot(st):
                if st.on(3):
                    dst = rotating(st, "oht").bitcast(BF16)
                    pe.wait_ge(onehot, st.batch(3) + 1)
                    for i in range(R):
                        twice = OH[:, st.slot(3), i, :, :].rearrange("p a t -> p (a t)")
                        last = nc.tensor.transpose(dst[:, i * P:(i + 1) * P], twice, IDENTB[:, :])
                    last.then_inc(bank_full, 1)

            def look_up(st):
                if st.on(3):
                    pe.wait_ge(bank_free, bank(st, "oht")[1])
                    dst = rotating(st, "look")
                    for i in range(R):
                        onehots = bass.ds(S * st.batch(3) + i * P, P)
                        nc.tensor.matmul(dst[:, i * LW:(i + 1) * LW], OHT[:, onehots], LTA[:, :], start=True,
                                         stop=False)
                        mm = nc.tensor.matmul(dst[:, i * LW:(i + 1) * LW], OHT[0:NT, onehots], LTB[:, :],
                                              start=False, stop=True)
                    mm.then_inc(bank_full, 1)

            def step(st):
                turn_x(st, 2)
                score(st, 0)
                turn_x(st, 3)
                score(st, 1)
                turn_x(st, 4)
                score(st, 2)
                turn_probs(st)
                score(st, 3)
                if not last_at(st, 2):
                    turn_onehot(st)
                turn_x(st, 5)
                score(st, 4)
                turn_x(st, 6)
                score(st, 5)
                if not last_at(st, 2):
                    look_up(st)
                turn_x(st, 7)
                score(st, 6)
                score(st, 7)
                if last_at(st, 1):
                    for n in range(2 * R):
                        readout(st, n)
                for c in range(NC - 1):
                    if not last_at(st, 1):
                        readout(st, c)
                    turn_h(st, c)
                    if c > 0:
                        key(st, c - 1)
                    if c == 3:
                        turn_context(st, 0)
                    if c == 4:
                        turn_scores(st)
                    if c == 5:
                        turn_context(st, 1)
                turn_x(st, 0, -1)
                turn_h(st, NC - 1)
                key(st, NC - 2)
                if not last_at(st, 1):
                    readout(st, NC - 1)
                turn_x(st, 1, -1)
                key(st, NC - 1)
                if last_at(st, 2):
                    turn_onehot(st)
                    look_up(st)

            steps(pe, step)

            pe.wait_ge(run_sb, 1)
            for w in range(2):
                last = nc.tensor.transpose(PS[0:NT, 0, w * P:(w + 1) * P], RUN2[:, w, :], IDENT[:, :])
            last.then_inc(run_t, 1)
            pe.wait_ge(table_ready, 1)

            def ranges(tiles):
                for n, t in enumerate(tiles):
                    onehots = slice(t * P, (t + 1) * P)
                    nc.tensor.matmul(PS[:, 7, 2 * n:2 * n + 2], OHT[:, onehots], M2A[:, :], start=True, stop=False)
                    mm = nc.tensor.matmul(PS[:, 7, 2 * n:2 * n + 2], OHT[0:NT, onehots], M2B[:, :], start=False,
                                          stop=True)
                mm.then_inc(range_full, 1)

            def fetch(g, n):
                for r in range(4):
                    tile = bass.ds(P * 4 * g + P * r, P)
                    nc.tensor.matmul(PS[:, 4 * n + r, :], OHT[:, tile], SPA[:, :], start=True, stop=False)
                    mm = nc.tensor.matmul(PS[:, 4 * n + r, :], OHT[0:NT, tile], SPB[:, :], start=False, stop=True)
                mm.then_inc(group_full, 1)

            ranges(RANGE_PARTS[0])
            fetch(0, 0)
            pe.wait_ge(range_sb, 1)
            ranges(RANGE_PARTS[1])
            pe.wait_ge(range_sb, 2)
            fetch(1, 1)
            with pe.Fori(1, GROUPS // 2) as i:
                for n in range(2):
                    pe.wait_ge(rows_used, 2 * i + n - 1)
                    fetch(2 * i + n, n)

        @block.vector
        def _(dve):
            made = [0]

            def link(instruction):
                made[0] += 1
                instruction.then_inc(v_chain, 1)
                dve.wait_ge(v_chain, made[0])

            nc.vector.memset(MASKF, 0.0).then_inc(padded, 1)
            dve.wait_ge(mask_in, 16)
            dve.wait_ge(padded, 1)
            nc.vector.tensor_copy(MASKF[0:NB, :], MASKU).then_inc(mask_f32, 1)
            dve.wait_ge(setup_t, 1)
            nc.vector.tensor_copy(MT[:, :, :], OB[0].rearrange("p (k b) -> p k b", k=KB)[:, :, 0:NB]).then_inc(mask_t, 1)
            dve.wait_ge(mask_t, 1)
            dve.wait_ge(setup_t, 2)
            link(nc.vector.tensor_scalar(HASLAST[:, :], CNTP[:, (KB - 1) * NB:KB * NB], 0.0, BIG, ALU.is_gt,
                                         ALU.mult))
            link(nc.vector.tensor_reduce(CNT[:, :], CNTP.rearrange("p (k b) -> p b k", k=KB), AX_X, ALU.add))
            link(nc.vector.tensor_scalar(HASBIG[:, :], CNT[:, :], 0.0, BIG, ALU.is_gt, ALU.mult))
            link(nc.vector.scalar_tensor_tensor(MBIAS[:, :], MT[:, KB - 1, :], -1.0, HASLAST[:, :], ALU.add, ALU.mult))
            link(nc.vector.tensor_reduce(OTHER[:, :], CNTP[:, 0:(KB - 1) * NB], AX_X, ALU.add))
            nc.vector.tensor_scalar(FLAG[:, :], OTHER[:, :], 0.0, None, ALU.is_gt).then_inc(flag_ready, 1)
            dve.wait_ge(tanh_done, 2)
            nc.vector.tensor_scalar(NTG2[:, :], TG2[:, :], -1.0, None, ALU.mult).then_inc(gates_ready, 1)
            link(nc.vector.tensor_scalar(TGV[:, :], CNT[:, :], 0.0, TG1[:, 0:1], ALU.is_gt, ALU.mult))

            tables_made = [0]

            def tables_link(instruction):
                tables_made[0] += 1
                instruction.then_inc(tables_chain, 1)
                dve.wait_ge(tables_chain, tables_made[0])

            def split(source, rest, high_middle, low, link):
                link(nc.vector.tensor_copy(high_middle[0:NT, :], source))
                link(nc.vector.tensor_tensor(rest, source, high_middle[0:NT, :], ALU.subtract))
                link(nc.vector.tensor_copy(low, rest))
                link(nc.vector.tensor_tensor(rest, rest, low, ALU.subtract))
                link(nc.vector.tensor_copy(high_middle[NT:2 * NT, :], low))
                return nc.vector.tensor_copy(low, rest)

            def constants():
                dve.wait_ge(consts, 17)
                for n in range(2):
                    nc.vector.tensor_copy(KC[:, n, :], KCI[n])
                nc.vector.memset(KONE[:, :], 1.0)
                nc.vector.tensor_copy(TOK[:, :], TOKI[:, :])
                nc.vector.tensor_copy(IDENTB[:, :], IDENT[:, :])
                nc.vector.memset(RUN[:, :, :, :], -BIG).then_inc(ran, 1)

            def tables():
                dve.wait_ge(params_in, 16 * 8)
                tables_link(nc.vector.tensor_reduce(SSUM[:, :], SLOPE[:, :, :], AX_X, ALU.add))
                tables_link(nc.vector.tensor_scalar(SIGN[:, :], SSUM[:, :], 0.0, None, ALU.is_gt))
                tables_link(nc.vector.tensor_scalar(SSUM[:, :], SSUM[:, :], 0.0, None, ALU.is_lt))
                tables_link(nc.vector.tensor_tensor(SIGN[:, :], SIGN[:, :], SSUM[:, :], ALU.subtract))
                nc.vector.tensor_tensor(KWS[:, :, :], SIGN[:, :].unsqueeze(2).to_broadcast([P, NC, TC]),
                                        KW[:, :].unsqueeze(1).to_broadcast([P, NC, TC]), ALU.mult)
                tables_link(nc.vector.tensor_copy(LT[:, 2 * DS:LW], LTI[:, :]))
                split(LT[:, :], LTR[:, :], LTA, LTB[:, :], tables_link)
                table = SPS.rearrange("t (a w) -> t a w", w=2)
                for w in range(2):
                    tables_link(nc.vector.tensor_scalar(table[:, :, w], SPRAW[w], OSC[:, 0:1], TG2[0:NT, 0:1],
                                                 ALU.mult, ALU.mult))
                split(SPS, SPR, SPA, SPB[:, :], tables_link).then_inc(setup_done, 1)

            with dve.If(general_flag(dve)):
                dve.wait_ge(flag_ready, 1).then_inc(g_x1, 1)
                with dve.Fori(0, NB) as b:
                    made_in_turn = 3 * R + 3 * KB + KB + 4 * R
                    done = [0]

                    def mark(instruction):
                        done[0] += 1
                        instruction.then_inc(g_chain, 1)

                    def wait():
                        wait_apart(dve, g_chain, made_in_turn * b + done[0], g_apart)

                    def g_link(instruction):
                        mark(instruction)
                        wait()

                    def statistics(source, mean_var, rows):
                        for i in range(rows):
                            for h in range(2):
                                mark(nc.vector.bn_stats(GSTATS[:, i, h, :], source[:, i, h * HALF:(h + 1) * HALF]))
                        wait()
                        for i in range(rows):
                            mark(nc.vector.bn_aggr(mean_var[:, i, :], GSTATS[:, i, :, :]))
                        wait()

                    dve.wait_ge(g_in, 48 * b + 48)
                    statistics(GX, GVX, R)
                    nc.vector.tensor_scalar(GVE, GVX[:, :, 1], EPS, None, ALU.add).then_inc(g_var, 1)
                    statistics(GCTX, GVC, KB)
                    for k in range(KB):
                        mark(nc.vector.tensor_scalar(GC[:, k, :], GCTX[:, k, :], GVC[:, k, 0:1], None, ALU.subtract))
                    wait()
                    nc.vector.tensor_scalar(GMB, GMASKU, -1.0, HASBIG[:, bass.ds(b, 1)], ALU.add,
                                            ALU.mult).then_inc(g_centred, 1)
                    dve.wait_ge(g_centred, b + 1)
                    dve.wait_ge(g_rstd, b + 1)
                    for i in range(R):
                        dve.wait_ge(g_scores, R * b + i + 1)
                        g_link(nc.vector.scalar_tensor_tensor(GS, SC, float(D) ** -0.5, GMB, ALU.mult, ALU.add))
                        g_link(nc.vector.tensor_reduce(MX[:, i:i + 1], GS, AX_X, ALU.max))
                        nc.vector.scalar_tensor_tensor(NBIAS[:, i:i + 1], MX[:, i:i + 1], -1.0, R1[:, i:i + 1],
                                                       ALU.mult, ALU.mult).then_inc(g_bias, 1)
                        dve.wait_ge(g_exp, R * b + i + 1)
                        g_link(nc.vector.reciprocal(REC[:, i:i + 1], SUMS[:, i:i + 1]))
                        g_link(nc.vector.tensor_scalar(COEF[:, i:i + 1], REC[:, i:i + 1], TGV[:, bass.ds(b, 1)],
                                                       None, ALU.mult))
                        for h in range(2):
                            dve.wait_ge(g_o, 2 * R * b + 2 * i + h + 1)
                            cols = slice(h * HALF, (h + 1) * HALF)
                            nc.vector.scalar_tensor_tensor(GX[:, i, cols], OB[h], COEF[:, i:i + 1], GX[:, i, cols],
                                                           ALU.mult, ALU.add).then_inc(g_x1, 1)
                    assert done[0] == made_in_turn
                nc.vector.memset(TGV[:, :], 0.0).then_inc(no_readout, 1)
                dve.wait_ge(no_readout, 1)
                dve.wait_ge(g_again, 48)
            with dve.Else():
                dve.wait_ge(flag_ready, 1)

            chain = Chain(dve, v_chain, {0: 11, 1: 3, 2: 5, 3: 21}, NB, made[0], v_apart)

            def softmax_bias(st):
                if st.on(1):
                    dve.wait_ge(turned, st.batch(1) + 1)
                    chain.link(nc.vector.tensor_reduce(MX[:, :], SN[:, :, :], AX_X, ALU.max))
                    dve.wait_ge(rstd_x, st.batch(1) + 1)
                    nc.vector.scalar_tensor_tensor(NBIAS[:, :], MX[:, :], -1.0, RX[:, st.slot(1), :],
                                                   ALU.mult, ALU.mult).then_inc(bias_ready, 1)

            def last_row(st):
                if st.on(2):
                    i = R - 1
                    dve.wait_ge(factors, st.batch(2) + 1)
                    if needs_gathered(st):
                        dve.wait_ge(gathered, st.batch(2))
                    nc.vector.tensor_scalar(normed_rows(st, 2)[:, i, :], X1[:, st.slot(2), i, :], RR[:, 1, i:i + 1],
                                            NMR[:, i:i + 1], ALU.mult, ALU.add).then_inc(normed_last, 1)

            def low_probs(st):
                if st.on(1):
                    dve.wait_ge(bank_free, bank(st, "pt")[1])
                    nc.vector.tensor_tensor(PTL[:, :], PT, PTH[:, :].bitcast(F32), ALU.subtract).then_inc(pt_low, 1)

            def coefficient(st):
                if st.on(1):
                    dve.wait_ge(exps, R * (st.batch(1) + 1))
                    chain.link(nc.vector.reciprocal(REC[:, :], SUMS[:, :]))
                    chain.link(nc.vector.tensor_scalar(COEF[:, :], REC[:, :], TGV[:, bass.ds(st.batch(1), 1)],
                                                       None, ALU.mult))

            def add_readout(st, n):
                if st.on(1):
                    i, h, k = n // 2, n % 2, st.slot(1)
                    if n == 0 and st.after(1, 3):
                        dve.wait_ge(y_out[k], 16 * R * st.round(1))
                    dve.wait_ge(o_full, 2 * R * st.batch(1) + n + 1)
                    cols = slice(h * HALF, (h + 1) * HALF)
                    nc.vector.scalar_tensor_tensor(X1[:, k, i, cols], OB[n % 2], COEF[:, i:i + 1],
                                                   X[:, k, i, cols], ALU.mult, ALU.add,
                                                   accum_out=OSUM[:, i, h:h + 1]).then_inc(x1_half, 1)

            def x1_stats(st, n):
                if st.on(2):
                    k = st.slot(2)
                    if n == 0:
                        dve.wait_ge(x1_half, 2 * R * (st.batch(2) + 1))
                        chain.mark(nc.vector.tensor_tensor(SM[:, :], OSUM[:, :, 0], OSUM[:, :, 1], ALU.add))
                    elif n == 1:
                        chain.mark(nc.vector.tensor_scalar(MEAN[:, k, :], SM[:, :], 1.0 / D, None, ALU.mult))
                    elif n == 2:
                        chain.mark(nc.vector.tensor_tensor(MSQ[:, :], MEAN[:, k, :], MEAN[:, k, :], ALU.mult))
                    elif n == 3:
                        dve.wait_ge(squares, R * (st.batch(2) + 1))
                        chain.mark(nc.vector.scalar_tensor_tensor(VAR[:, :], SQ[:, :], 1.0 / D, MSQ[:, :],
                                                                  ALU.mult, ALU.subtract))
                    elif n == 4:
                        if st.after(2, 1):
                            dve.wait_ge(ys_ready, st.batch(2))
                        chain.mark(nc.vector.tensor_scalar(WV[:, 0, :], VAR[:, :], EPS, None, ALU.add))
                    else:
                        nc.vector.scalar_tensor_tensor(WV[:, 1, :], WV[:, 0, :], EPS, VAR[:, :], ALU.mult,
                                                       ALU.add).then_inc(var_x1, 1)

            def pick_and_gather(st):
                drained = last_at(st, 2)
                if drained or not st.on(3):
                    for n in range(6):
                        x1_stats(st, n)
                        if st.on(2) and n < 5:
                            chain.wait()
                if drained:
                    last_row(st)
                if st.on(3):
                    dve.wait_ge(keys_full, st.batch(3) + 1)
                    x1_ready = [0]

                    def x1_between(n):
                        if not drained:
                            if n > 0:
                                chain.wait(value=x1_ready[0])
                            x1_stats(st, n)
                            x1_ready[0] = chain.local

                    chain.mark(nc.vector.tensor_reduce(KMAX[:, :], KEYP, AX_X, ALU.max))
                    x1_between(0)
                    chain.wait()
                    chain.mark(nc.vector.tensor_copy(KINT[:, :], KMAX[:, :]))
                    x1_between(1)
                    nc.vector.tensor_tensor(OH[:, st.slot(3), :, :, :],
                                            KEYP.unsqueeze(2).to_broadcast([P, R, 2, NT]),
                                            KMAX[:, :].unsqueeze(2).unsqueeze(3).to_broadcast([P, R, 2, NT]),
                                            ALU.is_equal).then_inc(onehot, 1)
                    chain.wait()
                    chain.mark(nc.vector.tensor_tensor(KBITS[:, :, :],
                                                       KINT[:, :].unsqueeze(2).to_broadcast([P, R, 6]),
                                                       BITS[:, :].unsqueeze(1).to_broadcast([P, R, 6]),
                                                       ALU.bitwise_and))
                    x1_between(2)
                    rows = normed_rows(st, 3)
                    ready = [chain.local, chain.local]
                    for n in range(6):
                        width = HALF >> n
                        for h, half in enumerate((slice(0, R // 2), slice(R // 2, R))):
                            if 2 * n + h < 3:
                                x1_between(3 + 2 * n + h)
                            chain.wait(apart=True, value=ready[h])
                            chain.mark(nc.vector.copy_predicated(
                                rows[:, half, D - width:D],
                                KBITS[:, half, n:n + 1].to_broadcast([P, R // 2, width]),
                                rows[:, half, D - 2 * width:D - width]))
                            ready[h] = chain.local
                    chain.wait()
                    nc.vector.tensor_copy(XS[:, :, :], rows[:, :, D - DS:D]).then_inc(gathered, 1)

            def x_stats(st, i):
                if st.on(0):
                    if i == 0:
                        dve.wait_ge(x_in[st.slot(0)], 16 * st.round(0) + 16)
                        if st.after(0, 1):
                            dve.wait_ge(rstd_x, st.batch(0))
                    for h in range(2):
                        chain.mark(nc.vector.bn_stats(ST1[:, i, h, :],
                                                      X[:, st.slot(0), i, h * HALF:(h + 1) * HALF]))
                    if i == R - 1:
                        chain.wait(apart=True)
                        for n in range(R):
                            ins = nc.vector.bn_aggr(MV1[:, n, :], ST1[:, n, :, :])
                            if n < R - 1:
                                chain.mark(ins)
                            else:
                                ins.then_inc(var_x, 1)

            def slices(st):
                if st.on(3):
                    k, b = st.slot(3), st.batch(3)
                    rows = bass.ds(R * b, R)

                    def wide(values):
                        return values.unsqueeze(2).to_broadcast([P, R, DS])

                    dve.wait_ge(gathered, b + 1)
                    dve.wait_ge(ys_ready, b + 1)
                    chain.mark(nc.vector.tensor_tensor(Y1[:, :, :], XS[:, :, :], wide(YS[:, k, :]), ALU.mult))
                    dve.wait_ge(bank_free, bank(st, "look")[1])
                    chain.link(nc.vector.tensor_tensor(E1[:, :, :], XS[:, :, :], LOOK[:, :, 0:DS], ALU.mult))
                    chain.mark(nc.vector.tensor_tensor(XN[:, rows, :], E1[:, :, :], LOOK[:, :, DS:2 * DS], ALU.add))
                    chain.mark(nc.vector.tensor_tensor(Y0S[:, rows, :], Y1[:, :, :], wide(MEAN[:, k, :]), ALU.add))
                    chain.link(nc.vector.tensor_copy(TK[:, rows], LOOK[:, :, 2 * DS]), apart=True)
                    if st.after(3, 1):
                        wait_apart(dve, cand_ready, 2 * b, v_apart)
                    chain.mark(nc.vector.tensor_reduce(V[:, 0, :], XN[:, rows, :], AX_X, ALU.max))
                    nc.vector.tensor_reduce(V[:, 1, :], XN[:, rows, :], AX_X, ALU.min,
                                            negate=True).then_inc(slice_done, 1)

            def take_candidates(st):
                if st.on(4):
                    dve.wait_ge(cand_ready, 2 * (st.batch(4) + 1))
                    dve.wait_ge(ran, st.batch(4) + 1)
                    nc.vector.tensor_tensor(RUN[:, :, :, :].rearrange("p w i t -> p (w i t)"),
                                            RUN[:, :, :, :].rearrange("p w i t -> p (w i t)"),
                                            CAND[:, :, :, :].rearrange("p w i t -> p (w i t)"),
                                            ALU.max).then_inc(ran, 1)

            def step(st):
                chain.begin(st)
                softmax_bias(st)
                pick_and_gather(st)
                if st.static and st.number() == 2:
                    tables()
                low_probs(st)
                if not last_at(st, 2):
                    last_row(st)
                x_stats(st, 0)
                coefficient(st)
                slices(st)
                add_readout(st, 0)
                add_readout(st, 1)
                x_stats(st, 1)
                add_readout(st, 2)
                add_readout(st, 3)
                x_stats(st, 2)
                add_readout(st, 4)
                add_readout(st, 5)
                x_stats(st, 3)
                add_readout(st, 6)
                take_candidates(st)
                add_readout(st, 7)
                if st.static and st.number() == 0:
                    constants()
                chain.end(st)

            steps(dve, step)

            made[0] += sum(chain.counts.of(s) for s in range(LAGS[0], NB + LAGS[-1]))
            nc.vector.scalar_tensor_tensor(IDX[:, :], TOK[:, :], float(NT), TK[:, :], ALU.mult,
                                           ALU.add).then_inc(idx_ready, 1)
            dve.wait_ge(ran, NB + 1)
            nc.vector.tensor_reduce(RUN2, RUN[:, :, :, :].rearrange("p w i t -> p w t i"), AX_X,
                                    ALU.max).then_inc(run_sb, 1)
            dve.wait_ge(run_t, 1)
            link(nc.vector.tensor_reduce(MM[:, :], PS[0:NT, 0, 0:2 * P].rearrange("p (w n) -> p w n", w=2), AX_X,
                                         ALU.max))
            nc.vector.tensor_copy(M2[:, 0:1], MM[:, 1:2])
            link(nc.vector.tensor_tensor(M2R[:, 0:1], MM[:, 0:1], MM[:, 1:2], ALU.add))
            link(nc.vector.tensor_scalar(M2R[:, 1:2], M2R[:, 0:1], 1e-8, None, ALU.add))
            link(nc.vector.reciprocal(MM[:, 1:2], M2R[:, 1:2]))
            link(nc.vector.tensor_scalar(M2[:, 1:2], MM[:, 1:2], float(GRID), None, ALU.mult))
            split(M2[:, :], M2R[:, :], M2A, M2B[:, :], link).then_inc(table_ready, 1)

            TOP = 0.9999989867210388 * GRID

            y0_slices = Y0S[:, :, :].rearrange("p t j -> p (t j)")
            final = FIN.rearrange("p t j -> p (t j)")
            PLACE_OPS = 11
            SPLINE_OPS = 6
            placed = [0]
            after = [0, 0]

            def mark(instruction):
                made[0] += 1
                instruction.then_inc(v_chain, 1)
                return made[0]

            def place_op(pair, k):
                tiles, cols = slice(8 * pair, 8 * (pair + 1)), slice(128 * pair, 128 * (pair + 1))
                if k == 0:
                    dve.wait_ge(range_sb, 1 if pair < 2 else 2)
                else:
                    dve.wait_ge(v_chain, placed[0])
                if k < 2:
                    source = XN[:, tiles, :] if k == 0 else U[:, cols].rearrange("p (t j) -> p t j", j=DS)
                    placed[0] = mark(nc.vector.tensor_tensor(
                        (U, U2)[k][:, cols].rearrange("p (t j) -> p t j", j=DS), source,
                        RANGE[:, tiles, k:k + 1].to_broadcast([P, 8, DS]), (ALU.add, ALU.mult)[k]))
                elif k == 2:
                    placed[0] = mark(nc.vector.tensor_scalar(VFRAC[:, cols], U2[:, cols], 0.0, TOP, ALU.max, ALU.min))
                elif k % 2 == 1:
                    n = (k - 3) // 2
                    placed[0] = mark(nc.vector.tensor_scalar(BIT[n][:, cols], VFRAC[:, cols], float(8 >> n), None,
                                                             ALU.is_ge))
                else:
                    n = (k - 3) // 2
                    placed[0] = mark(nc.vector.scalar_tensor_tensor(VFRAC[:, cols], BIT[n][:, cols], -float(8 >> n),
                                                                    VFRAC[:, cols], ALU.mult, ALU.add))

            def spline_op(g, k):
                n, width, sel = g % 2, GRID >> k, SEL[g % 4]
                at = slice(64 * g, 64 * (g + 1))
                if k == 0:
                    dve.wait_ge(lows_sb, g + 1)
                    dve.wait_ge(v_chain, placed[0])
                else:
                    dve.wait_ge(v_chain, after[n])
                if k < 4:
                    rows = PS[:, 4 * n:4 * n + 4, :].rearrange("p b (j c) -> p (b j) c", c=2 * GRID) if k == 0 else sel
                    instruction = nc.vector.copy_predicated(
                        sel[:, :, 0:width], BIT[k][:, at].unsqueeze(2).to_broadcast([P, 64, width]),
                        rows[:, :, width:2 * width])
                    before, after[n] = after[n], mark(instruction)
                    if k == 1:
                        dve.wait_ge(v_chain, before).then_inc(rows_used, 1)
                elif k == 4:
                    nc.vector.tensor_tensor(FT2[n], sel[:, :, 0], y0_slices[:, at], ALU.add)
                    after[n] = mark(nc.vector.tensor_tensor(FT[n], sel[:, :, 1], VFRAC[:, at], ALU.mult))
                else:
                    nc.vector.tensor_tensor(final[:, at], FT[n], FT2[n], ALU.add).then_inc(fin_ready, 1)

            for k in range(PLACE_OPS):
                place_op(0, k)
            for pair in range(GROUPS // 2):
                for m in range(2 * SPLINE_OPS):
                    n, k = (m // SPLINE_OPS, m % SPLINE_OPS) if pair < 2 else (m % 2, m // 2)
                    spline_op(2 * pair + n, k)
                    if m < PLACE_OPS and pair + 1 < GROUPS // 2:
                        place_op(pair + 1, m)
                dve.wait_ge(fin_ready, 2 * pair + 2)


_INS = ["x", "ctx_2048", "mask_BxS2_bk0", "g_xattn", "g_ffn", "L0_ffn_ln_gamma", "L0_ffn_ln_beta",
        "L0_ffn_spline_bases", "L0_ffn_spline_slopes", "L0_ffn_output_scale"]


def kernel(**inputs):
    import numpy as _np
    import concourse.bacc as _bacc
    from concourse import mybir as _mybir
    from concourse.bass_utils import run_bass_kernel_spmd as _run

    nc = _bacc.Bacc("TRN2", target_bir_lowering=False, num_devices=1)
    arrays, args = {}, []
    for name in _INS:
        a = _np.ascontiguousarray(inputs[name])
        if a.dtype.kind == "b":
            a = a.view(_np.int32)
        arrays[f"in_{name}_dram"] = a
        args.append(nc.dram_tensor(f"in_{name}_dram", a.shape, _mybir.dt.from_np(a.dtype), kind="ExternalInput").ap())
    args.append(nc.dram_tensor("out_0_dram", (16, 512, 1024), _mybir.dt.float32, kind="ExternalOutput").ap())
    build_kernel(nc, *args)
    r = _run(nc, [arrays], core_ids=[0])
    return r.results[0]["out_0_dram"]
```
